# Optimizing a Trainium2 kernel written in Bass

```python
import numpy as np
import jax
import jax.numpy as jnp

def _softmax(x, axis=-1):
    return jax.nn.softmax(x, axis=axis)

def _gelu(x):
    return jax.nn.gelu(x, approximate=True)

def _silu(x):
    return jax.nn.silu(x)

def _sigmoid(x):
    return jax.nn.sigmoid(x)

def _layernorm(x, axis=-1, eps=1e-05):
    m = jnp.mean(x, axis=axis, keepdims=True)
    v = jnp.var(x, axis=axis, keepdims=True)
    return (x - m) / jnp.sqrt(v + eps)

def _scatter_add(tgt, idx, src, axis=0):
    return tgt.at[idx].add(src)

def _segment_sum(src, seg, n):
    return jax.ops.segment_sum(src, seg, n)
kernel_name = 'mk_vit_tower_d1_tok_img512_r4_ed41d7'

def setup_inputs(seed: int=0):
    np.random.seed(seed)
    _w = jnp.asarray

    def _rec_inputs():
        import jax
        import jax.numpy as jnp
        _rk = jax.random.key(seed)
        x = -0.000190493 + 0.999948 * jax.random.normal(jax.random.fold_in(_rk, 1), (64, 2, 104, 104), jnp.float32)
        return x
    x = _rec_inputs()

    def _L0_tok_setup():
        import jax, jax.numpy as jnp
        import numpy as np
        HP = 4
        PATCH = 8
        EPS = 1e-07

        def _shifts(x):
            h, w = (x.shape[2], x.shape[3])
            pad2 = ((0, 0), (0, 0))
            left_up = jnp.pad(x[:, :, HP:, :w - HP], pad2 + ((0, HP), (HP, 0)))
            right_up = jnp.pad(x[:, :, HP:, HP:], pad2 + ((0, HP), (0, HP)))
            left_down = jnp.pad(x[:, :, :h - HP, :w - HP], pad2 + ((HP, 0), (HP, 0)))
            right_down = jnp.pad(x[:, :, :h - HP, HP:], pad2 + ((HP, 0), (0, HP)))
            return (left_up, right_up, left_down, right_down)
        key = jax.random.key(seed)
        k1, k2, k3, k4 = jax.random.split(key, 4)
        B, C, S = (128, 2, 104)
        embed_dim = 128
        x = jax.random.normal(k1, (B, C, S, S), dtype=jnp.float32)
        gamma = 1.0 + 0.05 * jax.random.normal(k2, (10, S, S), dtype=jnp.float32)
        beta = 0.05 * jax.random.normal(k3, (10, S, S), dtype=jnp.float32)
        W = 0.02 * jax.random.normal(k4, (embed_dim, 10, PATCH, PATCH), dtype=jnp.float32)
        b = jnp.zeros((embed_dim,), dtype=jnp.float32)
        return {'x': x, 'gamma': gamma, 'beta': beta, 'W': W, 'b': b}
    _L0_tok_all = _L0_tok_setup()
    _L0_tok_in = {k: v for k, v in _L0_tok_all.items() if k in ('gamma', 'beta', 'W', 'b')}
    del _L0_tok_all

    def _L0_attn_setup():
        import jax, jax.numpy as jnp
        import numpy as np
        HEADS = 8
        DIM_HEAD = 64
        NB_FEATURES = 64
        DIM = 128
        key = jax.random.key(seed)
        ks = jax.random.split(key, 4)
        b, n = (2, 2048)
        x = jax.random.normal(ks[0], (b, n, DIM), jnp.float32)
        Wqkv = jax.random.normal(ks[1], (3 * HEADS * DIM_HEAD, DIM), jnp.float32) / np.sqrt(DIM).astype(np.float32)
        Wout = jax.random.normal(ks[2], (DIM, HEADS * DIM_HEAD), jnp.float32) / np.sqrt(HEADS * DIM_HEAD).astype(np.float32)
        bout = jnp.zeros((DIM,), jnp.float32)
        proj = jax.random.normal(ks[3], (NB_FEATURES, DIM_HEAD), jnp.float32) / np.sqrt(DIM_HEAD).astype(np.float32)
        return {'x': x, 'Wqkv': Wqkv, 'Wout': Wout, 'bout': bout, 'proj': proj}
    _L0_attn_all = _L0_attn_setup()
    _L0_attn_in = {k: v for k, v in _L0_attn_all.items() if k in ('Wqkv', 'Wout', 'bout', 'proj')}
    del _L0_attn_all

    def _L0_ffn_setup():
        import jax, jax.numpy as jnp
        import numpy as np
        B, S, D, F, E, K = (4, 512, 128, 512, 8, 2)
        key = jax.random.key(seed)
        kx, kg, kw, kv, k2 = jax.random.split(key, 5)
        scale = 0.02
        return {'x': jax.random.normal(kx, (B, S, D), dtype=jnp.float32), 'Wg': jax.random.normal(kg, (D, E), dtype=jnp.float32) * scale, 'W': jax.random.normal(kw, (E, D, F), dtype=jnp.float32) * scale, 'V': jax.random.normal(kv, (E, D, F), dtype=jnp.float32) * scale, 'W2': jax.random.normal(k2, (E, F, D), dtype=jnp.float32) * scale}
    _L0_ffn_all = _L0_ffn_setup()
    _L0_ffn_in = {k: v for k, v in _L0_ffn_all.items() if k in ('Wg', 'W', 'V', 'W2')}
    del _L0_ffn_all
    return {'x': x, 'L0_tok_gamma': _L0_tok_in['gamma'], 'L0_tok_beta': _L0_tok_in['beta'], 'L0_tok_W': _L0_tok_in['W'], 'L0_tok_b': _L0_tok_in['b'], 'L0_attn_Wqkv': _L0_attn_in['Wqkv'], 'L0_attn_Wout': _L0_attn_in['Wout'], 'L0_attn_bout': _L0_attn_in['bout'], 'L0_attn_proj': _L0_attn_in['proj'], 'L0_ffn_Wg': _L0_ffn_in['Wg'], 'L0_ffn_W': _L0_ffn_in['W'], 'L0_ffn_V': _L0_ffn_in['V'], 'L0_ffn_W2': _L0_ffn_in['W2']}

def reference(x, L0_tok_gamma, L0_tok_beta, L0_tok_W, L0_tok_b, L0_attn_Wqkv, L0_attn_Wout, L0_attn_bout, L0_attn_proj, L0_ffn_Wg, L0_ffn_W, L0_ffn_V, L0_ffn_W2):
    import jax
    import jax.numpy as jnp

    def _L0_tok_ref(x, gamma, beta, W, b):
        import jax, jax.numpy as jnp
        import numpy as np
        HP = 4
        PATCH = 8
        EPS = 1e-07

        def _shifts(x):
            h, w = (x.shape[2], x.shape[3])
            pad2 = ((0, 0), (0, 0))
            left_up = jnp.pad(x[:, :, HP:, :w - HP], pad2 + ((0, HP), (HP, 0)))
            right_up = jnp.pad(x[:, :, HP:, HP:], pad2 + ((0, HP), (0, HP)))
            left_down = jnp.pad(x[:, :, :h - HP, :w - HP], pad2 + ((HP, 0), (HP, 0)))
            right_down = jnp.pad(x[:, :, :h - HP, HP:], pad2 + ((HP, 0), (0, HP)))
            return (left_up, right_up, left_down, right_down)
        lu, ru, ld, rd = _shifts(x)
        concat = jnp.concatenate((x, lu, ru, ld, rd), axis=1)
        mean = jnp.mean(concat, axis=(1, 2, 3), keepdims=True)
        var = jnp.var(concat, axis=(1, 2, 3), keepdims=True)
        normed = (concat - mean) * jax.lax.rsqrt(var + EPS)
        normed = normed * gamma[None] + beta[None]
        y = jax.lax.conv_general_dilated(normed, W, window_strides=(PATCH, PATCH), padding='VALID', dimension_numbers=('NCHW', 'OIHW', 'NCHW'))
        y = y + b[None, :, None, None]
        B, E = (y.shape[0], y.shape[1])
        y = y.reshape(B, E, -1).transpose(0, 2, 1)
        return y

    def _L0_attn_ref(x, Wqkv, Wout, bout, proj):
        import jax, jax.numpy as jnp
        import numpy as np
        HEADS = 8
        DIM_HEAD = 64
        NB_FEATURES = 64
        DIM = 128
        b, n, _ = x.shape
        scale = DIM_HEAD ** (-0.5)
        qkv = jnp.einsum('bnd,ed->bne', x, Wqkv)
        q, k, v = jnp.split(qkv, 3, axis=-1)
        to_heads = lambda t: t.reshape(b, n, HEADS, DIM_HEAD).transpose(0, 2, 1, 3)
        q = to_heads(q) * scale
        k = to_heads(k)
        v = to_heads(v)
        q_prime = jnp.exp(jnp.einsum('bhnd,fd->bhnf', q, proj))
        k_prime = jnp.exp(jnp.einsum('bhnd,fd->bhnf', k, proj))
        k_sum = k_prime.sum(axis=2)
        D = jnp.einsum('bhnf,bhf->bhn', q_prime, k_sum)
        D_inv = 1.0 / (D + 1e-06)
        context = jnp.einsum('bhmf,bhmd->bhfd', k_prime, v)
        out = jnp.einsum('bhnf,bhfd->bhnd', q_prime, context) * D_inv[..., None]
        out = out.transpose(0, 2, 1, 3).reshape(b, n, HEADS * DIM_HEAD)
        return jnp.einsum('bne,de->bnd', out, Wout) + bout

    def _L0_ffn_ref(x, Wg, W, V, W2):
        import jax, jax.numpy as jnp
        import numpy as np
        B, S, D, F, E, K = (4, 512, 128, 512, 8, 2)
        gate_logits = jnp.einsum('bsd,de->bse', x, Wg)
        topv, topi = jax.lax.top_k(gate_logits, K)
        w = jax.nn.softmax(topv, axis=-1)
        gw = jnp.sum(w[..., None] * jax.nn.one_hot(topi, E, dtype=x.dtype), axis=-2)
        y = jnp.zeros_like(x)
        n_experts = W.shape[0]
        for e in range(n_experts):
            h = jax.nn.silu(jnp.einsum('bsd,df->bsf', x, W[e])) * jnp.einsum('bsd,df->bsf', x, V[e])
            y = y + gw[..., e:e + 1] * jnp.einsum('bsf,fd->bsd', h, W2[e])
        return y
    h = _L0_tok_ref(x, L0_tok_gamma, L0_tok_beta, L0_tok_W, L0_tok_b)
    h = h + _L0_attn_ref(_layernorm(h, axis=-1), L0_attn_Wqkv, L0_attn_Wout, L0_attn_bout, L0_attn_proj)
    h = h + _L0_ffn_ref(_layernorm(h, axis=-1), L0_ffn_Wg, L0_ffn_W, L0_ffn_V, L0_ffn_W2)
    return h

_drawn_inputs = setup_inputs


def setup_inputs(seed=0):
    import zlib

    import numpy as np

    out = dict(_drawn_inputs(seed))
    spreads = {'L0_tok_b': (0.0, 0.1), 'L0_attn_bout': (0.0, 0.1)}
    factors = {'L0_ffn_Wg': 4.482, 'L0_ffn_W': 3.89, 'L0_ffn_V': 3.853, 'L0_ffn_W2': 3.857}
    for name, (base, spread) in spreads.items():
        noise = np.random.default_rng([zlib.crc32(name.encode()), seed]).standard_normal(out[name].shape)
        drawn = base * np.exp(spread * noise) if base else spread * noise
        out[name] = jnp.asarray(drawn.astype(out[name].dtype))
    for name, factor in factors.items():
        out[name] = (out[name] * factor).astype(out[name].dtype)
    return out
```

```python
from contextlib import ExitStack

import numpy as np

import concourse.bass as bass
from concourse import mybir

F32 = mybir.dt.float32
U32 = mybir.dt.uint32
I32 = mybir.dt.int32
ALU = mybir.AluOpType
ACT = mybir.ActivationFunctionType
AX_X = mybir.AxisListType.X

B, C, S = 64, 2, 104
PATCH, HALF = 8, 4
NP1 = S // PATCH
NP2 = NP1 + 1
TOK = NP1 * NP1
D = 128
HEADS, DH, NF = 8, 64, 64
F, E = 512, 8
NTOK = B * TOK
GI = 8
NG = B // GI
R0, R1 = GI * NP1, GI * NP2
PW = S + 2 * HALF
NPAIR = B // 2
PT = 2 * TOK
CH = 85
HALF_ROWS = [CH - 1, CH]
NSTAT = 5 * C * S * S
CAP = NTOK + 256
TT = 256
NT = (2 * NTOK) // TT + E
RW = D + 2
QS = DH ** -0.5

_SEGS = dict(ident=128, sel44=R1, sel0=R1, wab=2, selr=HEADS // 2 * 128, e127=HEADS * HEADS, iota8=8, iotacap=8,
             dup=8, tri=128, ones=128, tok=4, mhalf=4, padrow=2 * RW, padslot=16, tile=NT, steps=43, incl=E * E)
SEG, _o = {}, 0
for _k, _n in _SEGS.items():
    SEG[_k] = (_o, _o + _n)
    _o += _n
NCONST = _o


def constants():
    c = np.zeros((128, NCONST), np.float32)

    def seg(k):
        return c[:, SEG[k][0]:SEG[k][1]]

    p = np.arange(128)
    seg("ident")[:] = np.eye(128)
    same = (p[:R1, None] // NP2 == np.arange(R1)[None] // NP2) / NSTAT
    seg("sel44")[:R1] = same
    seg("sel0")[:R1, :R0] = (p[:R1, None] // NP2 == np.arange(R0)[None] // NP1) / NSTAT
    edge = ((p % NP2 == 0) | (p % NP2 == NP2 - 1)).astype(np.float32)
    seg("wab")[:, 0] = 5 - 2 * edge
    seg("wab")[:, 1] = edge - 2
    for h in range(HEADS):
        seg("selr")[h, h * NF:(h + 1) * NF] = 1
        seg("e127")[D - 1, h * HEADS + h] = 1
    seg("iota8")[:] = np.arange(8)
    seg("iotacap")[:] = np.arange(8) * CAP
    for ch in (0, 2):
        seg("dup")[CH - 1, 2 * ch:2 * ch + 2] = 100
    seg("tri")[:] = p[:, None] < p[None]
    seg("ones")[:] = 1
    for ch in range(4):
        seg("tok")[:, ch] = (ch // 2) * TOK + (ch % 2) * (CH - 1) + p
    seg("mhalf")[:] = -0.5
    for a in range(2):
        seg("padrow")[:, a * RW + RW - 1] = NTOK + a * 128 + p
        seg("padslot")[:, 8 * a:8 * a + 8] = np.arange(8)[None] * CAP + a * 128 + p[:, None]
    seg("tile")[:] = np.arange(NT)
    seg("steps")[:] = np.arange(43) * TT
    seg("incl")[:] = np.tril(np.ones((E, E))).reshape(-1)
    return c


def at_least(eng, sem, value):
    if not (isinstance(value, int) and value <= 0):
        eng.wait_ge(sem, value)


def wait_alone(eng, met, *waits):
    waits = [(q, v if isinstance(v, int) else eng.to_reg(v)) for q, v in waits]
    eng.wait_ge(*met)
    for q, v in waits:
        at_least(eng, q, v)


def build(nc, x, gamma, beta, convw, convb, wqkv, wout, bout, proj, wg, ffw, ffv, ffw2, const, out):
    with ExitStack() as ctx:
        cst = ctx.enter_context(nc.sbuf_tensor("cst", [128, NCONST], F32))
        counts = ctx.enter_context(nc.sbuf_tensor("counts", [128, E], F32))
        sorted_rows = nc.dram_tensor("sorted_rows", [E * CAP + TT, RW], F32, kind="Internal").ap()
        bank = [ctx.enter_context(nc.psum_tensor(f"bank{i}", [128, 512], F32)) for i in range(8)]
        tokens(nc, x, gamma, beta, convw, convb, wqkv, wout, bout, proj, wg, const, out, cst, counts, sorted_rows, bank)
        experts(nc, ffw, ffv, ffw2, out, cst, counts, sorted_rows, bank)


def tokens(nc, x, gamma, beta, convw, convb, wqkv, wout, bout, proj, wg, const, out, cst, counts, sorted_rows, bank):
    with ExitStack() as ctx:
        def sb(name, shape, dt=F32):
            return ctx.enter_context(nc.sbuf_tensor(name, shape, dt))

        def sem(name):
            return ctx.enter_context(nc.semaphore(name))

        def K(k):
            return cst[:, SEG[k][0]:SEG[k][1]]

        ident, ones, tri = K("ident"), K("ones"), K("tri")
        selr = K("selr").rearrange("p (j f) -> p j f", j=4)
        patches = sb("patches", [128, 2, 5, GI, TOK])
        raw0 = sb("raw0", [R0, C, PATCH, S])
        raw44 = sb("raw44", [R1, C, PATCH, PW])
        nrm0 = sb("nrm0", [R0, NP1, D])
        nrm44 = sb("nrm44", [R1, NP2, D])
        colsum = sb("colsum", [R1, 4])
        part = sb("part", [R1, 4])
        imgstat = sb("imgstat", [R1, 2, 2])
        imgtmp = sb("imgtmp", [R1, 2])
        imgvar = sb("imgvar", [R1, 2])
        imgrstd = sb("imgrstd", [R1, 2])
        gam = sb("gam", [128, 5, NP1, NP1])
        cbeta = sb("cbeta", [128, TOK])
        wct = sb("wct", [128, 5, D])
        wqp = sb("wqp", [128, HEADS * NF])
        wkp = sb("wkp", [128, HEADS * NF])
        wvo = sb("wvo", [128, HEADS, D + HEADS])
        wg_sb = sb("wg_sb", [128, E])
        bout_sb = sb("bout_sb", [128, 1])
        convb_sb = sb("convb_sb", [128, 1])
        h1T = sb("h1T", [128, 4, PT])
        xtok = sb("xtok", [CH, 2, 4, D])
        xT = sb("xT", [128, 2, PT])
        qf = sb("qf", [128, 2, 4, PT])
        kf = sb("kf", [CH, 4, HEADS * NF])
        gT = sb("gT", [128, 2, HEADS * NF])
        mm = sb("mm", [128, 2, 2, 4, D + HEADS])
        dsum = sb("dsum", [HEADS, PT])
        rden = sb("rden", [HEADS, PT])
        h2 = sb("h2", [CH, 2, 4, D])
        xrow = sb("xrow", [CH, 2, 2, 4, RW])
        x2T = sb("x2T", [128, PT])
        bns = sb("bns", [CH, 2, 4, 6])
        mv = sb("mv", [CH, 2, 4, 2])
        rstd = sb("rstd", [CH, 2, 4])
        vare = sb("vare", [CH, 2, 4])
        logit = sb("logit", [CH, 4, E])
        top = sb("top", [CH, 4, 8])
        topi = sb("topi", [CH, 4, 8], U32)
        topf = sb("topf", [CH, 4, 2])
        gap = sb("gap", [CH, 4])
        egap = sb("egap", [CH, 4])
        esum = sb("esum", [CH, 4])
        pick = sb("pick", [CH, 2, 4, E])
        both = sb("both", [CH, 4, E])
        before = sb("before", [CH, 5, E])
        slots = sb("slots", [CH, 4, E])
        pslot = sb("pslot", [CH, 2, 4, E])
        slotf = sb("slotf", [CH, 2, 4])
        sloti = sb("sloti", [CH, 2, 2, 4], U32)
        tokid = sb("tokid", [CH, 4])
        braw = sb("braw", [NP1, 5 * C, PATCH, S])
        big = patches[:].rearrange("p s g b t -> p (s g b t)")
        graw = big[0:NP1, 0:5 * C * PATCH * S].rearrange("p (c k x) -> p c k x", c=5 * C, k=PATCH)
        S_ = {}

        def s(name):
            if name not in S_:
                S_[name] = sem(name)
            return S_[name]

        w_conv = convw.rearrange("e c y x -> e (c y x)")
        w_qkv = wqkv.rearrange("(t j e) d -> e t j d", t=3, e=128)
        o = 5 * C * PATCH * S
        wc_raw = big[:, o:o + 640].rearrange("p (g k) -> p g k", g=5)
        wo_raw = big[:, o + 640:o + 1152].rearrange("p (j e) -> p j e", j=4)
        pj_raw = big[0:NF, o + 1152:o + 1280].rearrange("p (t d) -> p t d", t=2)
        pjT = big[:, o + 1280:o + 1408]
        woT = big[:, o + 1408:o + 2432].rearrange("p (j h n) -> p j h n", j=4, h=2)
        bT = big[:, o + 2432:o + 3277].rearrange("p (g y x) -> p g y x", g=5, y=NP1)
        wv_c = big[:, o + 3277:o + 3789].rearrange("p (j d) -> p j d", j=4)
        qkv_raw = sb("qkv_raw", [128, 3, 4, D])

        block = ctx.enter_context(nc.Block())

        def steps(eng, step):
            def group(g, first=False, fr=True, par=0):
                for k in range(4):
                    step(4 * g + k, k, g, par, True, not (first and k < 1), not (first and k < 2),
                         not (first and k < 3), fr)
            group(0, first=True)
            with eng.Fori(0, (NG - 2) // 2) as i:
                group(2 * i + 1, par=1)
                group(2 * i + 2, par=0)
            group(NG - 1, fr=False, par=1)
            for k in range(3):
                step(NPAIR + k, k, NG, 0, False, k < 1, k < 2, True, False)

        def pairs(n):
            return min(n, NPAIR) if isinstance(n, int) else n

        PIECES = [(0, 0, 4), (0, 4, 4), (0, 8, 4), (0, 12, 1), (1, 0, 4), (1, 4, 4), (1, 8, 4), (1, 12, 2)]
        NPIECE = len(PIECES)
        TURN = {0: [], 1: [0, 1, 2], 2: [3, 4, 5], 3: [6, 7]}

        def pieces_by(g, k, fr):
            return NPIECE * (g + 1) + (TURN[k][-1] + 1 if TURN[k] else 0) if fr else NPIECE * NG

        NRAW = 3 * GI + 4
        NSMALL = 10

        setup_met = (s("small_in"), 16 * NSMALL)

        @block.sync
        def _(sp):
            sp.dma_start(cst[:], const).then_inc(s("small_in"), 16)
            sp.dma_start(wc_raw, convw.rearrange("e (g c) y x -> e g (c y x)", g=5)).then_inc(s("small_in"), 16)
            sp.dma_start(qkv_raw[:], wqkv.rearrange("(t j e) d -> e t j d", t=3, e=128)).then_inc(s("small_in"), 16)
            sp.dma_start(wo_raw, wout.rearrange("o (j e) -> o j e", j=4)).then_inc(s("small_in"), 16)
            for t in range(2):
                sp.dma_start(pj_raw[:, t], proj).then_inc(s("small_in"), 16)
            sp.dma_start(wg_sb[:], wg).then_inc(s("small_in"), 16)
            sp.dma_start(bout_sb[:], bout.rearrange("(d a) -> d a", a=1)).then_inc(s("small_in"), 16)
            sp.dma_start(convb_sb[:], convb.rearrange("(d a) -> d a", a=1)).then_inc(s("small_in"), 16)
            sp.dma_start(tokid[:], const[0:CH, SEG["tok"][0]:SEG["tok"][1]]).then_inc(s("small_in"), 16)
            sp.dma_start(graw, gamma.rearrange("c (y k) x -> y c k x", k=PATCH)).then_inc(s("gamma_in"), 16)
            sp.dma_start(braw[:], beta.rearrange("c (y k) x -> y c k x", k=PATCH)).then_inc(s("beta_in"), 16)

            def load_group(g):
                at_least(sp, s("norm_done"), 2 * g)
                for b in range(GI):
                    img = x[bass.ds(GI * g + b, 1)].rearrange("b c y x -> (b c) y x")
                    sp.dma_start(raw0[NP1 * b:NP1 * (b + 1)], img.rearrange("c (y k) x -> y c k x", k=PATCH)
                                 ).then_inc(s("raw_in"), 16)
                    for c in range(C):
                        sp.dma_start(raw44[NP2 * b + 1:NP2 * b + NP1, c, :, HALF:HALF + S],
                                     img[c, HALF:S - HALF].rearrange("(y k) x -> y k x", k=PATCH)
                                     ).then_inc(s("raw_in"), 16)
                imgs = x[bass.ds(GI * g, GI)]
                for c in range(C):
                    for p0, k0, y0 in ((0, HALF, 0), (NP1, 0, S - HALF)):
                        sp.dma_start(raw44[p0:R1:NP2, c, k0:k0 + HALF, HALF:HALF + S], imgs[:, c, y0:y0 + HALF]
                                     ).then_inc(s("raw_in"), 16)

            sp.wait_ge(s("pads_zero"), 1)
            load_group(0)
            sp.wait_ge(s("small_in"), 16 * NSMALL)
            pad = K("padrow").rearrange("p (a n) -> p a n", a=2)
            sp.dma_start(out[NTOK:NTOK + TT].rearrange("(a p) n -> p a n", a=2), pad[:, :, 0:D]).then_inc(s("pads_out"), 16)
            sp.dma_start(sorted_rows[E * CAP:E * CAP + TT].rearrange("(a p) n -> p a n", a=2), pad).then_inc(s("pads_out"), 16)

            def step(n, k, g, par, a, b, c, d, fr):
                if fr and k == 0:
                    load_group(g + 1)
                if c:
                    m = n - 2
                    sp.wait_ge(s("h2_copied"), m + 1)
                    for ch in range(4):
                        r = HALF_ROWS[ch % 2]
                        sp.dma_start(out[bass.ds(m * PT + (ch // 2) * TOK + (ch % 2) * (CH - 1), r)],
                                     h2[0:r, k % 2, ch]).then_inc(s(f"h2_out{k % 2}"), 16)
            steps(sp, step)
            for q in range(2):
                sp.wait_ge(s(f"h2_out{q}"), NPAIR // 2 * 64)
            sp.wait_ge(s("pads_out"), 32)

        @block.tensor
        def _(pe):
            item = [0]

            def begin():
                at_least(pe, s("setup_copied"), item[0] - 7)
                item[0] += 1
                return bank[(item[0] - 1) % 8]

            def end(mm):
                mm.then_inc(s("setup_mm"), 1)

            pe.wait_ge(s("small_in"), 16 * NSMALL)
            o_ = begin()
            for g in range(4):
                mm_ = pe.transpose(o_[:, 128 * g:128 * g + 128], wc_raw[:, g], ident)
            end(mm_)
            o_ = begin()
            pe.transpose(o_[:, 0:128], wc_raw[:, 4], ident)
            end(pe.transpose(o_[:, 128:192], pj_raw.rearrange("p t d -> p (t d)"), ident[0:NF, 0:NF]))
            o_ = begin()
            for j in range(4):
                mm_ = pe.transpose(o_[:, 128 * j:128 * j + 128], wo_raw[:, j], ident)
            end(mm_)
            pe.wait_ge(s("setup_copied"), 2)
            for t in range(2):
                o_ = begin()
                for j in range(4):
                    mm_ = pe.matmul(o_[:, 128 * j:128 * j + 128], qkv_raw[:, t, j], pjT, start=True, stop=True)
                end(mm_)
            pe.wait_ge(s("setup_copied"), 3)
            pe.wait_ge(s("wv_centred"), 1)
            for jj in range(2):
                o_ = begin()
                for j in range(2 * jj, 2 * jj + 2):
                    mm_ = pe.matmul(o_[:, 256 * (j % 2):256 * (j % 2) + 256], wv_c[:, j],
                                    woT[:, j].rearrange("p h n -> p (h n)"), start=True, stop=True)
                end(mm_)
            for q in range(10):
                o_ = begin()
                pe.wait_ge(s("affine_patched"), q + 1)
                for px in range(NP1):
                    mm_ = pe.transpose(o_[:, NP1 * px:NP1 * px + NP1], (nrm0, nrm44)[q % 2][0:NP1, px], ident[0:NP1, 0:NP1])
                end(mm_)
            pe.wait_ge(s("setup_copied"), 17)
            o_ = begin()
            for g in range(5):
                mm_ = pe.matmul(o_[:, 0:TOK], wct[:, g], bT[:, g].rearrange("p y x -> p (y x)"), start=(g == 0), stop=(g == 4))
            end(mm_)
            pe.wait_ge(s("setup_copied"), item[0])

            def image_stats(G):
                pe.wait_ge(s("part_ready"), G + 1)
                pe.matmul(bank[0][0:R1, 504:506], K("sel44")[0:R1], part[:, 0:2], start=True, stop=True)
                pe.matmul(bank[0][0:R1, 506:508], K("sel0")[0:R1], part[:, 0:2], start=True, stop=True
                          ).then_inc(s("imgstat_done"), 1)

            def front_piece(G, f):
                kind, px0, w = PIECES[f]
                pe.wait_ge(s("norm_done"), 2 * (G + 1))
                at_least(pe, s("front_evac"), NPIECE * G + f)
                src, rows = ((nrm0, R0), (nrm44, R1))[kind]
                for i in range(w):
                    px = px0 + i
                    t = pe.transpose(bank[0][:, rows * i:rows * i + rows], src[:, px], ident[0:rows, 0:rows])
                t.then_inc(s("front_t"), 1)

            image_stats(0)
            for f in range(NPIECE):
                front_piece(0, f)

            def step(n, k, g, par, a, b, c, d, fr):
                mb, mc, md = n - 1, n - 2, n - 3
                pb, pc, pd = (k + 1) % 2, k % 2, (k + 1) % 2
                if a:
                    pe.wait_ge(s("front_evac"), NPIECE * (g + 1))
                    at_least(pe, s("m_evac"), 4 * (n - 1))
                    for q in range(5):
                        t = pe.matmul(bank[1][:, 0:PT], wct[:, q],
                                      patches[:, par, q, 2 * k:2 * k + 2].rearrange("p b t -> p (b t)"),
                                      start=(q == 0), stop=(q == 4))
                    t.then_inc(s("conv_done"), 1)
                if c:
                    pe.wait_ge(s("m_evac"), 4 * (mc + 1))
                    pe.wait_ge(s("q_exp"), 4 * (mc + 1))
                    at_least(pe, s("attn_added"), mc)
                    for i in range(2):
                        for j in range(4):
                            t = pe.matmul(bank[7][0:HEADS, TOK * i:TOK * i + TOK], mm[:, pc, i, j, D:],
                                          qf[:, pc, j, TOK * i:TOK * i + TOK], start=(j == 0), stop=(j == 3))
                    t.then_inc(s("d8_done"), 1)
                if d:
                    pe.wait_ge(s("ln2_x"), md + 1)
                    pe.wait_ge(s("xT_copied"), pairs(n))
                    transpose_tokens(lambda ch, r: xrow[0:r, pd, 0, ch, 0:D], s("x2t_done"))
                if b:
                    pe.wait_ge(s("xT_copied"), mb + 1)
                    at_least(pe, s("k_exp"), 4 * mb)
                    for j in range(2):
                        q_feature(mb, pb, j)
                if a:
                    pe.wait_ge(s("h1_ready"), n + 1)
                    at_least(pe, s("h2_copied"), n - 2)
                    for ch in range(4):
                        lo = (ch // 2) * TOK + (ch % 2) * (CH - 1)
                        t = pe.transpose(bank[2][0:CH, D * ch:D * ch + D], h1T[:, k, lo:lo + CH], ident)
                    t.then_inc(s("h1t_done"), 1)
                if b:
                    for j in range(2, 4):
                        pe.wait_ge(s("q_exp"), 4 * mb + j - 1)
                        q_feature(mb, pb, j)
                if fr:
                    at_least(pe, s("rank_read"), n - 3)
                    if k == 0:
                        image_stats(g + 1)
                    for f in TURN[k]:
                        front_piece(g + 1, f)
                if d:
                    pe.wait_ge(s("x2T_copied"), md + 1)
                    pe.wait_ge(s("front_evac"), pieces_by(g, k, fr))
                    if fr and k == 0:
                        pe.wait_ge(s("imgstat_read"), g + 2)
                    for ch in range(4):
                        lo = (ch // 2) * TOK + (ch % 2) * (CH - 1)
                        t = pe.matmul(bank[0][0:CH, E * ch:E * ch + E], x2T[:, lo:lo + CH], wg_sb[:], start=True, stop=True)
                    t.then_inc(s("logit_done"), 1)
                if c:
                    pe.wait_ge(s("rden_ready"), mc + 1)
                for j in range(4):
                    if c:
                        if j:
                            pe.wait_ge(s("qn_done"), 4 * mc + j)
                        pe.matmul(bank[7][:, 0:PT], selr[0:HEADS, j], rden[:], start=True, stop=True).then_inc(s("bc_done"), 1)
                    if b:
                        if j < 2:
                            pe.wait_ge(s("q_exp"), 4 * mb + 3 + j)
                        else:
                            pe.wait_ge(s("k_exp"), 4 * mb + j - 1)
                        lo = (j // 2) * TOK + (j % 2) * (CH - 1)
                        pe.matmul(bank[4 + j % 2][0:CH, :], xT[:, pb, lo:lo + CH], wkp[:], start=True, stop=True
                                  ).then_inc(s("k_mm"), 1)
                if a:
                    pe.wait_ge(s("ln1_x"), n + 1)
                    at_least(pe, s("x2T_copied"), n - 2)
                    transpose_tokens(lambda ch, r: xtok[0:r, pc, ch], s("xt_done"))
                if b:
                    pe.wait_ge(s("x_ones"), mb + 1)
                    pe.wait_ge(s("k_exp"), 4 * mb + 2)
                    at_least(pe, s("m_evac"), 4 * mb)
                    context(pb, 0, bank[6])
                if d:
                    pe.wait_ge(s("before_step"), 4 * (md + 1))
                    pe.wait_ge(s("logit_read"), md + 1)
                    pe.matmul(bank[0][:, 0:5 * E], ones[0:CH], before[:].rearrange("p c e -> p (c e)"), start=True, stop=False)
                    pe.matmul(bank[0][:, 0:4 * E], tri[0:CH], both[:].rearrange("p c e -> p (c e)"), start=False, stop=True
                              ).then_inc(s("rank_done"), 1)
                if c:
                    pe.wait_ge(s("qn_done"), 4 * mc + 4)
                    for i in range(2):
                        for j in range(4):
                            t = pe.matmul(bank[7][:, TOK * i:TOK * i + TOK], mm[:, pc, i, j, 0:D],
                                          qf[:, pc, j, TOK * i:TOK * i + TOK], start=(j == 0), stop=(j == 3))
                    t.then_inc(s("out_done"), 1)
                if b:
                    if a:
                        pe.wait_ge(s("h1_ready"), n + 1)
                    pe.wait_ge(s("k_exp"), 4 * mb + 4)
                    context(pb, 1, bank[1])
                    pe.wait_ge(s("g_copied"), 2 * mb + 1)
                    context_out(0, 0)
                if c:
                    pe.wait_ge(s("attn_added"), mc + 1)
                    if a:
                        pe.wait_ge(s("ln1_x"), n + 1)
                    for ch in range(4):
                        lo = (ch // 2) * TOK + (ch % 2) * (CH - 1)
                        t = pe.transpose(bank[2][0:CH, D * ch:D * ch + D], h1T[:, (k + 2) % 4, lo:lo + CH], ident)
                    t.then_inc(s("h2t_done"), 1)
                if b:
                    pe.wait_ge(s("g_copied"), 2 * mb + 2)
                    context_out(0, 1)
                    pe.wait_ge(s("m_evac"), 4 * mb + 1)
                    context_out(1, 0)
                    pe.wait_ge(s("m_evac"), 4 * mb + 2)
                    context_out(1, 1)

            def transpose_tokens(src, done):
                for ch in range(4):
                    r = HALF_ROWS[ch % 2]
                    lo = (ch // 2) * TOK + (ch % 2) * (CH - 1)
                    t = pe.transpose(bank[3][:, lo:lo + r], src(ch, r), ident[0:r, 0:r])
                t.then_inc(done, 1)

            def q_feature(m, p, j):
                pe.matmul(bank[4 + j % 2][:, 0:PT], wqp[:, 128 * j:128 * j + 128], xT[:, p], start=True, stop=True
                          ).then_inc(s("q_mm"), 1)

            def context(p, i, o_):
                for h in range(2):
                    r = HALF_ROWS[h]
                    t = pe.matmul(o_[:, :], xtok[0:r, p, 2 * i + h], kf[0:r, 2 * i + h], start=(h == 0), stop=(h == 1))
                t.then_inc(s("g_done"), 1)

            def context_out(i, jj):
                o_ = bank[(6, 1)[jj]]
                for h in range(4 * jj, 4 * jj + 4):
                    col = (h // 2 % 2) * (D + HEADS)
                    t = pe.matmul(o_[64 * (h % 2):64 * (h % 2) + 64, col:col + D + HEADS], gT[:, i, NF * h:NF * h + NF],
                                  wvo[:, h], start=True, stop=True)
                t.then_inc(s("m_done"), 1)

            steps(pe, step)

        @block.vector
        def _(ve):
            ve.memset(raw44[:], 0.0).then_inc(s("pads_zero"), 1)
            ve.memset(pjT, 0.0).then_inc(s("setup_zero"), 1)
            ve.memset(woT, 0.0).then_inc(s("setup_zero"), 1)
            ve.memset(before[:], 0.0).then_inc(s("setup_zero"), 1)
            ve.wait_ge(s("small_in"), 16 * NSMALL)
            ve.wait_ge(s("setup_zero"), 3)
            for j in range(4):
                t = ve.tensor_scalar(wv_c[:, j], qkv_raw[:, 2, j], qkv_raw[:, 2, j, D - 1:D], None, ALU.subtract)
            t.then_inc(s("wv_centred"), 1)
            ve.tensor_copy(wvo[:, :, D:], K("e127").rearrange("p (h g) -> p h g", h=HEADS)).then_inc(s("wvo_ready"), 1)
            item = [0]

            def begin():
                item[0] += 1
                ve.wait_ge(s("setup_mm"), item[0])
                return bank[(item[0] - 1) % 8]

            def end(t):
                t.then_inc(s("setup_copied"), 1)

            o_ = begin()
            end(ve.tensor_copy(wct[:, 0:4].rearrange("p g k -> p (g k)"), o_[:, :]))
            o_ = begin()
            ve.tensor_copy(wct[:, 4], o_[:, 0:128])
            for h in range(2):
                t = ve.tensor_copy(pjT[64 * h:64 * h + 64, 64 * h:64 * h + 64], o_[64 * h:64 * h + 64, 128:192])
            end(t)
            o_ = begin()
            for h in range(2):
                t = ve.tensor_copy(woT[64 * h:64 * h + 64, :, h], o_[64 * h:64 * h + 64, :].rearrange("p (j n) -> p j n", j=4))
            end(t)
            o_ = begin()
            end(ve.tensor_scalar(wqp[:], o_[:, :], QS, None, ALU.mult))
            o_ = begin()
            end(ve.tensor_copy(wkp[:], o_[:, :]))
            for jj in range(2):
                o_ = begin()
                end(ve.tensor_copy(wvo[:, 4 * jj:4 * jj + 4, 0:D], o_[:, :].rearrange("p (h n) -> p h n", h=4)))

            def patch_affine(q):
                raw, g = ((graw, q), (braw[:], q - 5))[q // 5]
                if q % 5 == 0:
                    ve.wait_ge(s(("gamma_in", "beta_in")[q // 5]), 16)
                ve.tensor_copy((nrm0, nrm44)[q % 2][0:NP1, 0:NP1].rearrange("p x (k i) -> p k x i", i=PATCH),
                               raw[:, C * g:C * g + C].rearrange("p c k (x i) -> p (c k) x i", i=PATCH)
                               ).then_inc(s("affine_patched"), 1)

            patch_affine(0)
            patch_affine(1)
            for g in range(5):
                o_ = begin()
                end(ve.tensor_copy(gam[:, g], o_[:, 0:TOK].rearrange("p (x y) -> p x y", x=NP1)))
                patch_affine(g + 2)
            for g in range(5):
                o_ = begin()
                if g < 3:
                    patch_affine(g + 7)
                end(ve.tensor_copy(bT[:, g].rearrange("p y x -> p x y"), o_[:, 0:TOK].rearrange("p (x y) -> p x y", x=NP1)))
            o_ = begin()
            end(ve.tensor_scalar(cbeta[:], o_[:, 0:TOK], convb_sb[:, 0:1], None, ALU.add))
            ve.wait_ge(s("setup_copied"), item[0])

            def image_parts(G):
                ve.wait_ge(s("colsum_ready"), 4 * (G + 1))
                sums = colsum[:].rearrange("p (s e) -> p e s", e=2)
                ve.tensor_scalar(part[:, 2:4], sums[:, 0], K("wab")[0:R1, 0:1], None, ALU.mult).then_inc(s("part_a"), 1)
                ve.wait_ge(s("part_a"), G + 1)
                at_least(ve, s("imgstat_done"), G)
                ve.scalar_tensor_tensor(out=part[:, 0:2], in0=sums[:, 1], scalar=K("wab")[0:R1, 1:2], in1=part[:, 2:4],
                                        op0=ALU.mult, op1=ALU.add).then_inc(s("part_ready"), 1)

            def image_var(G):
                ve.wait_ge(s("imgstat_done"), G + 1)
                ve.tensor_copy(imgstat[:], bank[0][0:R1, 504:508].rearrange("p (l s) -> p l s", l=2)).then_inc(s("imgstat_read"), 1)
                ve.wait_ge(s("imgstat_read"), G + 1)
                ve.tensor_tensor(imgtmp[:], imgstat[:, :, 0], imgstat[:, :, 0], ALU.mult).then_inc(s("mean_squared"), 1)
                ve.wait_ge(s("mean_squared"), G + 1)
                ve.tensor_tensor(imgvar[:], imgstat[:, :, 1], imgtmp[:], ALU.subtract).then_inc(s("imgvar_ready"), 1)

            def image_norm(G):
                ve.wait_ge(s("imgrstd_ready"), G + 1)
                at_least(ve, s("front_t"), NPIECE * G)
                ve.tensor_scalar(nrm44[:].rearrange("p x (k i) -> p k x i", i=PATCH),
                                 raw44[:].rearrange("p c k (x i) -> p (c k) x i", i=PATCH), imgstat[:, 0, 0:1], imgrstd[:, 0:1], ALU.subtract, ALU.mult
                                 ).then_inc(s("norm_done"), 1)
                ve.tensor_scalar(nrm0[:].rearrange("p x (k i) -> p k x i", i=PATCH),
                                 raw0[:].rearrange("p c k (x i) -> p (c k) x i", i=PATCH), imgstat[0:R0, 1, 0:1], imgrstd[0:R0, 1:2], ALU.subtract, ALU.mult
                                 ).then_inc(s("norm_done"), 1)

            def front_piece(G, f, par):
                kind, px0, w = PIECES[f]
                ve.wait_ge(s("front_t"), NPIECE * G + f + 1)
                n_ = NP1 if kind == 0 else NP2
                src = bank[0][:, 0:GI * n_ * w].rearrange("p (x b y) -> p x b y", x=w, b=GI)
                for q, dy, dx in ([(0, 0, 0)] if kind == 0 else [(1, 1, 0), (2, 1, 1), (3, 0, 0), (4, 0, 1)]):
                    lo, hi = max(px0 - dx, 0), min(px0 + w - dx, NP1)
                    if lo >= hi:
                        continue
                    i0 = lo + dx - px0
                    dst = patches[:, par, q].rearrange("p b (y x) -> p x b y", y=NP1)
                    for px in range(lo, hi):
                        t = ve.tensor_tensor(dst[:, px], src[:, i0 + px - lo, :, dy:dy + NP1],
                                             gam[:, q, px].unsqueeze(1).to_broadcast([128, GI, NP1]), ALU.mult)
                t.then_inc(s("front_evac"), 1)

            def norm_stats(src, which, m, stat, agg):
                for ch in range(4):
                    ve.bn_stats(bns[:, which, ch], src(ch)).then_inc(stat, 1)
                wait_alone(ve, setup_met, (stat, 4 * m + 4))
                for ch in range(4):
                    ve.bn_aggr(mv[:, which, ch], bns[:, which, ch]).then_inc(agg, 1)

            image_parts(0)
            image_var(0)
            image_norm(0)
            for f in range(NPIECE):
                front_piece(0, f, 0)

            def step(n, k, g, par, a, b, c, d, fr):
                mb, mc, md = n - 1, n - 2, n - 3
                pb, pc, pd = (k + 1) % 2, k % 2, (k + 1) % 2
                half = lambda off: 2 * g + (k + off) // 2
                if a:
                    ve.wait_ge(s("conv_done"), n + 1)
                    at_least(ve, s("h2t_done"), n - 3)
                    ve.tensor_tensor(h1T[:, k].rearrange("p (b t) -> p b t", b=2),
                                     bank[1][:, 0:PT].rearrange("p (b t) -> p b t", b=2),
                                     cbeta[:].unsqueeze(1).to_broadcast([128, 2, TOK]), ALU.add).then_inc(s("h1_ready"), 1)
                if c:
                    ve.wait_ge(s("d8_done"), mc + 1)
                    ve.tensor_scalar(dsum[:], bank[7][0:HEADS, 0:PT], 1e-6, None, ALU.add).then_inc(s("dsum_ready"), 1)
                    ve.wait_ge(s("dsum_ready"), mc + 1)
                    ve.reciprocal(rden[:], dsum[:]).then_inc(s("rden_ready"), 1)
                if fr and k == 0:
                    image_parts(g + 1)
                if a:
                    ve.wait_ge(s("h1t_done"), n + 1)
                    norm_stats(lambda ch: bank[2][0:CH, D * ch:D * ch + D], 0, n, s("ln1_bn"), s("ln1_mv"))
                    ve.wait_ge(s("ln1_rstd"), n + 1)
                    at_least(ve, s("g_done"), 2 * (n - 1))
                    for ch in range(4):
                        t = ve.tensor_scalar(xtok[:, pc, ch], bank[2][0:CH, D * ch:D * ch + D], mv[:, 0, ch, 0:1],
                                             rstd[:, 0, ch:ch + 1], ALU.subtract, ALU.mult)
                    t.then_inc(s("ln1_x"), 1)
                if fr:
                    if k == 0:
                        image_var(g + 1)
                    if k == 1:
                        at_least(ve, s("conv_done"), 4 * g)
                    for f in TURN[k]:
                        front_piece(g + 1, f, 1 - par)
                if d:
                    choose(md)
                if c:
                    for j in range(4):
                        ve.wait_ge(s("bc_done"), 4 * mc + j + 1)
                        ve.tensor_tensor(qf[:, pc, j], qf[:, pc, j], bank[7][:, 0:PT], ALU.mult).then_inc(s("qn_done"), 1)
                if d:
                    place(md, pd, 128 * half(-3))
                if c:
                    ve.wait_ge(s("out_done"), mc + 1)
                    ve.scalar_tensor_tensor(out=h1T[:, (k + 2) % 4], in0=bank[7][:, 0:PT], scalar=bout_sb[:, 0:1],
                                            in1=h1T[:, (k + 2) % 4], op0=ALU.add, op1=ALU.add).then_inc(s("attn_added"), 1)
                if b:
                    at_least(ve, s("out_done"), mb - 1)
                    for f in range(4):
                        ve.wait_ge(s("m_done"), 4 * mb + f + 1)
                        i, jj = f // 2, f % 2
                        ve.tensor_copy(mm[:, pb, i, 2 * jj:2 * jj + 2],
                                       bank[(6, 1)[jj]][:, 0:2 * (D + HEADS)].rearrange("p (j n) -> p j n", j=2)
                                       ).then_inc(s("m_evac"), 1)
                        if a and f == 0:
                            ve.wait_ge(s("xt_done"), n + 1)
                            ve.memset(xtok[:, pc, :, D - 1:D], 1.0).then_inc(s("x_ones"), 1)
                elif a:
                    ve.wait_ge(s("xt_done"), n + 1)
                    ve.memset(xtok[:, pc, :, D - 1:D], 1.0).then_inc(s("x_ones"), 1)
                if c:
                    ve.wait_ge(s("h2_copied"), mc + 1)
                    norm_stats(lambda ch: h2[:, pc, ch], 1, mc, s("ln2_bn"), s("ln2_mv"))
                    ve.wait_ge(s("ln2_rstd"), mc + 1)
                    at_least(ve, s(f"scattered{pc}"), 128 * half(-2))
                    at_least(ve, s("x2t_done"), mc - 1)
                    for ch in range(4):
                        t = ve.tensor_scalar(xrow[:, pc, 0, ch, 0:D], h2[:, pc, ch], mv[:, 1, ch, 0:1],
                                             rstd[:, 1, ch:ch + 1], ALU.subtract, ALU.mult)
                    t.then_inc(s("ln2_x"), 1)
                if fr and k == 0:
                    image_norm(g + 1)

            def choose(m):
                p = None
                ve.wait_ge(s("logit_done"), m + 1)
                ve.tensor_copy(logit[:], bank[0][0:CH, 0:4 * E].rearrange("p (c e) -> p c e", c=4)).then_inc(s("logit_read"), 1)
                wait_alone(ve, setup_met, (s("logit_read"), m + 1))
                for ch in range(4):
                    ve.max(top[:, ch], logit[:, ch]).then_inc(s("top_ready"), 1)
                ve.wait_ge(s("top_ready"), 4 * m + 4)
                ve.tensor_tensor(gap[:], top[:, :, 1], top[:, :, 0], ALU.subtract).then_inc(s("gap_ready"), 1)
                for ch in range(4):
                    t = ve.max_index(topi[:, ch], top[:, ch], logit[:, ch])
                t.then_inc(s("topi_ready"), 1)
                ve.wait_ge(s("topi_ready"), m + 1)
                ve.tensor_tensor(topf[:], topi[:, :, 0:2], K("dup")[0:CH].rearrange("p (c j) -> p c j", c=4), ALU.add
                                 ).then_inc(s("topf_ready"), 1)
                ve.wait_ge(s("topf_ready"), m + 1)
                for j in range(2):
                    t = ve.tensor_tensor(pick[:, j], K("iota8")[0:CH].unsqueeze(1).to_broadcast([CH, 4, E]),
                                         topf[:, :, j:j + 1].to_broadcast([CH, 4, E]), ALU.is_equal)
                t.then_inc(s("pick_ready"), 1)
                ve.wait_ge(s("pick_ready"), m + 1)
                ve.tensor_tensor(both[:], pick[:, 0], pick[:, 1], ALU.add).then_inc(s("both_ready"), 1)
                ve.wait_ge(s("both_ready"), m + 1)
                for ch in range(4):
                    ve.tensor_tensor(before[:, ch + 1], before[:, ch], both[:, ch], ALU.add).then_inc(s("before_step"), 1)
                    if ch < 3:
                        ve.wait_ge(s("before_step"), 4 * m + ch + 1)
                ve.wait_ge(s("before_step"), 4 * m + 4)

            def place(m, p, scattered):
                ve.wait_ge(s("egap_ready"), m + 1)
                ve.tensor_scalar(esum[:], egap[:], 1.0, None, ALU.add).then_inc(s("esum_ready"), 1)
                ve.wait_ge(s("esum_ready"), m + 1)
                ve.reciprocal(xrow[:, p, 0, :, D], esum[:]).then_inc(s("w0_ready"), 1)
                ve.wait_ge(s("w0_ready"), m + 1)
                ve.tensor_tensor(xrow[:, p, 1, :, D], egap[:], xrow[:, p, 0, :, D], ALU.mult).then_inc(s("w1_ready"), 1)
                ve.wait_ge(s("rank_done"), m + 1)
                ranks = bank[0][:, 0:5 * E].rearrange("p (c e) -> p c e", c=5)
                ve.tensor_tensor(slots[:], ranks[0:CH, 0:4], K("iotacap")[0:CH].unsqueeze(1).to_broadcast([CH, 4, E]), ALU.add
                                 ).then_inc(s("slots_ready"), 1)
                ve.tensor_copy(counts[:], ranks[:, 4]).then_inc(s("counts_ready"), 1)
                ve.tensor_copy(before[0:1, 0], ranks[0:1, 4]).then_inc(s("rank_read"), 1)
                ve.wait_ge(s("slots_ready"), m + 1)
                ve.tensor_tensor(pslot[:], slots[:].unsqueeze(1).to_broadcast([CH, 2, 4, E]), pick[:], ALU.mult).then_inc(s("pslot_ready"), 1)
                ve.wait_ge(s("pslot_ready"), m + 1)
                ve.tensor_reduce(slotf[:], pslot[:], AX_X, ALU.add).then_inc(s("slotf_ready"), 1)
                ve.wait_ge(s("slotf_ready"), m + 1)
                at_least(ve, s(f"scattered{p}"), scattered)
                ve.tensor_copy(sloti[:, p], slotf[:]).then_inc(s("sloti_ready"), 1)

            steps(ve, step)

        @block.scalar
        def _(ac):
            edges = sb("edges", [R1, C * PATCH, 2, HALF])
            edge_out = sb("edge_out", [R1, C * PATCH, 2, HALF])

            def image_sums(G):
                at_least(ac, s("front_t"), NPIECE * G)
                at_least(ac, s("norm_done"), 2 * G)
                at_least(ac, s("part_ready"), G)
                ac.wait_ge(s("raw_in"), 16 * NRAW * (G + 1))
                rows = raw44[:].rearrange("p c k x -> p (c k) x")
                for e_, lo in ((0, HALF), (1, S)):
                    ac.activation(edges[:, :, e_], rows[:, :, lo:lo + HALF], ACT.Copy).then_inc(s("edges_ready"), 1)
                ac.activation(nrm44[:].rearrange("p x n -> p (x n)"), raw44[:].rearrange("p c k x -> p (c k x)"), ACT.Copy, accum_out=colsum[:, 0:1]).then_inc(s("colsum_ready"), 1)
                ac.wait_ge(s("edges_ready"), 2 * (G + 1))
                ac.activation(edge_out[:], edges[:], ACT.Copy, accum_out=colsum[:, 1:2]).then_inc(s("colsum_ready"), 1)
                ac.wait_ge(s("colsum_ready"), 4 * G + 2)
                ac.activation(nrm44[:].rearrange("p x n -> p (x n)"), raw44[:].rearrange("p c k x -> p (c k x)"), ACT.Square, accum_out=colsum[:, 2:3]).then_inc(s("colsum_ready"), 1)
                ac.activation(edge_out[:], edges[:], ACT.Square, accum_out=colsum[:, 3:4]).then_inc(s("colsum_ready"), 1)

            ac.wait_ge(s("setup_mm"), 17)
            image_sums(0)

            def step(n, k, g, par, a, b, c, d, fr):
                mb, mc, md = n - 1, n - 2, n - 3
                pb, pc, pd = (k + 1) % 2, k % 2, (k + 1) % 2
                if d:
                    ac.wait_ge(s("x2t_done"), md + 1)
                    at_least(ac, s("logit_done"), md)
                    ac.copy(x2T[:], bank[3][:, 0:PT]).then_inc(s("x2T_copied"), 1)
                if b:
                    at_least(ac, s("out_done"), mb - 1)
                    for j in range(4):
                        ac.wait_ge(s("q_mm"), 4 * mb + j + 1)
                        ac.activation(qf[:, pb, j], bank[4 + j % 2][:, 0:PT], ACT.Exp).then_inc(s("q_exp"), 1)
                if fr and k == 0:
                    image_sums(g + 1)
                if d:
                    ac.wait_ge(s("gap_ready"), md + 1)
                    at_least(ac, s("w1_ready"), md)
                    ac.activation(egap[:], gap[:], ACT.Exp).then_inc(s("egap_ready"), 1)
                if b:
                    at_least(ac, s("g_done"), 2 * mb)
                    for ch in range(4):
                        ac.wait_ge(s("k_mm"), 4 * mb + ch + 1)
                        ac.activation(kf[:, ch], bank[4 + ch % 2][0:CH, :], ACT.Exp).then_inc(s("k_exp"), 1)
                if a:
                    ac.wait_ge(s("xt_done"), n + 1)
                    at_least(ac, s("k_mm"), 4 * (n - 1))
                    ac.copy(xT[:, pc], bank[3][:, 0:PT]).then_inc(s("xT_copied"), 1)
                if b:
                    at_least(ac, s("m_done"), 4 * mb)
                    for i in range(2):
                        ac.wait_ge(s("g_done"), 2 * mb + i + 1)
                        ac.copy(gT[:, i], bank[(6, 1)[i]][:, :]).then_inc(s("g_copied"), 1)
                if c:
                    ac.wait_ge(s("h2t_done"), mc + 1)
                    at_least(ac, s(f"h2_out{pc}"), 64 * (2 * g + (k - 2) // 2))
                    at_least(ac, s("ln2_x"), mc - 1)
                    ac.copy(h2[:, pc].rearrange("p c n -> p (c n)"), bank[2][0:CH, :]).then_inc(s("h2_copied"), 1)
            steps(ac, step)

        @block.gpsimd
        def _(po):
            def root(dst, src, tmp, eps, half, start, v_done, r_done, turn):
                po.tensor_scalar(tmp, src, eps, 1.0, ALU.add, ALU.mult).then_inc(v_done, 1)
                po.wait_ge(v_done, turn + 1)
                po.tensor_tensor(dst, tmp, half, ALU.pow).then_inc(r_done, 1)

            def image_root(G):
                wait_alone(po, setup_met, (s("imgvar_ready"), G + 1), (s("norm_done"), 2 * G))
                root(imgrstd[:], imgvar[:], imgeps[:], 1e-7, K("mhalf")[0:R1, 0:2], 0, s("imgeps_ready"), s("imgrstd_ready"), G)

            imgeps = sb("imgeps", [R1, 2])
            po.wait_ge(s("small_in"), 16 * NSMALL)
            image_root(0)

            def step(n, k, g, par, a, b, c, d, fr):
                mb, mc, md = n - 1, n - 2, n - 3
                pb, pc, pd = (k + 1) % 2, k % 2, (k + 1) % 2
                if a:
                    wait_alone(po, setup_met, (s("ln1_mv"), 4 * (n + 1)), (s("ln1_x"), n))
                    root(rstd[:, 0], mv[:, 0, :, 1], vare[:, 0], 1e-5, K("mhalf")[0:CH], 0, s("ln1_vare"), s("ln1_rstd"), n)
                if fr and k == 0:
                    image_root(g + 1)
                if d:
                    wait_alone(po, setup_met, (s("sloti_ready"), md + 1), (s("w1_ready"), md + 1),
                               (s("row_ready"), 3 * (md + 1)))
                    for ch in range(4):
                        r = HALF_ROWS[ch % 2]
                        for j in range(2):
                            po.indirect_dma_start(sorted_rows, bass.IndirectOffsetOnAxis(sloti[0:r, pd, j, ch:ch + 1], 0),
                                                  xrow[0:r, pd, j, ch], None).then_inc(s(f"scattered{pd}"), 16)
                if c:
                    wait_alone(po, setup_met, (s("ln2_mv"), 4 * (mc + 1)), (s("ln2_x"), mc))
                    root(rstd[:, 1], mv[:, 1, :, 1], vare[:, 1], 1e-5, K("mhalf")[0:CH], 0, s("ln2_vare"), s("ln2_rstd"), mc)
                    wait_alone(po, setup_met, (s("ln2_x"), mc + 1), (s("tok_next"), mc))
                    po.tensor_copy(xrow[:, pc, 1, :, 0:D], xrow[:, pc, 0, :, 0:D]).then_inc(s("row_ready"), 1)
                    for j in range(2):
                        po.tensor_copy(xrow[:, pc, j, :, D + 1], tokid[:]).then_inc(s("row_ready"), 1)
                    wait_alone(po, setup_met, (s("row_ready"), 3 * (mc + 1)))
                    po.tensor_scalar(tokid[:], tokid[:], float(PT), 1.0, ALU.add, ALU.mult).then_inc(s("tok_next"), 1)
            steps(po, step)
            for q in range(2):
                po.wait_ge(s(f"scattered{q}"), NPAIR // 2 * 128)



def experts(nc, ffw, ffv, ffw2, out, cst, counts, sorted_rows, bank):
    with ExitStack() as ctx:
        def sb(name, shape, dt=F32):
            return ctx.enter_context(nc.sbuf_tensor(name, shape, dt))

        def K(k):
            return cst[:, SEG[k][0]:SEG[k][1]]

        ident = K("ident")
        padidx = sb("padidx", [128, 16])
        padidxi = sb("padidxi", [128, 16], U32)
        has = sb("has", [1, E, 43])
        tiles = sb("tiles", [1, E])
        upto = sb("upto", [1, E, E])
        cum = sb("cum", [1, E])
        past = sb("past", [1, NT, E])
        pastn = sb("pastn", [1, NT, E])
        owner = sb("owner", [1, NT])
        first = sb("first", [1, NT])
        inner = sb("inner", [1, NT])
        base = sb("base", [1, NT])
        row = sb("row", [1, NT])
        table = sb("table", [1, NT, 2], I32)
        xr = sb("xr", [128, 2, 2, RW])
        gate = sb("gate", [128, 2, 2])
        dest = sb("dest", [128, 2, 2], U32)
        xT = sb("xT_e", [128, 2, TT])
        wv = sb("wv", [128, 2, 2, F])
        w2 = sb("w2", [128, 2, 4, D])
        sil = sb("sil", [128, 2, TT])
        hid = sb("hid", [128, 2, 4, TT])
        yo = sb("yo", [128, 2, 2, D])
        S_ = {}

        def s(name):
            if name not in S_:
                S_[name] = ctx.enter_context(nc.semaphore(name))
            return S_[name]

        def steps(step):
            def run(eng):
                step(0, 0, 0, True, False)
                step(1, 0, 1, True, True)
                with eng.Fori(0, (NT - 4) // 2) as i:
                    step(2 * i + 2, i + 1, 0, True, True)
                    step(2 * i + 3, i + 1, 1, True, True)
                step(NT - 2, NT // 2 - 1, 0, True, True)
                step(NT - 1, NT // 2 - 1, 1, False, True)
            return run

        block = ctx.enter_context(nc.Block())

        @block.sync
        def _(sp):
            sp.wait_ge(s("table_ready"), 1)
            sp.wait_ge(s("padded"), 256)

            def load(t, h, p):
                r = sp.value_load(table[0:1, bass.ds(t, 1), 0], min_val=0, max_val=E * CAP)
                e = sp.value_load(table[0:1, bass.ds(t, 1), 1], min_val=0, max_val=E - 1)
                at_least(sp, s("tok_t"), t - 1)
                at_least(sp, s("meta_done"), t - 1)
                sp.dma_start(xr[:, p], sorted_rows[bass.ds(r, TT)].rearrange("(p a) n -> p a n", a=2)
                             ).then_inc(s(f"rows_in{p}"), 16)
                at_least(sp, s("hv_done"), 4 * (t - 1))
                sp.dma_start(wv[:, p, 0], ffw[bass.ds(e, 1)].rearrange("e d f -> (e d) f")).then_inc(s(f"wv_in{p}"), 16)
                sp.dma_start(wv[:, p, 1], ffv[bass.ds(e, 1)].rearrange("e d f -> (e d) f")).then_inc(s(f"wv_in{p}"), 16)
                at_least(sp, s("y_done"), t - 1)
                sp.dma_start(w2[:, p], ffw2[bass.ds(e, 1)].rearrange("e (c f) d -> (e f) c d", c=4)
                             ).then_inc(s(f"w2_in{p}"), 16)

            load(0, 0, 0)
            load(1, 0, 1)
            with sp.Fori(0, (NT - 2) // 2) as i:
                load(2 * i + 2, i + 1, 0)
                load(2 * i + 3, i + 1, 1)

        @block.tensor
        def _(pe):
            def turn(t, h, p):
                pe.wait_ge(s(f"rows_in{p}"), 16 * (h + 1))
                at_least(pe, s("xT_copied_e"), t - 1)
                for a in range(2):
                    q = pe.transpose(bank[6 + p][:, 128 * a:128 * a + 128], xr[:, p, a, 0:D], ident)
                q.then_inc(s("tok_t"), 1)

            def hidden(t, h, p, fc):
                if fc == 0:
                    pe.wait_ge(s("xT_copied_e"), t + 1)
                    pe.wait_ge(s(f"wv_in{p}"), 32 * (h + 1))
                at_least(pe, s("h_done"), 4 * (t - 1) + fc + 1)
                for m in range(2):
                    q = pe.matmul(bank[fc][:, TT * m:TT * m + TT], wv[:, p, m, 128 * fc:128 * fc + 128], xT[:, p], start=True, stop=True)
                q.then_inc(s("hv_done"), 1)

            def down(t, h, p):
                pe.wait_ge(s("h_done"), 4 * t + 4)
                pe.wait_ge(s(f"w2_in{p}"), 16 * (h + 1))
                at_least(pe, s("y_scaled"), t - 1)
                for a in range(2):
                    for fc in range(4):
                        q = pe.matmul(bank[4 + p][:, D * a:D * a + D], hid[:, p, fc, 128 * a:128 * a + 128], w2[:, p, fc],
                                      start=(fc == 0), stop=(fc == 3))
                q.then_inc(s("y_done"), 1)

            def step(t, h, p, more, prev):
                hidden(t, h, p, 0)
                hidden(t, h, p, 1)
                if prev:
                    down(t - 1, h - 1 + p, 1 - p)
                hidden(t, h, p, 2)
                hidden(t, h, p, 3)
                if more:
                    turn(t + 1, h + p, 1 - p)

            turn(0, 0, 0)
            steps(step)(pe)
            down(NT - 1, (NT - 1) // 2, 1)

        @block.scalar
        def _(ac):
            def copy_x(t, h, p):
                ac.wait_ge(s("tok_t"), t + 1)
                at_least(ac, s("hv_done"), 4 * (t - 1))
                ac.copy(xT[:, p], bank[6 + p][:, 0:TT]).then_inc(s("xT_copied_e"), 1)

            def step(t, h, p, more, prev):
                for fc in range(4):
                    ac.wait_ge(s("hv_done"), 4 * t + fc + 1)
                    at_least(ac, s("h_done"), 4 * t + fc - 1)
                    ac.activation(sil[:, fc % 2], bank[fc][:, 0:TT], ACT.Silu).then_inc(s("silu_done"), 1)
                if more:
                    copy_x(t + 1, h + p, 1 - p)

            copy_x(0, 0, 0)
            steps(step)(ac)

        @block.vector
        def _(ve):
            link = [0]

            def chain(q):
                link[0] += 1
                q.then_inc(s("table_step"), 1)
                ve.wait_ge(s("table_step"), link[0])

            chain(ve.tensor_tensor(padidx[:].rearrange("p (a e) -> p a e", a=2), K("padslot").rearrange("p (a e) -> p a e", a=2),
                                   counts[:].unsqueeze(1).to_broadcast([128, 2, E]), ALU.add))
            ve.tensor_copy(padidxi[:], padidx[:]).then_inc(s("padidx_ready"), 1)
            chain(ve.tensor_tensor(has[:], counts[0:1].unsqueeze(2).to_broadcast([1, E, 43]),
                                   K("steps")[0:1].unsqueeze(1).to_broadcast([1, E, 43]), ALU.is_gt))
            chain(ve.tensor_reduce(tiles[:], has[:], AX_X, ALU.add))
            chain(ve.tensor_tensor(upto[:], tiles[:].unsqueeze(1).to_broadcast([1, E, E]),
                                   K("incl")[0:1].rearrange("p (a b) -> p a b", a=E), ALU.mult))
            chain(ve.tensor_reduce(cum[:], upto[:], AX_X, ALU.add))
            chain(ve.tensor_tensor(past[:], K("tile")[0:1].unsqueeze(2).to_broadcast([1, NT, E]),
                                   cum[:].unsqueeze(1).to_broadcast([1, NT, E]), ALU.is_ge))
            chain(ve.tensor_tensor(pastn[:], past[:], tiles[:].unsqueeze(1).to_broadcast([1, NT, E]), ALU.mult))
            chain(ve.tensor_reduce(owner[:], past[:], AX_X, ALU.add))
            chain(ve.tensor_reduce(first[:], pastn[:], AX_X, ALU.add))
            chain(ve.tensor_tensor(inner[:], K("tile")[0:1], first[:], ALU.subtract))
            chain(ve.tensor_scalar(base[:], owner[:], float(CAP), None, ALU.mult))
            chain(ve.scalar_tensor_tensor(out=row[:], in0=inner[:], scalar=float(TT), in1=base[:], op0=ALU.mult, op1=ALU.add))
            ve.tensor_scalar(table[:, :, 0], row[:], float(E * CAP), None, ALU.min)
            ve.tensor_scalar(table[:, :, 1], owner[:], float(E - 1), None, ALU.min).then_inc(s("table_ready"), 1)

            def meta(t, h, p):
                ve.wait_ge(s(f"rows_in{p}"), 16 * (h + 1))
                at_least(ve, s("added"), 32 * (t - 1))
                ve.tensor_copy(gate[:, p], xr[:, p, :, D])
                ve.tensor_copy(dest[:, p], xr[:, p, :, D + 1]).then_inc(s("meta_done"), 1)

            def product(t, p, fc):
                ve.wait_ge(s("silu_done"), 4 * t + fc + 1)
                if fc == 0:
                    at_least(ve, s("y_done"), t - 1)
                ve.tensor_tensor(hid[:, p, fc], sil[:, fc % 2], bank[fc][:, TT:2 * TT], ALU.mult).then_inc(s("h_done"), 1)

            def scale(t, p):
                ve.wait_ge(s("y_done"), t + 1)
                ve.wait_ge(s("meta_done"), t + 1)
                at_least(ve, s("added"), 32 * (t - 1))
                for a in range(2):
                    q = ve.tensor_scalar(yo[:, p, a], bank[4 + p][:, D * a:D * a + D], gate[:, p, a:a + 1], None, ALU.mult)
                q.then_inc(s("y_scaled"), 1)

            def step(t, h, p, more, prev):
                product(t, p, 0)
                product(t, p, 1)
                if prev:
                    scale(t - 1, 1 - p)
                product(t, p, 2)
                product(t, p, 3)
                if more:
                    meta(t + 1, h + p, 1 - p)

            meta(0, 0, 0)
            steps(step)(ve)
            scale(NT - 1, 1)

        @block.gpsimd
        def _(po):
            po.wait_ge(s("padidx_ready"), 1)
            pad = K("padrow").rearrange("p (a n) -> p a n", a=2)
            for e in range(E):
                for a in range(2):
                    po.indirect_dma_start(sorted_rows, bass.IndirectOffsetOnAxis(padidxi[:, E * a + e:E * a + e + 1], 0),
                                          pad[:, a], None).then_inc(s("padded"), 16)

            def add(t, p):
                wait_alone(po, (s("padidx_ready"), 1), (s("y_scaled"), t + 1), (s("added"), 32 * t))
                for a in range(2):
                    po.indirect_dma_start(out, bass.IndirectOffsetOnAxis(dest[:, p, a:a + 1], 0), yo[:, p, a], None,
                                          compute_op=ALU.add).then_inc(s("added"), 16)

            add(0, 0)
            add(1, 1)
            with po.Fori(1, NT // 2) as i:
                add(2 * i, 0)
                add(2 * i + 1, 1)
            po.wait_ge(s("added"), 32 * NT)


_INS = ["x", "L0_tok_gamma", "L0_tok_beta", "L0_tok_W", "L0_tok_b", "L0_attn_Wqkv", "L0_attn_Wout", "L0_attn_bout",
        "L0_attn_proj", "L0_ffn_Wg", "L0_ffn_W", "L0_ffn_V", "L0_ffn_W2"]


def kernel(**inputs):
    import numpy as _np
    import concourse.bacc as _bacc
    from concourse import mybir as _mybir
    from concourse.bass_utils import run_bass_kernel_spmd as _run

    nc = _bacc.Bacc("TRN2", target_bir_lowering=False, num_devices=1)
    arrays, args = {}, []
    for name in _INS:
        a = _np.ascontiguousarray(inputs[name])
        arrays[f"in_{name}"] = a
        args.append(nc.dram_tensor(f"in_{name}", a.shape, _mybir.dt.from_np(a.dtype), kind="ExternalInput").ap())
    c = constants()
    arrays["in_const"] = c
    args.append(nc.dram_tensor("in_const", c.shape, F32, kind="ExternalInput").ap())
    args.append(nc.dram_tensor("out_rows", (NTOK + TT, D), F32, kind="ExternalOutput").ap())
    build(nc, *args)
    r = _run(nc, [arrays], core_ids=[0])
    return r.results[0]["out_rows"][:NTOK].reshape(B, TOK, D)
```

```python
from contextlib import ExitStack

import numpy as np

import concourse.bass as bass
from concourse import mybir

F32 = mybir.dt.float32
F32R = mybir.dt.float32r
U32 = mybir.dt.uint32
I32 = mybir.dt.int32
ALU = mybir.AluOpType
ACT = mybir.ActivationFunctionType
AX_X = mybir.AxisListType.X

B, C, S = 64, 2, 104
PATCH, HALF = 8, 4
NP1 = S // PATCH
NP2 = NP1 + 1
TOK = NP1 * NP1
D = 128
HEADS, DH, NF = 8, 64, 64
F, E = 512, 8
NTOK = B * TOK
GI = 8
NG = B // GI
R0, R1 = GI * NP1, GI * NP2
PW = S + 2 * HALF
NPAIR = B // 2
PT = 2 * TOK
CH = 85
HALF_ROWS = [CH - 1, CH]
NSTAT = 5 * C * S * S
CAP = NTOK + 256
TT = 256
NT = (2 * NTOK) // TT + E
RW = D + 2
QS = DH ** -0.5

_SEGS = dict(ident=128, sel44=R1, sel0=R1, wab=2, selr=HEADS // 2 * 128, e127=HEADS * HEADS, iota8=8, iotacap=8,
             dup=8, tri=128, ones=128, tok=4, mhalf=4, padrow=2 * RW, padslot=16, tile=NT, steps=43, incl=E * E)
SEG, _o = {}, 0
for _k, _n in _SEGS.items():
    SEG[_k] = (_o, _o + _n)
    _o += _n
NCONST = _o


def constants():
    c = np.zeros((128, NCONST), np.float32)

    def seg(k):
        return c[:, SEG[k][0]:SEG[k][1]]

    p = np.arange(128)
    seg("ident")[:] = np.eye(128)
    same = (p[:R1, None] // NP2 == np.arange(R1)[None] // NP2) / NSTAT
    seg("sel44")[:R1] = same
    seg("sel0")[:R1, :R0] = (p[:R1, None] // NP2 == np.arange(R0)[None] // NP1) / NSTAT
    edge = ((p % NP2 == 0) | (p % NP2 == NP2 - 1)).astype(np.float32)
    seg("wab")[:, 0] = 5 - 2 * edge
    seg("wab")[:, 1] = edge - 2
    for h in range(HEADS):
        seg("selr")[h, h * NF:(h + 1) * NF] = 1
        seg("selr")[32 + h, h * NF:(h + 1) * NF] = 1
        seg("e127")[D - 1, h * HEADS + h] = 1
    seg("iota8")[:] = np.arange(8)
    seg("iotacap")[:] = np.arange(8) * CAP
    for ch in (0, 2):
        seg("dup")[CH - 1, 2 * ch:2 * ch + 2] = 100
    seg("tri")[:] = p[:, None] < p[None]
    seg("ones")[:] = 1
    for ch in range(4):
        seg("tok")[:, ch] = (ch // 2) * TOK + (ch % 2) * (CH - 1) + p
    seg("mhalf")[:] = -0.5
    for a in range(2):
        seg("padrow")[:, a * RW + RW - 1] = NTOK + a * 128 + p
        seg("padslot")[:, 8 * a:8 * a + 8] = np.arange(8)[None] * CAP + a * 128 + p[:, None]
    seg("tile")[:] = np.arange(NT)
    seg("steps")[:] = np.arange(43) * TT
    seg("incl")[:] = np.tril(np.ones((E, E))).reshape(-1)
    return c


def at_least(eng, sem, value):
    if not (isinstance(value, int) and value <= 0):
        eng.wait_ge(sem, value)


def wait_alone(eng, met, *waits):
    waits = [(q, v if isinstance(v, int) else eng.to_reg(v)) for q, v in waits]
    eng.wait_ge(*met)
    for q, v in waits:
        at_least(eng, q, v)


def build(nc, x, gamma, beta, convw, convb, wqkv, wout, bout, proj, wg, ffw, ffv, ffw2, const, out):
    with ExitStack() as ctx:
        cst = ctx.enter_context(nc.sbuf_tensor("cst", [128, NCONST], F32))
        counts = ctx.enter_context(nc.sbuf_tensor("counts", [128, E], F32))
        table = ctx.enter_context(nc.sbuf_tensor("table", [1, NT, 2], I32))
        sorted_rows = nc.dram_tensor("sorted_rows", [E * CAP + TT, RW], F32, kind="Internal").ap()
        bank = [ctx.enter_context(nc.psum_tensor(f"bank{i}", [128, 512], F32)) for i in range(8)]
        tokens(nc, x, gamma, beta, convw, convb, wqkv, wout, bout, proj, wg, const, out, cst, counts, table, sorted_rows, bank)
        experts(nc, ffw, ffv, ffw2, out, cst, table, sorted_rows, bank)


def tokens(nc, x, gamma, beta, convw, convb, wqkv, wout, bout, proj, wg, const, out, cst, counts, table, sorted_rows, bank):
    with ExitStack() as ctx:
        def sb(name, shape, dt=F32):
            return ctx.enter_context(nc.sbuf_tensor(name, shape, dt))

        def sem(name):
            return ctx.enter_context(nc.semaphore(name))

        def K(k):
            return cst[:, SEG[k][0]:SEG[k][1]]

        ident, ones, tri = K("ident"), K("ones"), K("tri")
        patches = sb("patches", [128, 2, 5, GI, TOK])
        raw0 = sb("raw0", [R0, C, PATCH, S])
        raw44 = sb("raw44", [R1, C, PATCH, PW])
        nrm0 = sb("nrm0", [R0, NP1, D])
        nrm44 = sb("nrm44", [R1, NP2, D])
        colsum = sb("colsum", [R1, 4])
        part = sb("part", [R1, 4])
        imgstat = sb("imgstat", [R1, 2, 2])
        imgtmp = sb("imgtmp", [R1, 2])
        imgvar = sb("imgvar", [R1, 2])
        imgrstd = sb("imgrstd", [R1, 2])
        gam = sb("gam", [128, 5, NP1, NP1])
        cbeta = sb("cbeta", [128, TOK])
        wct = sb("wct", [128, 5, D])
        wqp = sb("wqp", [128, 2, HEADS * NF], F32R)
        wkp = sb("wkp", [128, 2, HEADS * NF], F32R)
        pick_head = sb("pick_head", [40, 4, 128], F32R)
        wvo = sb("wvo", [128, HEADS, D + HEADS])
        wg_sb = sb("wg_sb", [128, E])
        bout_sb = sb("bout_sb", [128, 1])
        convb_sb = sb("convb_sb", [128, 1])
        h1T = sb("h1T", [128, 4, PT])
        xtok = sb("xtok", [CH, 2, 4, D])
        xT = sb("xT", [128, 2, 2, 384], F32R)
        attn = sb("attn", [128, 8 * PT + 6 * HEADS * NF + 16 * (D + HEADS) + 8 * D])
        taken = [0]

        def piece(width, rows=128):
            taken[0] += width
            return attn[0:rows, taken[0] - width:taken[0]]

        qf = piece(8 * PT).rearrange("p (s j t) -> p s j t", s=2, j=4)
        kf = piece(4 * HEADS * NF, CH).rearrange("p (c n) -> p c n", c=4)
        gT = piece(2 * HEADS * NF).rearrange("p (i n) -> p i n", i=2)
        mm = piece(16 * (D + HEADS)).rearrange("p (s i j n) -> p s i j n", s=2, i=2, j=4)
        h2 = piece(8 * D, CH).rearrange("p (s c n) -> p s c n", s=2, c=4)
        braw = attn[0:NP1, 0:5 * C * PATCH * S].rearrange("p (c k x) -> p c k x", c=5 * C, k=PATCH)
        dsum = sb("dsum", [HEADS, PT])
        rden = sb("rden", [HEADS, PT])
        rparts = sb("rparts", [40, PT], F32R)
        xrow = sb("xrow", [CH, 2, 2, 4, RW])
        x2T = sb("x2T", [128, PT])
        bns = sb("bns", [CH, 2, 4, 6])
        mv = sb("mv", [CH, 2, 4, 2])
        rstd = sb("rstd", [CH, 2, 4])
        vare = sb("vare", [CH, 2, 4])
        logit = sb("logit", [CH, 4, E])
        top = sb("top", [CH, 4, 8])
        topi = sb("topi", [CH, 4, 8], U32)
        topf = sb("topf", [CH, 4, 2])
        gap = sb("gap", [CH, 4])
        egap = sb("egap", [CH, 4])
        esum = sb("esum", [CH, 4])
        pick = sb("pick", [CH, 2, 4, E])
        both = sb("both", [CH, 4, E])
        before = sb("before", [CH, 5, E])
        slots = sb("slots", [CH, 4, E])
        pslot = sb("pslot", [CH, 2, 4, E])
        slotf = sb("slotf", [CH, 2, 4])
        sloti = sb("sloti", [CH, 2, 2, 4], U32)
        tokid = sb("tokid", [CH, 4])
        zeros = sb("zeros", [128, 384])
        endf = sb("endf", [1, E])
        ends = sb("ends", [1, E], I32)
        has = sb("has", [1, E, 43])
        tiles = sb("tiles", [1, E])
        upto = sb("upto", [1, E, E])
        cum = sb("cum", [1, E])
        past = sb("past", [1, NT, E])
        pastn = sb("pastn", [1, NT, E])
        owner = sb("owner", [1, NT])
        first_tile = sb("first_tile", [1, NT])
        inner = sb("inner", [1, NT])
        base = sb("base", [1, NT])
        row = sb("row", [1, NT])
        big = patches[:].rearrange("p s g b t -> p (s g b t)")
        graw = big[0:NP1, 0:5 * C * PATCH * S].rearrange("p (c k x) -> p c k x", c=5 * C, k=PATCH)
        S_ = {}

        def s(name):
            if name not in S_:
                S_[name] = sem(name)
            return S_[name]

        w_conv = convw.rearrange("e c y x -> e (c y x)")
        w_qkv = wqkv.rearrange("(t j e) d -> e t j d", t=3, e=128)
        o = 5 * C * PATCH * S
        wc_raw = big[:, o:o + 640].rearrange("p (g k) -> p g k", g=5)
        wo_raw = big[:, o + 640:o + 1152].rearrange("p (j e) -> p j e", j=4)
        pj_raw = big[0:NF, o + 1152:o + 1280].rearrange("p (t d) -> p t d", t=2)
        pjT = big[:, o + 1280:o + 1408]
        woT = big[:, o + 1408:o + 2432].rearrange("p (j h n) -> p j h n", j=4, h=2)
        bT = big[:, o + 2432:o + 3277].rearrange("p (g y x) -> p g y x", g=5, y=NP1)
        wv_c = big[:, o + 3277:o + 3789].rearrange("p (j d) -> p j d", j=4)
        qkv_raw = sb("qkv_raw", [128, 3, 4, D])

        image_sum = bank[0][0:R1, 0:4]
        logits = bank[6][:, 0:4 * E]
        ranks = bank[2][:, 0:5 * E]

        block = ctx.enter_context(nc.Block())

        def steps(eng, step):
            def group(g, first=False, fr=True, par=0):
                for k in range(4):
                    step(4 * g + k, k, g, par, True, not (first and k < 1), not (first and k < 2),
                         not (first and k < 3), fr)
            group(0, first=True)
            with eng.Fori(0, (NG - 2) // 2) as i:
                group(2 * i + 1, par=1)
                group(2 * i + 2, par=0)
            group(NG - 1, fr=False, par=1)
            for k in range(3):
                step(NPAIR + k, k, NG, 0, False, k < 1, k < 2, True, False)

        def pairs(n):
            return min(n, NPAIR) if isinstance(n, int) else n

        def pairs4(n):
            return 4 * pairs(n)

        PIECES = [(0, 0, 4), (0, 4, 4), (0, 8, 4), (0, 12, 1), (1, 0, 4), (1, 4, 4), (1, 8, 4), (1, 12, 2)]
        NPIECE = len(PIECES)
        TURN = {0: [], 1: [], 2: [0, 1, 2, 3], 3: [4, 5, 6, 7]}

        NRAW = 3 * GI + 4
        NSMALL = 10

        setup_met = (s("small_in"), 16 * NSMALL)

        @block.sync
        def _(sp):
            sp.dma_start(cst[:], const).then_inc(s("small_in"), 16)
            sp.dma_start(wc_raw, convw.rearrange("e (g c) y x -> e g (c y x)", g=5)).then_inc(s("small_in"), 16)
            sp.dma_start(qkv_raw[:], wqkv.rearrange("(t j e) d -> e t j d", t=3, e=128)).then_inc(s("small_in"), 16)
            sp.dma_start(wo_raw, wout.rearrange("o (j e) -> o j e", j=4)).then_inc(s("small_in"), 16)
            for t in range(2):
                sp.dma_start(pj_raw[:, t], proj).then_inc(s("small_in"), 16)
            sp.dma_start(wg_sb[:], wg).then_inc(s("small_in"), 16)
            sp.dma_start(bout_sb[:], bout.rearrange("(d a) -> d a", a=1)).then_inc(s("small_in"), 16)
            sp.dma_start(convb_sb[:], convb.rearrange("(d a) -> d a", a=1)).then_inc(s("small_in"), 16)
            sp.dma_start(tokid[:], const[0:CH, SEG["tok"][0]:SEG["tok"][1]]).then_inc(s("small_in"), 16)
            sp.dma_start(graw, gamma.rearrange("c (y k) x -> y c k x", k=PATCH)).then_inc(s("gamma_in"), 16)
            sp.dma_start(braw, beta.rearrange("c (y k) x -> y c k x", k=PATCH)).then_inc(s("beta_in"), 16)

            def load_group(g):
                at_least(sp, s("norm_done"), 2 * g)
                for b in range(GI):
                    img = x[bass.ds(GI * g + b, 1)].rearrange("b c y x -> (b c) y x")
                    sp.dma_start(raw0[NP1 * b:NP1 * (b + 1)], img.rearrange("c (y k) x -> y c k x", k=PATCH)
                                 ).then_inc(s("raw_in"), 16)
                    for c in range(C):
                        sp.dma_start(raw44[NP2 * b + 1:NP2 * b + NP1, c, :, HALF:HALF + S],
                                     img[c, HALF:S - HALF].rearrange("(y k) x -> y k x", k=PATCH)
                                     ).then_inc(s("raw_in"), 16)
                imgs = x[bass.ds(GI * g, GI)]
                for c in range(C):
                    for p0, k0, y0 in ((0, HALF, 0), (NP1, 0, S - HALF)):
                        sp.dma_start(raw44[p0:R1:NP2, c, k0:k0 + HALF, HALF:HALF + S], imgs[:, c, y0:y0 + HALF]
                                     ).then_inc(s("raw_in"), 16)

            sp.wait_ge(s("pads_zero"), 1)
            load_group(0)
            sp.wait_ge(s("small_in"), 16 * NSMALL)
            pad = K("padrow").rearrange("p (a n) -> p a n", a=2)
            sp.dma_start(out[NTOK:NTOK + TT].rearrange("(a p) n -> p a n", a=2), pad[:, :, 0:D]).then_inc(s("pads_out"), 16)
            sp.dma_start(sorted_rows[E * CAP:E * CAP + TT].rearrange("(a p) n -> p a n", a=2), pad).then_inc(s("pads_out"), 16)

            def step(n, k, g, par, a, b, c, d, fr):
                if fr and k == 0:
                    load_group(g + 1)
                if c:
                    m = n - 2
                    sp.wait_ge(s("h2_copied"), m + 1)
                    for ch in range(4):
                        r = HALF_ROWS[ch % 2]
                        sp.dma_start(out[bass.ds(m * PT + (ch // 2) * TOK + (ch % 2) * (CH - 1), r)],
                                     h2[0:r, k % 2, ch]).then_inc(s(f"h2_out{k % 2}"), 16)
            steps(sp, step)
            sp.wait_ge(s("ends_ready"), 1)
            for e in range(E):
                r = sp.value_load(ends[0:1, e:e + 1], min_val=e * CAP, max_val=e * CAP + NTOK)
                sp.dma_start(sorted_rows[bass.ds(r, TT)].rearrange("(a p) n -> p a n", a=2), pad).then_inc(s("pads_out"), 16)
            for q in range(2):
                sp.wait_ge(s(f"h2_out{q}"), NPAIR // 2 * 64)
            sp.wait_ge(s("pads_out"), 16 * (2 + E))

        @block.tensor
        def _(pe):
            item = [0]

            def begin():
                at_least(pe, s("setup_copied"), item[0] - 7)
                item[0] += 1
                return bank[(item[0] - 1) % 8]

            def end(mm):
                mm.then_inc(s("setup_mm"), 1)

            pe.wait_ge(s("small_in"), 16 * NSMALL)
            o_ = begin()
            for g in range(4):
                mm_ = pe.transpose(o_[:, 128 * g:128 * g + 128], wc_raw[:, g], ident)
            end(mm_)
            o_ = begin()
            pe.transpose(o_[:, 0:128], wc_raw[:, 4], ident)
            end(pe.transpose(o_[:, 128:192], pj_raw.rearrange("p t d -> p (t d)"), ident[0:NF, 0:NF]))
            o_ = begin()
            for j in range(4):
                mm_ = pe.transpose(o_[:, 128 * j:128 * j + 128], wo_raw[:, j], ident)
            end(mm_)
            pe.wait_ge(s("setup_copied"), 2)
            for t in range(2):
                o_ = begin()
                for j in range(4):
                    mm_ = pe.matmul(o_[:, 128 * j:128 * j + 128], qkv_raw[:, t, j], pjT, start=True, stop=True)
                end(mm_)
            pe.wait_ge(s("setup_copied"), 3)
            pe.wait_ge(s("wv_centred"), 1)
            for jj in range(2):
                o_ = begin()
                for j in range(2 * jj, 2 * jj + 2):
                    mm_ = pe.matmul(o_[:, 256 * (j % 2):256 * (j % 2) + 256], wv_c[:, j],
                                    woT[:, j].rearrange("p h n -> p (h n)"), start=True, stop=True)
                end(mm_)
            for q in range(10):
                o_ = begin()
                pe.wait_ge(s("affine_patched"), q + 1)
                for px in range(NP1):
                    mm_ = pe.transpose(o_[:, NP1 * px:NP1 * px + NP1], (nrm0, nrm44)[q % 2][0:NP1, px], ident[0:NP1, 0:NP1])
                end(mm_)
            pe.wait_ge(s("setup_copied"), 17)
            o_ = begin()
            for g in range(5):
                mm_ = pe.matmul(o_[:, 0:TOK], wct[:, g], bT[:, g].rearrange("p y x -> p (y x)"), start=(g == 0), stop=(g == 4))
            end(mm_)
            pe.wait_ge(s("setup_copied"), item[0])

            def image_stats(G):
                pe.wait_ge(s("part_ready"), G + 1)
                at_least(pe, s("front_evac"), NPIECE * G)
                pe.matmul(image_sum[:, 0:2], K("sel44")[0:R1], part[:, 0:2], start=True, stop=True)
                pe.matmul(image_sum[:, 2:4], K("sel0")[0:R1], part[:, 0:2], start=True, stop=True
                          ).then_inc(s("imgstat_done"), 1)

            def front_piece(G, f):
                kind, px0, w = PIECES[f]
                pe.wait_ge(s("norm_done"), 2 * (G + 1))
                at_least(pe, s("front_evac"), NPIECE * G + f)
                if f == 0:
                    pe.wait_ge(s("imgstat_read"), G + 1)
                src, rows = ((nrm0, R0), (nrm44, R1))[kind]
                for i in range(w):
                    px = px0 + i
                    t = pe.transpose(bank[0][:, rows * i:rows * i + rows], src[:, px], ident[0:rows, 0:rows])
                t.then_inc(s("front_t"), 1)

            image_stats(0)
            for f in range(NPIECE):
                front_piece(0, f)

            def step(n, k, g, par, a, b, c, d, fr):
                mb, mc, md = n - 1, n - 2, n - 3
                pb, pc, pd = (k + 1) % 2, k % 2, (k + 1) % 2

                def front(i):
                    if fr and len(TURN[k]) > i:
                        front_piece(g + 1, TURN[k][i])

                def broadcast(j):
                    pe.matmul(bank[(7, 1)[j % 2]][:, 0:PT], pick_head[:, j], rparts[:], start=True, stop=True
                              ).then_inc(s("bc_done"), 1)

                def k_tokens(j):
                    lo = (j // 2) * TOK + (j % 2) * (CH - 1)
                    products(bank[4 + j % 2][:, :], lambda a_: xT[:, pb, a_, lo:lo + 128], lambda a_: wkp[:, a_]
                             ).then_inc(s("k_mm"), 1)

                def q_feature(j):
                    products(bank[4 + j % 2][:, 0:PT], lambda a_: wqp[:, a_, 128 * j:128 * j + 128],
                             lambda a_: xT[:, pb, a_, 0:PT]).then_inc(s("q_mm"), 1)

                if b:
                    pe.wait_ge(s("xT_low"), mb + 1)
                    at_least(pe, s("k_exp"), 4 * mb)
                    for j in range(2):
                        q_feature(j)
                if c:
                    pe.wait_ge(s("m_evac"), 4 * (mc + 1))
                    pe.wait_ge(s("q_exp"), 4 * (mc + 1))
                    at_least(pe, s("attn_added"), mc)
                    for i in range(2):
                        for j in range(4):
                            t = pe.matmul(bank[7][0:HEADS, TOK * i:TOK * i + TOK], mm[:, pc, i, j, D:],
                                          qf[:, pc, j, TOK * i:TOK * i + TOK], start=(j == 0), stop=(j == 3))
                    t.then_inc(s("d8_done"), 1)
                if a:
                    pe.wait_ge(s("front_evac"), NPIECE * (g + 1))
                    at_least(pe, s("m_evac"), 4 * (n - 1))
                    for q in range(5):
                        t = pe.matmul(bank[1][:, 0:PT], wct[:, q],
                                      patches[:, par, q, 2 * k:2 * k + 2].rearrange("p b t -> p (b t)"),
                                      start=(q == 0), stop=(q == 4))
                    t.then_inc(s("conv_done"), 1)
                if b:
                    for j in range(2, 4):
                        pe.wait_ge(s("q_exp"), 4 * mb + j - 1)
                        q_feature(j)
                if d:
                    pe.wait_ge(s("ln2_x"), md + 1)
                    pe.wait_ge(s("xT_low"), pairs(n))
                    transpose_tokens(lambda ch, r: xrow[0:r, pd, 0, ch, 0:D], s("x2t_done"))
                if a:
                    pe.wait_ge(s("h1_ready"), n + 1)
                    at_least(pe, s("h2_copied"), n - 2)
                    for ch in range(4):
                        lo = (ch // 2) * TOK + (ch % 2) * (CH - 1)
                        t = pe.transpose(bank[2][0:CH, D * ch:D * ch + D], h1T[:, k, lo:lo + CH], ident)
                    t.then_inc(s("h1t_done"), 1)
                front(0)
                if d:
                    pe.wait_ge(s("x2T_copied"), md + 1)
                    at_least(pe, s("m_evac"), pairs4(mb))
                    for ch in range(4):
                        lo = (ch // 2) * TOK + (ch % 2) * (CH - 1)
                        t = pe.matmul(logits[0:CH, E * ch:E * ch + E], x2T[:, lo:lo + CH], wg_sb[:], start=True, stop=True)
                    t.then_inc(s("logit_done"), 1)
                if c:
                    pe.wait_ge(s("rden_ready"), mc + 1)
                    broadcast(0)
                    if a:
                        pe.wait_ge(s("h1_ready"), n + 1)
                    broadcast(1)
                if b:
                    for j in range(2):
                        pe.wait_ge(s("q_exp"), 4 * mb + 3 + j)
                        k_tokens(j)
                front(1)
                if b:
                    for j in range(2, 4):
                        pe.wait_ge(s("k_exp"), 4 * mb + j - 1)
                        k_tokens(j)
                if c:
                    for j in range(2, 4):
                        pe.wait_ge(s("qn_done"), 4 * mc + j - 1)
                        broadcast(j)
                if b:
                    pe.wait_ge(s("x_ones"), mb + 1)
                    pe.wait_ge(s("k_exp"), 4 * mb + 2)
                    at_least(pe, s("m_evac"), 4 * mb)
                    if d:
                        pe.wait_ge(s("logit_read"), md + 1)
                    context(pb, 0, bank[6])
                if a:
                    pe.wait_ge(s("ln1_x"), n + 1)
                    at_least(pe, s("x2T_copied"), n - 2)
                    transpose_tokens(lambda ch, r: xtok[0:r, pc, ch], s("xt_done"))
                front(2)
                if d:
                    pe.wait_ge(s("before_step"), 4 * (md + 1))
                    if a:
                        pe.wait_ge(s("ln1_x"), n + 1)
                    else:
                        pe.wait_ge(s("h2_copied"), n - 2)
                    pe.matmul(ranks[:, :], ones[0:CH], before[:].rearrange("p c e -> p (c e)"), start=True, stop=False)
                    pe.matmul(ranks[:, 0:4 * E], tri[0:CH], both[:].rearrange("p c e -> p (c e)"), start=False, stop=True
                              ).then_inc(s("rank_done"), 1)
                if c:
                    pe.wait_ge(s("qn_done"), 4 * mc + 4)
                    for i in range(2):
                        for j in range(4):
                            t = pe.matmul(bank[7][:, TOK * i:TOK * i + TOK], mm[:, pc, i, j, 0:D],
                                          qf[:, pc, j, TOK * i:TOK * i + TOK], start=(j == 0), stop=(j == 3))
                    t.then_inc(s("out_done"), 1)
                if b:
                    if a:
                        pe.wait_ge(s("h1_ready"), n + 1)
                    pe.wait_ge(s("k_exp"), 4 * mb + 4)
                    context(pb, 1, bank[1])
                    pe.wait_ge(s("g_copied"), 2 * mb + 1)
                    context_out(0, 0)
                if c:
                    pe.wait_ge(s("attn_added"), mc + 1)
                    if a:
                        pe.wait_ge(s("ln1_x"), n + 1)
                    if d:
                        pe.wait_ge(s("rank_read"), md + 1)
                    for ch in range(4):
                        lo = (ch // 2) * TOK + (ch % 2) * (CH - 1)
                        t = pe.transpose(bank[2][0:CH, D * ch:D * ch + D], h1T[:, (k + 2) % 4, lo:lo + CH], ident)
                    t.then_inc(s("h2t_done"), 1)
                if b:
                    pe.wait_ge(s("g_copied"), 2 * mb + 2)
                    context_out(0, 1)
                front(3)
                if fr and k == 1:
                    image_stats(g + 1)
                if b:
                    pe.wait_ge(s("m_evac"), 4 * mb + 1)
                    context_out(1, 0)
                    pe.wait_ge(s("m_evac"), 4 * mb + 2)
                    context_out(1, 1)

            def products(o_, left, right):
                pe.matmul(o_, left(0), right(0), start=True, stop=False)
                pe.matmul(o_, left(0), right(1), start=False, stop=False)
                return pe.matmul(o_, left(1), right(0), start=False, stop=True)

            def transpose_tokens(src, done):
                for ch in range(4):
                    r = HALF_ROWS[ch % 2]
                    lo = (ch // 2) * TOK + (ch % 2) * (CH - 1)
                    t = pe.transpose(bank[3][:, lo:lo + r], src(ch, r), ident[0:r, 0:r])
                t.then_inc(done, 1)

            def context(p, i, o_):
                for h in range(2):
                    r = HALF_ROWS[h]
                    t = pe.matmul(o_[:, :], xtok[0:r, p, 2 * i + h], kf[0:r, 2 * i + h], start=(h == 0), stop=(h == 1))
                t.then_inc(s("g_done"), 1)

            def context_out(i, jj):
                o_ = bank[(6, 1)[jj]]
                for h in range(4 * jj, 4 * jj + 4):
                    col = (h // 2 % 2) * (D + HEADS)
                    t = pe.matmul(o_[64 * (h % 2):64 * (h % 2) + 64, col:col + D + HEADS], gT[:, i, NF * h:NF * h + NF],
                                  wvo[:, h], start=True, stop=True)
                t.then_inc(s("m_done"), 1)

            steps(pe, step)

        @block.vector
        def _(ve):
            ve.memset(raw44[:], 0.0).then_inc(s("pads_zero"), 1)
            ve.memset(pjT, 0.0).then_inc(s("setup_zero"), 1)
            ve.memset(woT, 0.0).then_inc(s("setup_zero"), 1)
            ve.memset(before[:], 0.0).then_inc(s("setup_zero"), 1)
            ve.memset(zeros[:], 0.0).then_inc(s("setup_zero"), 1)
            ve.wait_ge(s("small_in"), 16 * NSMALL)
            ve.wait_ge(s("setup_zero"), 4)
            ve.tensor_copy(rparts[:], zeros[0:40, 0:PT])
            for p in range(2):
                for a_ in range(2):
                    t = ve.tensor_copy(xT[:, p, a_], zeros[:])
            t.then_inc(s("parts_zero"), 1)
            ve.wait_ge(s("parts_zero"), 1)
            ve.tensor_copy(pick_head[:], K("selr")[0:40].rearrange("p (j f) -> p j f", j=4))
            for j in range(4):
                t = ve.tensor_scalar(wv_c[:, j], qkv_raw[:, 2, j], qkv_raw[:, 2, j, D - 1:D], None, ALU.subtract)
            t.then_inc(s("wv_centred"), 1)
            ve.tensor_copy(wvo[:, :, D:], K("e127").rearrange("p (h g) -> p h g", h=HEADS)).then_inc(s("wvo_ready"), 1)
            item = [0]

            def begin():
                item[0] += 1
                ve.wait_ge(s("setup_mm"), item[0])
                return bank[(item[0] - 1) % 8]

            def end(t):
                t.then_inc(s("setup_copied"), 1)

            o_ = begin()
            end(ve.tensor_copy(wct[:, 0:4].rearrange("p g k -> p (g k)"), o_[:, :]))
            o_ = begin()
            ve.tensor_copy(wct[:, 4], o_[:, 0:128])
            for h in range(2):
                t = ve.tensor_copy(pjT[64 * h:64 * h + 64, 64 * h:64 * h + 64], o_[64 * h:64 * h + 64, 128:192])
            end(t)
            o_ = begin()
            for h in range(2):
                t = ve.tensor_copy(woT[64 * h:64 * h + 64, :, h], o_[64 * h:64 * h + 64, :].rearrange("p (j n) -> p j n", j=4))
            end(t)
            o_ = begin()
            ve.tensor_scalar(wqp[:, 0], o_[:, :], QS, None, ALU.mult).then_inc(s("high_weights"), 1)
            ve.wait_ge(s("high_weights"), 1)
            end(ve.scalar_tensor_tensor(out=wqp[:, 1], in0=o_[:, :], scalar=QS, in1=wqp[:, 0].bitcast(F32),
                                        op0=ALU.mult, op1=ALU.subtract))
            o_ = begin()
            ve.tensor_copy(wkp[:, 0], o_[:, :]).then_inc(s("high_weights"), 1)
            ve.wait_ge(s("high_weights"), 2)
            end(ve.tensor_tensor(wkp[:, 1], o_[:, :], wkp[:, 0].bitcast(F32), ALU.subtract))
            for jj in range(2):
                o_ = begin()
                end(ve.tensor_copy(wvo[:, 4 * jj:4 * jj + 4, 0:D], o_[:, :].rearrange("p (h n) -> p h n", h=4)))

            def patch_affine(q):
                raw, g = ((graw, q), (braw, q - 5))[q // 5]
                if q % 5 == 0:
                    ve.wait_ge(s(("gamma_in", "beta_in")[q // 5]), 16)
                ve.tensor_copy((nrm0, nrm44)[q % 2][0:NP1, 0:NP1].rearrange("p x (k i) -> p k x i", i=PATCH),
                               raw[:, C * g:C * g + C].rearrange("p c k (x i) -> p (c k) x i", i=PATCH)
                               ).then_inc(s("affine_patched"), 1)

            patch_affine(0)
            patch_affine(1)
            for g in range(5):
                o_ = begin()
                end(ve.tensor_copy(gam[:, g], o_[:, 0:TOK].rearrange("p (x y) -> p x y", x=NP1)))
                patch_affine(g + 2)
            for g in range(5):
                o_ = begin()
                if g < 3:
                    patch_affine(g + 7)
                end(ve.tensor_copy(bT[:, g].rearrange("p y x -> p x y"), o_[:, 0:TOK].rearrange("p (x y) -> p x y", x=NP1)))
            o_ = begin()
            end(ve.tensor_scalar(cbeta[:], o_[:, 0:TOK], convb_sb[:, 0:1], None, ALU.add))
            ve.wait_ge(s("setup_copied"), item[0])

            def image_parts(G):
                ve.wait_ge(s("colsum_ready"), 4 * (G + 1))
                sums = colsum[:].rearrange("p (s e) -> p e s", e=2)
                ve.tensor_scalar(part[:, 2:4], sums[:, 0], K("wab")[0:R1, 0:1], None, ALU.mult).then_inc(s("part_a"), 1)
                ve.wait_ge(s("part_a"), G + 1)
                at_least(ve, s("imgstat_done"), G)
                ve.scalar_tensor_tensor(out=part[:, 0:2], in0=sums[:, 1], scalar=K("wab")[0:R1, 1:2], in1=part[:, 2:4],
                                        op0=ALU.mult, op1=ALU.add).then_inc(s("part_ready"), 1)

            def image_var(G):
                ve.wait_ge(s("imgstat_done"), G + 1)
                ve.tensor_copy(imgstat[:], image_sum[:, :].rearrange("p (l s) -> p l s", l=2)).then_inc(s("imgstat_read"), 1)
                ve.wait_ge(s("imgstat_read"), G + 1)
                ve.tensor_tensor(imgtmp[:], imgstat[:, :, 0], imgstat[:, :, 0], ALU.mult).then_inc(s("mean_squared"), 1)
                ve.wait_ge(s("mean_squared"), G + 1)
                ve.tensor_tensor(imgvar[:], imgstat[:, :, 1], imgtmp[:], ALU.subtract).then_inc(s("imgvar_ready"), 1)

            def image_norm(G):
                ve.wait_ge(s("imgrstd_ready"), G + 1)
                at_least(ve, s("front_t"), NPIECE * G)
                ve.tensor_scalar(nrm44[:].rearrange("p x (k i) -> p k x i", i=PATCH),
                                 raw44[:].rearrange("p c k (x i) -> p (c k) x i", i=PATCH), imgstat[:, 0, 0:1], imgrstd[:, 0:1], ALU.subtract, ALU.mult
                                 ).then_inc(s("norm_done"), 1)
                ve.tensor_scalar(nrm0[:].rearrange("p x (k i) -> p k x i", i=PATCH),
                                 raw0[:].rearrange("p c k (x i) -> p (c k) x i", i=PATCH), imgstat[0:R0, 1, 0:1], imgrstd[0:R0, 1:2], ALU.subtract, ALU.mult
                                 ).then_inc(s("norm_done"), 1)

            def front_piece(G, f, par):
                kind, px0, w = PIECES[f]
                ve.wait_ge(s("front_t"), NPIECE * G + f + 1)
                n_ = NP1 if kind == 0 else NP2
                src = bank[0][:, 0:GI * n_ * w].rearrange("p (x b y) -> p x b y", x=w, b=GI)
                for q, dy, dx in ([(0, 0, 0)] if kind == 0 else [(1, 1, 0), (2, 1, 1), (3, 0, 0), (4, 0, 1)]):
                    lo, hi = max(px0 - dx, 0), min(px0 + w - dx, NP1)
                    if lo >= hi:
                        continue
                    i0 = lo + dx - px0
                    dst = patches[:, par, q].rearrange("p b (y x) -> p x b y", y=NP1)
                    t = ve.tensor_tensor(dst[:, lo:hi], src[:, i0:i0 + hi - lo, :, dy:dy + NP1],
                                         gam[:, q, lo:hi].unsqueeze(2).to_broadcast([128, hi - lo, GI, NP1]), ALU.mult)
                t.then_inc(s("front_evac"), 1)

            def norm_stats(src, which, m, stat, agg):
                for ch in range(4):
                    ve.bn_stats(bns[:, which, ch], src(ch)).then_inc(stat, 1)
                wait_alone(ve, setup_met, (stat, 4 * m + 4))
                for ch in range(4):
                    ve.bn_aggr(mv[:, which, ch], bns[:, which, ch]).then_inc(agg, 1)

            image_parts(0)
            image_var(0)
            image_norm(0)
            for f in range(NPIECE):
                front_piece(0, f, 0)

            def step(n, k, g, par, a, b, c, d, fr):
                mb, mc, md = n - 1, n - 2, n - 3
                pb, pc, pd = (k + 1) % 2, k % 2, (k + 1) % 2
                half = lambda off: 2 * g + (k + off) // 2

                def front(i):
                    if fr and len(TURN[k]) > i:
                        if TURN[k][i] == 0:
                            at_least(ve, s("conv_done"), 4 * g)
                        front_piece(g + 1, TURN[k][i], 1 - par)

                def normalise(j):
                    ve.wait_ge(s("bc_done"), 4 * mc + j + 1)
                    ve.tensor_tensor(qf[:, pc, j], qf[:, pc, j], bank[(7, 1)[j % 2]][:, 0:PT], ALU.mult).then_inc(s("qn_done"), 1)

                if c:
                    ve.wait_ge(s("d8_done"), mc + 1)
                    ve.tensor_scalar(dsum[:], bank[7][0:HEADS, 0:PT], 1e-6, None, ALU.add).then_inc(s("dsum_ready"), 1)
                    ve.wait_ge(s("dsum_ready"), mc + 1)
                    ve.reciprocal(rden[:], dsum[:]).then_inc(s("rden_whole"), 1)
                    ve.wait_ge(s("rden_whole"), mc + 1)
                    ve.tensor_copy(rparts[0:HEADS], rden[:]).then_inc(s("rden_high"), 1)
                    ve.wait_ge(s("rden_high"), mc + 1)
                    ve.tensor_tensor(rparts[32:32 + HEADS], rden[:], rparts[0:HEADS].bitcast(F32), ALU.subtract
                                     ).then_inc(s("rden_ready"), 1)
                if a:
                    ve.wait_ge(s("conv_done"), n + 1)
                    at_least(ve, s("h2t_done"), n - 3)
                    ve.tensor_tensor(h1T[:, k].rearrange("p (b t) -> p b t", b=2),
                                     bank[1][:, 0:PT].rearrange("p (b t) -> p b t", b=2),
                                     cbeta[:].unsqueeze(1).to_broadcast([128, 2, TOK]), ALU.add).then_inc(s("h1_ready"), 1)
                    ve.wait_ge(s("h1t_done"), n + 1)
                    norm_stats(lambda ch: bank[2][0:CH, D * ch:D * ch + D], 0, n, s("ln1_bn"), s("ln1_mv"))
                if d:
                    best(md)
                if c:
                    normalise(0)
                    normalise(1)
                front(0)
                if a:
                    ve.wait_ge(s("ln1_rstd"), n + 1)
                    at_least(ve, s("g_done"), 2 * (n - 1))
                    for ch in range(4):
                        t = ve.tensor_scalar(xtok[:, pc, ch], bank[2][0:CH, D * ch:D * ch + D], mv[:, 0, ch, 0:1],
                                             rstd[:, 0, ch:ch + 1], ALU.subtract, ALU.mult)
                    t.then_inc(s("ln1_x"), 1)
                if d:
                    choose(md)
                if c:
                    normalise(2)
                    normalise(3)
                front(1)
                if fr and k == 1:
                    image_parts(g + 1)
                if d:
                    place(md, pd, 128 * half(-3))
                if a:
                    ve.wait_ge(s("xt_done"), n + 1)
                    ve.memset(xtok[:, pc, :, D - 1:D], 1.0).then_inc(s("x_ones"), 1)
                    ve.wait_ge(s("xT_high"), n + 1)
                    ve.tensor_tensor(xT[:, pc, 1, 0:PT], bank[3][:, 0:PT], xT[:, pc, 0, 0:PT].bitcast(F32), ALU.subtract
                                     ).then_inc(s("xT_low"), 1)
                front(2)
                if c:
                    ve.wait_ge(s("out_done"), mc + 1)
                    ve.scalar_tensor_tensor(out=h1T[:, (k + 2) % 4], in0=bank[7][:, 0:PT], scalar=bout_sb[:, 0:1],
                                            in1=h1T[:, (k + 2) % 4], op0=ALU.add, op1=ALU.add).then_inc(s("attn_added"), 1)
                    ve.wait_ge(s("h2_copied"), mc + 1)
                    norm_stats(lambda ch: h2[:, pc, ch], 1, mc, s("ln2_bn"), s("ln2_mv"))
                front(3)
                if fr and k == 1:
                    image_var(g + 1)
                if c:
                    ve.wait_ge(s("ln2_rstd"), mc + 1)
                    at_least(ve, s(f"scattered{pc}"), 128 * half(-2))
                    at_least(ve, s("x2t_done"), mc - 1)
                    for ch in range(4):
                        t = ve.tensor_scalar(xrow[:, pc, 0, ch, 0:D], h2[:, pc, ch], mv[:, 1, ch, 0:1],
                                             rstd[:, 1, ch:ch + 1], ALU.subtract, ALU.mult)
                    t.then_inc(s("ln2_x"), 1)
                if fr and k == 1:
                    image_norm(g + 1)

            def best(m):
                ve.wait_ge(s("logit_done"), m + 1)
                ve.tensor_copy(logit[:], logits[0:CH, :].rearrange("p (c e) -> p c e", c=4)).then_inc(s("logit_read"), 1)
                wait_alone(ve, setup_met, (s("logit_read"), m + 1))
                for ch in range(4):
                    ve.max(top[:, ch], logit[:, ch]).then_inc(s("top_ready"), 1)
                ve.wait_ge(s("top_ready"), 4 * m + 4)
                ve.tensor_tensor(gap[:], top[:, :, 1], top[:, :, 0], ALU.subtract).then_inc(s("gap_ready"), 1)

            def choose(m):
                for ch in range(4):
                    t = ve.max_index(topi[:, ch], top[:, ch], logit[:, ch])
                t.then_inc(s("topi_ready"), 1)
                ve.wait_ge(s("topi_ready"), m + 1)
                ve.tensor_tensor(topf[:], topi[:, :, 0:2], K("dup")[0:CH].rearrange("p (c j) -> p c j", c=4), ALU.add
                                 ).then_inc(s("topf_ready"), 1)
                ve.wait_ge(s("topf_ready"), m + 1)
                for j in range(2):
                    t = ve.tensor_tensor(pick[:, j], K("iota8")[0:CH].unsqueeze(1).to_broadcast([CH, 4, E]),
                                         topf[:, :, j:j + 1].to_broadcast([CH, 4, E]), ALU.is_equal)
                t.then_inc(s("pick_ready"), 1)
                ve.wait_ge(s("pick_ready"), m + 1)
                ve.tensor_tensor(both[:], pick[:, 0], pick[:, 1], ALU.add).then_inc(s("both_ready"), 1)
                ve.wait_ge(s("both_ready"), m + 1)
                for ch in range(4):
                    ve.tensor_tensor(before[:, ch + 1], before[:, ch], both[:, ch], ALU.add).then_inc(s("before_step"), 1)
                    if ch < 3:
                        ve.wait_ge(s("before_step"), 4 * m + ch + 1)
                ve.wait_ge(s("before_step"), 4 * m + 4)

            def place(m, p, scattered):
                ve.wait_ge(s("egap_ready"), m + 1)
                ve.tensor_scalar(esum[:], egap[:], 1.0, None, ALU.add).then_inc(s("esum_ready"), 1)
                ve.wait_ge(s("esum_ready"), m + 1)
                ve.reciprocal(xrow[:, p, 0, :, D], esum[:]).then_inc(s("w0_ready"), 1)
                ve.wait_ge(s("w0_ready"), m + 1)
                ve.tensor_tensor(xrow[:, p, 1, :, D], egap[:], xrow[:, p, 0, :, D], ALU.mult).then_inc(s("w1_ready"), 1)
                ve.wait_ge(s("rank_done"), m + 1)
                rank = ranks[:, :].rearrange("p (c e) -> p c e", c=5)
                ve.tensor_tensor(slots[:], rank[0:CH, 0:4], K("iotacap")[0:CH].unsqueeze(1).to_broadcast([CH, 4, E]), ALU.add
                                 ).then_inc(s("slots_ready"), 1)
                ve.tensor_copy(counts[:], rank[:, 4]).then_inc(s("counts_ready"), 1)
                ve.tensor_copy(before[0:1, 0], rank[0:1, 4]).then_inc(s("rank_read"), 1)
                ve.wait_ge(s("slots_ready"), m + 1)
                ve.tensor_tensor(pslot[:], slots[:].unsqueeze(1).to_broadcast([CH, 2, 4, E]), pick[:], ALU.mult).then_inc(s("pslot_ready"), 1)
                ve.wait_ge(s("pslot_ready"), m + 1)
                ve.tensor_reduce(slotf[:], pslot[:], AX_X, ALU.add).then_inc(s("slotf_ready"), 1)
                ve.wait_ge(s("slotf_ready"), m + 1)
                at_least(ve, s(f"scattered{p}"), scattered)
                ve.tensor_copy(sloti[:, p], slotf[:]).then_inc(s("sloti_ready"), 1)

            steps(ve, step)

            link = [0]

            def chain(q):
                link[0] += 1
                q.then_inc(s("table_step"), 1)
                ve.wait_ge(s("table_step"), link[0])

            ve.wait_ge(s("counts_ready"), NPAIR)
            chain(ve.tensor_tensor(endf[:], counts[0:1], K("iotacap")[0:1], ALU.add))
            ve.tensor_copy(ends[:], endf[:]).then_inc(s("ends_ready"), 1)
            chain(ve.tensor_tensor(has[:], counts[0:1].unsqueeze(2).to_broadcast([1, E, 43]),
                                   K("steps")[0:1].unsqueeze(1).to_broadcast([1, E, 43]), ALU.is_gt))
            chain(ve.tensor_reduce(tiles[:], has[:], AX_X, ALU.add))
            chain(ve.tensor_tensor(upto[:], tiles[:].unsqueeze(1).to_broadcast([1, E, E]),
                                   K("incl")[0:1].rearrange("p (a b) -> p a b", a=E), ALU.mult))
            chain(ve.tensor_reduce(cum[:], upto[:], AX_X, ALU.add))
            chain(ve.tensor_tensor(past[:], K("tile")[0:1].unsqueeze(2).to_broadcast([1, NT, E]),
                                   cum[:].unsqueeze(1).to_broadcast([1, NT, E]), ALU.is_ge))
            chain(ve.tensor_tensor(pastn[:], past[:], tiles[:].unsqueeze(1).to_broadcast([1, NT, E]), ALU.mult))
            chain(ve.tensor_reduce(owner[:], past[:], AX_X, ALU.add))
            chain(ve.tensor_reduce(first_tile[:], pastn[:], AX_X, ALU.add))
            chain(ve.tensor_tensor(inner[:], K("tile")[0:1], first_tile[:], ALU.subtract))
            chain(ve.tensor_scalar(base[:], owner[:], float(CAP), None, ALU.mult))
            chain(ve.scalar_tensor_tensor(out=row[:], in0=inner[:], scalar=float(TT), in1=base[:], op0=ALU.mult, op1=ALU.add))
            ve.tensor_scalar(table[:, :, 0], row[:], float(E * CAP), None, ALU.min).then_inc(s("table_ready"), 1)
            ve.tensor_scalar(table[:, :, 1], owner[:], float(E - 1), None, ALU.min).then_inc(s("table_ready"), 1)

        @block.scalar
        def _(ac):
            edges = sb("edges", [R1, C * PATCH, 2, HALF])
            edge_out = sb("edge_out", [R1, C * PATCH, 2, HALF])

            def image_sums(G):
                at_least(ac, s("front_t"), NPIECE * G)
                at_least(ac, s("norm_done"), 2 * G)
                at_least(ac, s("part_ready"), G)
                ac.wait_ge(s("raw_in"), 16 * NRAW * (G + 1))
                rows = raw44[:].rearrange("p c k x -> p (c k) x")
                for e_, lo in ((0, HALF), (1, S)):
                    ac.activation(edges[:, :, e_], rows[:, :, lo:lo + HALF], ACT.Copy).then_inc(s("edges_ready"), 1)
                ac.activation(nrm44[:].rearrange("p x n -> p (x n)"), raw44[:].rearrange("p c k x -> p (c k x)"), ACT.Copy,
                              accum_out=colsum[:, 0:1]).then_inc(s("colsum_ready"), 1)
                ac.wait_ge(s("edges_ready"), 2 * (G + 1))
                ac.activation(edge_out[:], edges[:], ACT.Copy, accum_out=colsum[:, 1:2]).then_inc(s("colsum_ready"), 1)

            def image_squares(G):
                ac.wait_ge(s("colsum_ready"), 4 * G + 2)
                ac.activation(nrm44[:].rearrange("p x n -> p (x n)"), raw44[:].rearrange("p c k x -> p (c k x)"), ACT.Square,
                              accum_out=colsum[:, 2:3]).then_inc(s("colsum_ready"), 1)
                ac.activation(edge_out[:], edges[:], ACT.Square, accum_out=colsum[:, 3:4]).then_inc(s("colsum_ready"), 1)

            ac.wait_ge(s("setup_mm"), 17)
            image_sums(0)
            image_squares(0)

            def step(n, k, g, par, a, b, c, d, fr):
                mb, mc, md = n - 1, n - 2, n - 3
                pb, pc, pd = (k + 1) % 2, k % 2, (k + 1) % 2

                def m_copy(f):
                    i, jj = f // 2, f % 2
                    ac.wait_ge(s("m_done"), 4 * mb + f + 1)
                    ac.copy(mm[:, pb, i, 2 * jj:2 * jj + 2],
                            bank[(6, 1)[jj]][:, 0:2 * (D + HEADS)].rearrange("p (j n) -> p j n", j=2)).then_inc(s("m_evac"), 1)

                if b:
                    at_least(ac, s("out_done"), mb - 1)
                    for j in range(4):
                        ac.wait_ge(s("q_mm"), 4 * mb + j + 1)
                        ac.activation(qf[:, pb, j], bank[4 + j % 2][:, 0:PT], ACT.Exp).then_inc(s("q_exp"), 1)
                if d:
                    ac.wait_ge(s("x2t_done"), md + 1)
                    at_least(ac, s("logit_done"), md)
                    ac.copy(x2T[:], bank[3][:, 0:PT]).then_inc(s("x2T_copied"), 1)
                if fr and k == 1:
                    image_sums(g + 1)
                if b:
                    at_least(ac, s("g_done"), 2 * mb)
                    for ch in range(4):
                        ac.wait_ge(s("k_mm"), 4 * mb + ch + 1)
                        ac.activation(kf[:, ch], bank[4 + ch % 2][0:CH, :], ACT.Exp).then_inc(s("k_exp"), 1)
                if d:
                    ac.wait_ge(s("gap_ready"), md + 1)
                    at_least(ac, s("w1_ready"), md)
                    ac.activation(egap[:], gap[:], ACT.Exp).then_inc(s("egap_ready"), 1)
                if fr and k == 1:
                    image_squares(g + 1)
                if b:
                    at_least(ac, s("m_done"), 4 * mb)
                    ac.wait_ge(s("g_done"), 2 * mb + 1)
                    ac.copy(gT[:, 0], bank[6][:, :]).then_inc(s("g_copied"), 1)
                if a:
                    ac.wait_ge(s("xt_done"), n + 1)
                    at_least(ac, s("k_mm"), 4 * (n - 1))
                    ac.copy(xT[:, pc, 0, 0:PT], bank[3][:, 0:PT]).then_inc(s("xT_high"), 1)
                if b:
                    ac.wait_ge(s("g_done"), 2 * mb + 2)
                    ac.copy(gT[:, 1], bank[1][:, :]).then_inc(s("g_copied"), 1)
                    at_least(ac, s("out_done"), mb - 1)
                    m_copy(0)
                if c:
                    ac.wait_ge(s("h2t_done"), mc + 1)
                    at_least(ac, s(f"h2_out{pc}"), 64 * (2 * g + (k - 2) // 2))
                    at_least(ac, s("ln2_x"), mc - 1)
                    ac.copy(h2[:, pc].rearrange("p c n -> p (c n)"), bank[2][0:CH, :]).then_inc(s("h2_copied"), 1)
                if b:
                    for f in range(1, 4):
                        m_copy(f)
            steps(ac, step)

        @block.gpsimd
        def _(po):
            def root(dst, src, tmp, eps, half, start, v_done, r_done, turn):
                po.tensor_scalar(tmp, src, eps, 1.0, ALU.add, ALU.mult).then_inc(v_done, 1)
                po.wait_ge(v_done, turn + 1)
                po.tensor_tensor(dst, tmp, half, ALU.pow).then_inc(r_done, 1)

            def image_root(G):
                wait_alone(po, setup_met, (s("imgvar_ready"), G + 1), (s("norm_done"), 2 * G))
                root(imgrstd[:], imgvar[:], imgeps[:], 1e-7, K("mhalf")[0:R1, 0:2], 0, s("imgeps_ready"), s("imgrstd_ready"), G)

            imgeps = sb("imgeps", [R1, 2])
            po.wait_ge(s("small_in"), 16 * NSMALL)
            image_root(0)

            def step(n, k, g, par, a, b, c, d, fr):
                mb, mc, md = n - 1, n - 2, n - 3
                pb, pc, pd = (k + 1) % 2, k % 2, (k + 1) % 2
                if a:
                    wait_alone(po, setup_met, (s("ln1_mv"), 4 * (n + 1)), (s("ln1_x"), n))
                    root(rstd[:, 0], mv[:, 0, :, 1], vare[:, 0], 1e-5, K("mhalf")[0:CH], 0, s("ln1_vare"), s("ln1_rstd"), n)
                if d:
                    wait_alone(po, setup_met, (s("sloti_ready"), md + 1), (s("w1_ready"), md + 1),
                               (s("row_ready"), 3 * (md + 1)))
                    for ch in range(4):
                        r = HALF_ROWS[ch % 2]
                        for j in range(2):
                            po.indirect_dma_start(sorted_rows, bass.IndirectOffsetOnAxis(sloti[0:r, pd, j, ch:ch + 1], 0),
                                                  xrow[0:r, pd, j, ch], None).then_inc(s(f"scattered{pd}"), 16)
                if c:
                    wait_alone(po, setup_met, (s("ln2_mv"), 4 * (mc + 1)), (s("ln2_x"), mc))
                    root(rstd[:, 1], mv[:, 1, :, 1], vare[:, 1], 1e-5, K("mhalf")[0:CH], 0, s("ln2_vare"), s("ln2_rstd"), mc)
                    wait_alone(po, setup_met, (s("ln2_x"), mc + 1), (s("tok_next"), mc))
                    po.tensor_copy(xrow[:, pc, 1, :, 0:D], xrow[:, pc, 0, :, 0:D]).then_inc(s("row_ready"), 1)
                    for j in range(2):
                        po.tensor_copy(xrow[:, pc, j, :, D + 1], tokid[:]).then_inc(s("row_ready"), 1)
                    wait_alone(po, setup_met, (s("row_ready"), 3 * (mc + 1)))
                    po.tensor_scalar(tokid[:], tokid[:], float(PT), 1.0, ALU.add, ALU.mult).then_inc(s("tok_next"), 1)
                if fr and k == 1:
                    image_root(g + 1)
            steps(po, step)
            for q in range(2):
                po.wait_ge(s(f"scattered{q}"), NPAIR // 2 * 128)



def experts(nc, ffw, ffv, ffw2, out, cst, table, sorted_rows, bank):
    with ExitStack() as ctx:
        def sb(name, shape, dt=F32):
            return ctx.enter_context(nc.sbuf_tensor(name, shape, dt))

        def K(k):
            return cst[:, SEG[k][0]:SEG[k][1]]

        ident = K("ident")
        xr = sb("xr", [128, 2, 2, RW])
        meta_ = sb("meta_", [128, 2, 2, 2])
        dest = sb("dest", [128, 2, 2], U32)
        xT = sb("xT_e", [128, 2, 2, TT], F32R)
        wv_all = sb("wv_all", [128, E, 2, F])
        wv = sb("wv", [128, 2, 2, 2, F], F32R)
        w2 = sb("w2", [128, E, 4, D])
        sil = sb("sil", [128, 2, TT])
        hid = sb("hid", [128, 2, 4, TT])
        yo = sb("yo", [128, 2, 2, D])
        S_ = {}

        def s(name):
            if name not in S_:
                S_[name] = ctx.enter_context(nc.semaphore(name))
            return S_[name]

        def steps(step):
            def run(eng):
                step(0, 0, 0, True, False)
                step(1, 0, 1, True, True)
                with eng.Fori(0, (NT - 4) // 2) as i:
                    step(2 * i + 2, i + 1, 0, True, True)
                    step(2 * i + 3, i + 1, 1, True, True)
                step(NT - 2, NT // 2 - 1, 0, True, True)
                step(NT - 1, NT // 2 - 1, 1, False, True)
            return run

        block = ctx.enter_context(nc.Block())

        @block.sync
        def _(sp):
            def rows(t, h, p):
                r = sp.value_load(table[0:1, bass.ds(t, 1), 0], min_val=0, max_val=E * CAP)
                at_least(sp, s("tok_t"), t - 1)
                at_least(sp, s("meta_done"), t - 1)
                sp.dma_start(xr[:, p], sorted_rows[bass.ds(r, TT)].rearrange("(p a) n -> p a n", a=2)
                             ).then_inc(s(f"rows_in{p}"), 16)

            for e in range(E):
                sp.dma_start(wv_all[:, e, 0], ffw[e]).then_inc(s("wv_in"), 16)
                if e == 0:
                    rows(0, 0, 0)
                    rows(1, 0, 1)
            with sp.Fori(0, (NT - 2) // 2) as i:
                rows(2 * i + 2, i + 1, 0)
                rows(2 * i + 3, i + 1, 1)

        @block.tensor
        def _(pe):
            def turn(t, h, p):
                pe.wait_ge(s(f"rows_in{p}"), 16 * (h + 1))
                at_least(pe, s("xT_low_e"), t - 1)
                for a in range(2):
                    q = pe.transpose(bank[6 + p][:, 128 * a:128 * a + 128], xr[:, p, a, 0:D], ident)
                q.then_inc(s("tok_t"), 1)

            def hidden(t, p, fc):
                if fc == 0:
                    pe.wait_ge(s("xT_low_e"), t + 1)
                    pe.wait_ge(s("w_low"), 2 * t + 2)
                at_least(pe, s("h_done"), 4 * (t - 1) + fc + 1)
                cols = slice(128 * fc, 128 * fc + 128)
                for m in range(2):
                    for w_, x_ in ((0, 0), (0, 1), (1, 0)):
                        q = pe.matmul(bank[fc][:, TT * m:TT * m + TT],
                                      wv[:, p, w_, m, cols], xT[:, p, x_],
                                      start=(w_ + x_ == 0), stop=(w_ == 1))
                q.then_inc(s("hv_done"), 1)

            def down(t, p, e):
                pe.wait_ge(s("h_done"), 4 * t + 4)
                at_least(pe, s("y_scaled"), t - 1)
                for a in range(2):
                    for fc in range(4):
                        q = pe.matmul(bank[4 + p][:, D * a:D * a + D], hid[:, p, fc, 128 * a:128 * a + 128],
                                      w2[:, bass.ds(e, 1), fc].rearrange("p e n -> p (e n)"), start=(fc == 0), stop=(fc == 3))
                q.then_inc(s("y_done"), 1)

            def expert(t):
                return pe.value_load(table[0:1, bass.ds(t, 1), 1], min_val=0, max_val=E - 1)

            def step(t, h, p, more, prev):
                hidden(t, p, 0)
                hidden(t, p, 1)
                if more:
                    turn(t + 1, h + p, 1 - p)
                if prev:
                    down(t - 1, 1 - p, expert(t - 1))
                hidden(t, p, 2)
                hidden(t, p, 3)

            turn(0, 0, 0)
            pe.wait_ge(s("w2_in"), 16)
            steps(step)(pe)
            down(NT - 1, 1, expert(NT - 1))

        @block.scalar
        def _(ac):
            def high_w(t, p, ms=(0, 1)):
                e = ac.value_load(table[0:1, bass.ds(t, 1), 1], min_val=0, max_val=E - 1)
                at_least(ac, s("hv_done"), 4 * (t - 1))
                for m in ms:
                    ac.copy(wv[:, p, 0, m], wv_all[:, bass.ds(e, 1), m].rearrange("p e n -> p (e n)")).then_inc(s("w_high"), 1)

            def copy_x(t, h, p):
                ac.wait_ge(s("tok_t"), t + 1)
                at_least(ac, s("hv_done"), 4 * (t - 1))
                ac.copy(xT[:, p, 0], bank[6 + p][:, 0:TT]).then_inc(s("xT_high_e"), 1)

            def step(t, h, p, more, prev):
                for fc in range(4):
                    if more and fc == 2:
                        copy_x(t + 1, h + p, 1 - p)
                        high_w(t + 1, 1 - p)
                    ac.wait_ge(s("hv_done"), 4 * t + fc + 1)
                    at_least(ac, s("h_done"), 4 * t + fc - 1)
                    ac.activation(sil[:, fc % 2], bank[fc][:, 0:TT], ACT.Silu).then_inc(s("silu_done"), 1)

            for e in range(E):
                ac.dma_start(wv_all[:, e, 1], ffv[e]).then_inc(s("wv_in"), 16)
            ac.dma_start(w2[:], ffw2.rearrange("e (c f) d -> f e c d", c=4)).then_inc(s("w2_in"), 16)
            ac.wait_ge(s("wv_in"), 16 * 2 * E)
            high_w(0, 0)
            copy_x(0, 0, 0)
            steps(step)(ac)

        @block.vector
        def _(ve):
            def low_w(t, p, ms=(0, 1)):
                e = ve.value_load(table[0:1, bass.ds(t, 1), 1], min_val=0, max_val=E - 1)
                for m in ms:
                    ve.wait_ge(s("w_high"), 2 * t + m + 1)
                    ve.tensor_tensor(wv[:, p, 1, m], wv_all[:, bass.ds(e, 1), m].rearrange("p e n -> p (e n)"),
                                     wv[:, p, 0, m].bitcast(F32), ALU.subtract).then_inc(s("w_low"), 1)

            def meta(t, h, p):
                ve.wait_ge(s(f"rows_in{p}"), 16 * (h + 1))
                at_least(ve, s("y_scaled"), t - 1)
                ve.tensor_copy(meta_[:, p], xr[:, p, :, D:]).then_inc(s("meta_done"), 1)

            def low_x(t, p):
                ve.wait_ge(s("xT_high_e"), t + 1)
                ve.tensor_tensor(xT[:, p, 1], bank[6 + p][:, 0:TT], xT[:, p, 0].bitcast(F32), ALU.subtract
                                 ).then_inc(s("xT_low_e"), 1)

            def product(t, p, fc):
                ve.wait_ge(s("silu_done"), 4 * t + fc + 1)
                if fc == 0:
                    at_least(ve, s("y_done"), t - 1)
                ve.tensor_tensor(hid[:, p, fc], sil[:, fc % 2], bank[fc][:, TT:2 * TT], ALU.mult).then_inc(s("h_done"), 1)

            def scale(t, p):
                ve.wait_ge(s("y_done"), t + 1)
                ve.wait_ge(s("meta_done"), t + 1)
                at_least(ve, s("added"), 32 * (t - 1))
                ve.tensor_copy(dest[:, p], meta_[:, p, :, 1])
                for a in range(2):
                    q = ve.tensor_scalar(yo[:, p, a], bank[4 + p][:, D * a:D * a + D], meta_[:, p, a, 0:1], None, ALU.mult)
                q.then_inc(s("y_scaled"), 1)

            def step(t, h, p, more, prev):
                product(t, p, 0)
                product(t, p, 1)
                if more:
                    low_x(t + 1, 1 - p)
                    low_w(t + 1, 1 - p)
                if prev:
                    scale(t - 1, 1 - p)
                if more:
                    meta(t + 1, h + p, 1 - p)
                product(t, p, 2)
                product(t, p, 3)

            meta(0, 0, 0)
            low_w(0, 0)
            low_x(0, 0)
            steps(step)(ve)
            scale(NT - 1, 1)

        @block.gpsimd
        def _(po):
            def add(t, p):
                wait_alone(po, (s("w2_in"), 16), (s("y_scaled"), t + 1), (s("added"), 32 * t))
                for a in range(2):
                    po.indirect_dma_start(out, bass.IndirectOffsetOnAxis(dest[:, p, a:a + 1], 0), yo[:, p, a], None,
                                          compute_op=ALU.add).then_inc(s("added"), 16)

            add(0, 0)
            add(1, 1)
            with po.Fori(1, NT // 2) as i:
                add(2 * i, 0)
                add(2 * i + 1, 1)
            po.wait_ge(s("added"), 32 * NT)


_INS = ["x", "L0_tok_gamma", "L0_tok_beta", "L0_tok_W", "L0_tok_b", "L0_attn_Wqkv", "L0_attn_Wout", "L0_attn_bout",
        "L0_attn_proj", "L0_ffn_Wg", "L0_ffn_W", "L0_ffn_V", "L0_ffn_W2"]


def kernel(**inputs):
    import numpy as _np
    import concourse.bacc as _bacc
    from concourse import mybir as _mybir
    from concourse.bass_utils import run_bass_kernel_spmd as _run

    nc = _bacc.Bacc("TRN2", target_bir_lowering=False, num_devices=1)
    arrays, args = {}, []
    for name in _INS:
        a = _np.ascontiguousarray(inputs[name])
        arrays[f"in_{name}"] = a
        args.append(nc.dram_tensor(f"in_{name}", a.shape, _mybir.dt.from_np(a.dtype), kind="ExternalInput").ap())
    c = constants()
    arrays["in_const"] = c
    args.append(nc.dram_tensor("in_const", c.shape, F32, kind="ExternalInput").ap())
    args.append(nc.dram_tensor("out_rows", (NTOK + TT, D), F32, kind="ExternalOutput").ap())
    build(nc, *args)
    r = _run(nc, [arrays], core_ids=[0])
    return r.results[0]["out_rows"][:NTOK].reshape(B, TOK, D)
```

```python
from contextlib import ExitStack

import numpy as np

import concourse.bass as bass
from concourse import mybir

F32 = mybir.dt.float32
F32R = mybir.dt.float32r
U32 = mybir.dt.uint32
I32 = mybir.dt.int32
ALU = mybir.AluOpType
ACT = mybir.ActivationFunctionType
AX_X = mybir.AxisListType.X

B, C, S = 64, 2, 104
PATCH, HALF = 8, 4
NP1 = S // PATCH
NP2 = NP1 + 1
TOK = NP1 * NP1
D = 128
HEADS, DH, NF = 8, 64, 64
F, E = 512, 8
NTOK = B * TOK
GI = 8
NG = B // GI
R0, R1 = GI * NP1, GI * NP2
PW = S + 2 * HALF
NPAIR = B // 2
PT = 2 * TOK
NCH, HEAD = 3, 128
TAIL = TOK - HEAD
PLACES = [(0, 0, 0, HEAD), (1, 0, TOK, HEAD), (2, 0, HEAD, TAIL), (2, 64, TOK + HEAD, TAIL)]
PTW = TOK + HEAD + 64
NSTAT = 5 * C * S * S
TT = 256
CAP = NTOK + TT
TILES_E = -(-NTOK // TT)
NT = (2 * NTOK) // TT + E
RW = D + 2
QS = DH ** -0.5

_SEGS = dict(ident=128, sel44=R1, sel0=R1, wab=2, e127=HEADS * HEADS, iota8=8, iotacap=8,
             dup=2 * NCH, tri=128, ones=128, tok=NCH, mhalf=4, padrow=2 * RW, tile=NT, steps=TILES_E, incl=E * E,
             selr=2 * (HEADS // 2) * 128)
SEG, _o = {}, 0
for _k, _n in _SEGS.items():
    SEG[_k] = (_o, _o + _n)
    _o += _n
NCONST = _o
NKEPT = SEG["selr"][0]


def constants():
    c = np.zeros((128, NCONST), np.float32)

    def seg(k):
        return c[:, SEG[k][0]:SEG[k][1]]

    p = np.arange(128)
    seg("ident")[:] = np.eye(128)
    same = (p[:R1, None] // NP2 == np.arange(R1)[None] // NP2) / NSTAT
    seg("sel44")[:R1] = same
    seg("sel0")[:R1, :R0] = (p[:R1, None] // NP2 == np.arange(R0)[None] // NP1) / NSTAT
    edge = ((p % NP2 == 0) | (p % NP2 == NP2 - 1)).astype(np.float32)
    seg("wab")[:, 0] = 5 - 2 * edge
    seg("wab")[:, 1] = edge - 2
    for h in range(HEADS):
        for i in range(2):
            for r in (0, 64):
                seg("selr")[r + 32 * i + h, (i * HEADS + h) * NF:(i * HEADS + h + 1) * NF] = 1
        seg("e127")[D - 1, h * HEADS + h] = 1
    seg("iota8")[:] = np.arange(8)
    seg("iotacap")[:] = np.arange(8) * CAP
    seg("dup")[:, 4:6] = np.where(p % 64 >= TAIL, 100, 0)[:, None]
    seg("tri")[:] = p[:, None] < p[None]
    seg("ones")[:] = 1
    seg("tok")[:] = np.stack([p, TOK + p, HEAD + p // 64 * TOK + p % 64], 1)
    seg("mhalf")[:] = -0.5
    for a in range(2):
        seg("padrow")[:, a * RW + RW - 1] = NTOK + a * 128 + p
    seg("tile")[:] = np.arange(NT)
    seg("steps")[:] = np.arange(TILES_E) * TT
    seg("incl")[:] = np.tril(np.ones((E, E))).reshape(-1)
    return c


def at_least(eng, sem, value):
    if not (isinstance(value, int) and value <= 0):
        eng.wait_ge(sem, value)


def wait_alone(eng, met, *waits):
    waits = [(q, v if isinstance(v, int) else eng.to_reg(v)) for q, v in waits]
    eng.wait_ge(*met)
    for q, v in waits:
        at_least(eng, q, v)


def build(nc, x, gamma, beta, convw, convb, wqkv, wout, bout, proj, wg, ffw, ffv, ffw2, const, out):
    with ExitStack() as ctx:
        cst = ctx.enter_context(nc.sbuf_tensor("cst", [128, NKEPT], F32))
        counts = ctx.enter_context(nc.sbuf_tensor("counts", [128, E], F32))
        table = ctx.enter_context(nc.sbuf_tensor("table", [1, NT, 2], I32))
        wv_all = ctx.enter_context(nc.sbuf_tensor("wv_all", [128, E, 2, F], F32))
        sorted_rows = nc.dram_tensor("sorted_rows", [E * CAP + TT, RW], F32, kind="Internal").ap()
        bank = [ctx.enter_context(nc.psum_tensor(f"bank{i}", [128, 512], F32)) for i in range(8)]
        tokens(nc, x, gamma, beta, convw, convb, wqkv, wout, bout, proj, wg, ffw, ffv, const, out, cst, counts, table,
               wv_all, sorted_rows, bank)
        experts(nc, ffw2, out, cst, table, wv_all, sorted_rows, bank)


def tokens(nc, x, gamma, beta, convw, convb, wqkv, wout, bout, proj, wg, ffw, ffv, const, out, cst, counts, table,
               wv_all, sorted_rows, bank):
    with ExitStack() as ctx:
        def sb(name, shape, dt=F32):
            return ctx.enter_context(nc.sbuf_tensor(name, shape, dt))

        def sem(name):
            return ctx.enter_context(nc.semaphore(name))

        def K(k):
            return cst[:, SEG[k][0]:SEG[k][1]]

        ident, ones, tri = K("ident"), K("ones"), K("tri")
        patches = sb("patches", [128, 2, 5, GI, TOK])
        raw0 = sb("raw0", [R0, C, PATCH, S])
        raw44 = sb("raw44", [R1, C, PATCH, PW])
        nrm0 = sb("nrm0", [R0, NP1, D])
        nrm44 = sb("nrm44", [R1, NP2, D])
        colsum = sb("colsum", [R1, 4])
        part = sb("part", [R1, 4])
        imgstat = sb("imgstat", [R1, 2, 2])
        imgtmp = sb("imgtmp", [R1, 2])
        imgvar = sb("imgvar", [R1, 2])
        imgrstd = sb("imgrstd", [R1, 2])
        gam = sb("gam", [128, 5, NP1, NP1])
        cbeta = sb("cbeta", [128, TOK])
        wct = sb("wct", [128, 5, D])
        wqp = sb("wqp", [128, 2, HEADS * NF], F32R)
        wkp = sb("wkp", [128, 2, HEADS * NF], F32R)
        pick_head = sb("pick_head", [104, 2, 4, 128], F32R)
        wvo = sb("wvo", [128, HEADS, D + HEADS])
        wg_sb = sb("wg_sb", [128, E])
        bout_sb = sb("bout_sb", [128, 1])
        convb_sb = sb("convb_sb", [128, 1])
        h1T = sb("h1T", [128, 4, PTW])
        xtok = sb("xtok", [128, 2, NCH, D])
        xT = sb("xT", [128, 2, 2, NCH * 128], F32R)
        attn = sb("attn", [128, 8 * PT + 6 * HEADS * NF + 16 * (D + HEADS) + 8 * D])
        taken = [0]

        def piece(width, rows=128):
            taken[0] += width
            return attn[0:rows, taken[0] - width:taken[0]]

        qf = piece(8 * PT).rearrange("p (s j t) -> p s j t", s=2, j=4)
        kf = piece(NCH * HEADS * NF).rearrange("p (c n) -> p c n", c=NCH)
        gT = piece(2 * HEADS * NF).rearrange("p (i n) -> p i n", i=2)
        mm = piece(16 * (D + HEADS)).rearrange("p (s i j n) -> p s i j n", s=2, i=2, j=4)
        h2 = piece(2 * NCH * D).rearrange("p (s c n) -> p s c n", s=2, c=NCH)
        braw = attn[0:NP1, 0:5 * C * PATCH * S].rearrange("p (c k x) -> p c k x", c=5 * C, k=PATCH)
        dsum = sb("dsum", [40, TOK])
        rden = sb("rden", [40, TOK])
        rparts = sb("rparts", [104, TOK + 1], F32R)
        xrow_all = sb("xrow_all", [128, 16 * RW])
        xrow = xrow_all[:, 0:4 * NCH * RW].rearrange("p (s j c n) -> p s j c n", s=2, j=2, c=NCH)
        x2T = sb("x2T", [128, NCH * 128])
        bns = sb("bns", [128, 2, NCH, 6])
        mv = sb("mv", [128, 2, NCH, 2])
        rstd = sb("rstd", [128, 2, NCH])
        vare = sb("vare", [128, 2, NCH])
        logit = sb("logit", [128, NCH, E])
        top = sb("top", [128, NCH, 8])
        topi = sb("topi", [128, NCH, 8], U32)
        topf = sb("topf", [128, NCH, 2])
        gap = sb("gap", [128, NCH])
        egap = sb("egap", [128, NCH])
        esum = sb("esum", [128, NCH])
        pick = sb("pick", [128, 2, NCH, E])
        both = sb("both", [128, NCH, E])
        before = sb("before", [128, NCH + 1, E])
        slots = sb("slots", [128, NCH, E])
        pslot = sb("pslot", [128, 2, NCH, E])
        slotf = sb("slotf", [128, 2, NCH])
        sloti = sb("sloti", [128, 2, 2, len(PLACES)], U32)
        tokid = sb("tokid", [128, NCH])
        endf = sb("endf", [1, E])
        ends = sb("ends", [1, E], I32)
        taken[0] = 0
        has = piece(E * TILES_E, 1).rearrange("p (e n) -> p e n", e=E)
        tiles = piece(E, 1)
        upto = piece(E * E, 1).rearrange("p (e n) -> p e n", e=E)
        cum = piece(E, 1)
        past = piece(NT * E, 1).rearrange("p (t e) -> p t e", t=NT)
        pastn = piece(NT * E, 1).rearrange("p (t e) -> p t e", t=NT)
        owner, first_tile, inner, base, row = [piece(NT, 1) for _ in range(5)]
        big = patches[:].rearrange("p s g b t -> p (s g b t)")
        graw = big[0:NP1, 0:5 * C * PATCH * S].rearrange("p (c k x) -> p c k x", c=5 * C, k=PATCH)
        patched = [[wv_all[0:NP1].rearrange("p e m f -> p (e m f)")[:, C * PATCH * S * (2 * t + q):C * PATCH * S * (2 * t + q + 1)]
                    .rearrange("p (x n) -> p x n", x=NP1) for q in range(2)] for t in range(2)]
        S_ = {}

        def s(name):
            if name not in S_:
                S_[name] = sem(name)
            return S_[name]

        o = 5 * C * PATCH * S
        wc_raw = big[:, o:o + 640].rearrange("p (g k) -> p g k", g=5)
        wo_raw = big[:, o + 640:o + 1152].rearrange("p (j e) -> p j e", j=4)
        pj_raw = big[0:NF, o + 1152:o + 1280].rearrange("p (t d) -> p t d", t=2)
        pjT = big[:, o + 1280:o + 1408]
        woT = big[:, o + 1408:o + 2432].rearrange("p (j h n) -> p j h n", j=4, h=2)
        bT = big[:, o + 2432:o + 3277].rearrange("p (g y x) -> p g y x", g=5, y=NP1)
        selr = big[:, o + 3789:o + 4813]
        wv_c = big[:, o + 3277:o + 3789].rearrange("p (j d) -> p j d", j=4)
        qkv_raw = xrow_all[:, 0:12 * D].rearrange("p (t j d) -> p t j d", t=3, j=4)
        zeros = xrow_all[:, 12 * D:12 * D + 384]

        def tails(columns):
            return columns[:, 2 * HEAD:].rearrange("p (i t) -> p i t", i=2)[:, :, 0:TAIL]

        def by_image(columns):
            return columns.rearrange("p (i t) -> p i t", i=2)

        image_sum = bank[0][0:R1, 0:4]
        logits = bank[6][:, 0:NCH * E]
        ranks = bank[2][:, 0:(NCH + 1) * E]

        block = ctx.enter_context(nc.Block())

        def steps(eng, step):
            def group(g, first=False, fr=True, par=0):
                for k in range(4):
                    step(4 * g + k, k, g, par, True, not (first and k < 1), not (first and k < 2),
                         not (first and k < 3), fr)
            group(0, first=True)
            with eng.Fori(0, (NG - 2) // 2) as i:
                group(2 * i + 1, par=1)
                group(2 * i + 2, par=0)
            group(NG - 1, fr=False, par=1)
            for k in range(3):
                step(NPAIR + k, k, NG, 0, False, k < 1, k < 2, True, False)

        def pairs(n):
            return min(n, NPAIR) if isinstance(n, int) else n

        def pairs4(n):
            return 4 * pairs(n)

        PIECES = [[(0, 0, 4)], [(0, 4, 4)], [(0, 8, 4)], [(1, 0, 4)], [(1, 4, 4)], [(1, 8, 4)], [(1, 12, 2), (0, 12, 1)]]
        NPIECE = len(PIECES)
        TURN = {2: [None, 0, 1, 2], 3: [3, 4, 5, 6]}

        NRAW = 3 * GI + 4
        NSMALL = 11

        setup_met = (s("small_in"), 16 * NSMALL)

        @block.sync
        def _(sp):
            sp.dma_start(cst[:], const[:, 0:NKEPT]).then_inc(s("small_in"), 16)
            sp.dma_start(selr, const[:, NKEPT:]).then_inc(s("small_in"), 16)
            sp.dma_start(wc_raw, convw.rearrange("e (g c) y x -> e g (c y x)", g=5)).then_inc(s("small_in"), 16)
            sp.dma_start(qkv_raw, wqkv.rearrange("(t j e) d -> e t j d", t=3, e=128)).then_inc(s("small_in"), 16)
            sp.dma_start(wo_raw, wout.rearrange("o (j e) -> o j e", j=4)).then_inc(s("small_in"), 16)
            for t in range(2):
                sp.dma_start(pj_raw[:, t], proj).then_inc(s("small_in"), 16)
            sp.dma_start(wg_sb[:], wg).then_inc(s("small_in"), 16)
            sp.dma_start(bout_sb[:], bout.rearrange("(d a) -> d a", a=1)).then_inc(s("small_in"), 16)
            sp.dma_start(convb_sb[:], convb.rearrange("(d a) -> d a", a=1)).then_inc(s("small_in"), 16)
            sp.dma_start(tokid[:], const[:, SEG["tok"][0]:SEG["tok"][1]]).then_inc(s("small_in"), 16)
            sp.dma_start(graw, gamma.rearrange("c (y k) x -> y c k x", k=PATCH)).then_inc(s("gamma_in"), 16)
            sp.dma_start(braw, beta.rearrange("c (y k) x -> y c k x", k=PATCH)).then_inc(s("beta_in"), 16)

            def load_group(g):
                at_least(sp, s("norm_done"), 2 * g)
                for b in range(GI):
                    img = x[bass.ds(GI * g + b, 1)].rearrange("b c y x -> (b c) y x")
                    sp.dma_start(raw0[NP1 * b:NP1 * (b + 1)], img.rearrange("c (y k) x -> y c k x", k=PATCH)
                                 ).then_inc(s("raw_in"), 16)
                    for c in range(C):
                        sp.dma_start(raw44[NP2 * b + 1:NP2 * b + NP1, c, :, HALF:HALF + S],
                                     img[c, HALF:S - HALF].rearrange("(y k) x -> y k x", k=PATCH)
                                     ).then_inc(s("raw_in"), 16)
                imgs = x[bass.ds(GI * g, GI)]
                for c in range(C):
                    for p0, k0, y0 in ((0, HALF, 0), (NP1, 0, S - HALF)):
                        sp.dma_start(raw44[p0:R1:NP2, c, k0:k0 + HALF, HALF:HALF + S], imgs[:, c, y0:y0 + HALF]
                                     ).then_inc(s("raw_in"), 16)

            sp.wait_ge(s("pads_zero"), 1)
            load_group(0)
            sp.wait_ge(s("small_in"), 16 * NSMALL)
            pad = K("padrow").rearrange("p (a n) -> p a n", a=2)
            sp.dma_start(out[NTOK:NTOK + TT].rearrange("(a p) n -> p a n", a=2), pad[:, :, 0:D]).then_inc(s("pads_out"), 16)
            sp.dma_start(sorted_rows[E * CAP:E * CAP + TT].rearrange("(a p) n -> p a n", a=2), pad).then_inc(s("pads_out"), 16)

            def step(n, k, g, par, a, b, c, d, fr):
                if fr and k == 0:
                    load_group(g + 1)
                if isinstance(n, int) and n == 2:
                    sp.wait_ge(s("setup_mm"), 12)
                    sp.wait_ge(s("beta_mm"), 5)
                    for e in range(E):
                        sp.dma_start(wv_all[:, e, 0], ffw[e]).then_inc(s("weights_in"), 16)
                        sp.dma_start(wv_all[:, e, 1], ffv[e]).then_inc(s("weights_in"), 16)
                if c:
                    m = n - 2
                    sp.wait_ge(s("h2_copied"), m + 1)
                    for ch, row, first, rows in PLACES:
                        sp.dma_start(out[bass.ds(m * PT + first, rows)], h2[row:row + rows, k % 2, ch]).then_inc(s(f"h2_out{k % 2}"), 16)
            steps(sp, step)
            sp.wait_ge(s("ends_ready"), 1)
            for e in range(E):
                r = sp.value_load(ends[0:1, e:e + 1], min_val=e * CAP, max_val=e * CAP + NTOK)
                sp.dma_start(sorted_rows[bass.ds(r, TT)].rearrange("(a p) n -> p a n", a=2), pad).then_inc(s("pads_out"), 16)
            for q in range(2):
                sp.wait_ge(s(f"h2_out{q}"), NPAIR // 2 * 64)
            sp.wait_ge(s("pads_out"), 16 * (2 + E))
            sp.wait_ge(s("weights_in"), 16 * 2 * E)

        @block.tensor
        def _(pe):
            item = [0]

            def begin():
                at_least(pe, s("setup_copied"), item[0] - 5)
                item[0] += 1
                return bank[(item[0] - 1) % 6]

            def end(mm):
                mm.then_inc(s("setup_mm"), 1)

            pe.wait_ge(s("small_in"), 16 * NSMALL)
            o_ = begin()
            for g in range(4):
                mm_ = pe.transpose(o_[:, 128 * g:128 * g + 128], wc_raw[:, g], ident)
            end(mm_)
            o_ = begin()
            pe.transpose(o_[:, 0:128], wc_raw[:, 4], ident)
            end(pe.transpose(o_[:, 128:192], pj_raw.rearrange("p t d -> p (t d)"), ident[0:NF, 0:NF]))
            o_ = begin()
            for j in range(4):
                mm_ = pe.transpose(o_[:, 128 * j:128 * j + 128], wo_raw[:, j], ident)
            end(mm_)
            pe.wait_ge(s("setup_copied"), 2)
            for t in range(2):
                o_ = begin()
                for j in range(4):
                    mm_ = pe.matmul(o_[:, 128 * j:128 * j + 128], qkv_raw[:, t, j], pjT, start=True, stop=True)
                end(mm_)
            pe.wait_ge(s("setup_copied"), 3)
            pe.wait_ge(s("wv_centred"), 1)
            for jj in range(2):
                o_ = begin()
                for j in range(2 * jj, 2 * jj + 2):
                    mm_ = pe.matmul(o_[:, 256 * (j % 2):256 * (j % 2) + 256], wv_c[:, j],
                                    woT[:, j].rearrange("p h n -> p (h n)"), start=True, stop=True)
                end(mm_)
            def beta(g):
                pe.wait_ge(s("beta_patched"), g + 1)
                at_least(pe, s("beta_copied"), g - 1)
                for px in range(NP1):
                    q = pe.transpose(bank[6 + g % 2][:, NP1 * px:NP1 * px + NP1], patched[1][g % 2][:, px], ident[0:NP1, 0:NP1])
                q.then_inc(s("beta_mm"), 1)

            for g in range(5):
                o_ = begin()
                pe.wait_ge(s("gamma_patched"), g + 1)
                for px in range(NP1):
                    mm_ = pe.transpose(o_[:, NP1 * px:NP1 * px + NP1], patched[0][g % 2][:, px], ident[0:NP1, 0:NP1])
                end(mm_)
            beta(0)
            beta(1)
            pe.wait_ge(s("setup_copied"), item[0])

            def image_stats(G):
                pe.wait_ge(s("part_ready"), G + 1)
                at_least(pe, s("front_evac"), NPIECE * G)
                pe.matmul(image_sum[:, 0:2], K("sel44")[0:R1], part[:, 0:2], start=True, stop=True)
                pe.matmul(image_sum[:, 2:4], K("sel0")[0:R1], part[:, 0:2], start=True, stop=True
                          ).then_inc(s("imgstat_done"), 1)

            def front_piece(G, f, at_bank=0, ahead=0):
                pe.wait_ge(s("norm_done"), 2 * G + 1 + PIECES[f][0][0])
                at_least(pe, s("front_evac"), NPIECE * G + f - ahead)
                if f == 0:
                    pe.wait_ge(s("imgstat_read"), G + 1)
                at = 0
                for kind, px0, w in PIECES[f]:
                    src, rows = ((nrm0, R0), (nrm44, R1))[kind]
                    for px in range(px0, px0 + w):
                        t = pe.transpose(bank[at_bank][:, at:at + rows], src[:, px], ident[0:rows, 0:rows])
                        at += rows
                t.then_inc(s("front_t"), 1)

            image_stats(0)
            for f in range(NPIECE):
                front_piece(0, f, f % 4, 3)
                if f < 3:
                    beta(f + 2)
            pe.wait_ge(s("beta_copied"), 5)
            for g in range(5):
                mm_ = pe.matmul(bank[7][:, 0:TOK], wct[:, g], bT[:, g].rearrange("p y x -> p (y x)"), start=(g == 0), stop=(g == 4))
            mm_.then_inc(s("cbeta_mm"), 1)
            pe.wait_ge(s("front_evac"), NPIECE)
            pe.wait_ge(s("cbeta_ready"), 1)

            def step(n, k, g, par, a, b, c, d, fr):
                mb, mc, md = n - 1, n - 2, n - 3
                pb, pc, pd = (k + 1) % 2, k % 2, (k + 1) % 2

                def front(i):
                    if fr and k in TURN and TURN[k][i] is not None:
                        front_piece(g + 1, TURN[k][i])

                def broadcast(j):
                    for i in range(2):
                        t = pe.matmul(bank[(7, 1)[j % 2]][:, (TOK + 1) * i:(TOK + 1) * (i + 1)], pick_head[:, i, j], rparts[:],
                                      start=True, stop=True)
                    t.then_inc(s("bc_done"), 1)

                def k_tokens(j):
                    products(bank[4 + j % 2][:, :], lambda a_: xT[:, pb, a_, 128 * j:128 * j + 128], lambda a_: wkp[:, a_]
                             ).then_inc(s("k_mm"), 1)

                def q_feature(j):
                    products(bank[4 + j % 2][:, 0:NCH * 128], lambda a_: wqp[:, a_, 128 * j:128 * j + 128],
                             lambda a_: xT[:, pb, a_]).then_inc(s("q_mm"), 1)

                if b:
                    pe.wait_ge(s("xT_low"), mb + 1)
                    at_least(pe, s("k_exp"), NCH * mb)
                    for j in range(2):
                        q_feature(j)
                if c:
                    pe.wait_ge(s("m_evac"), 4 * (mc + 1))
                    pe.wait_ge(s("q_exp"), 4 * (mc + 1))
                    at_least(pe, s("attn_added"), mc)
                    for j in range(4):
                        for i in range(2):
                            t = pe.matmul(bank[7][32 * i:32 * i + HEADS, 0:TOK], mm[:, pc, i, j, D:],
                                          qf[:, pc, j, TOK * i:TOK * i + TOK], start=(j == 0), stop=(j == 3))
                    t.then_inc(s("d8_done"), 1)
                if a:
                    pe.wait_ge(s("front_evac"), NPIECE * (g + 1))
                    at_least(pe, s("m_evac"), 4 * (n - 1))
                    for q in range(5):
                        t = pe.matmul(bank[1][:, 0:PT], wct[:, q],
                                      patches[:, par, q, 2 * k:2 * k + 2].rearrange("p b t -> p (b t)"),
                                      start=(q == 0), stop=(q == 4))
                    t.then_inc(s("conv_done"), 1)
                if d:
                    pe.wait_ge(s("ln2_x"), md + 1)
                    pe.wait_ge(s("xT_low"), pairs(n))
                    transpose_tokens(lambda ch: xrow[:, pd, 0, ch, 0:D], s("x2t_done"))
                if b:
                    for j in range(2, 4):
                        pe.wait_ge(s("q_exp"), 4 * mb + j - 1)
                        q_feature(j)
                if a:
                    pe.wait_ge(s("h1_ready"), n + 1)
                    at_least(pe, s("h2_copied"), n - 2)
                    t = token_rows(h1T[:, k])
                    t.then_inc(s("h1t_done"), 1)
                front(0)
                if d:
                    pe.wait_ge(s("x2T_copied"), md + 1)
                    at_least(pe, s("m_evac"), pairs4(mb))
                    for ch in range(NCH):
                        t = pe.matmul(logits[:, E * ch:E * ch + E], x2T[:, 128 * ch:128 * ch + 128], wg_sb[:], start=True, stop=True)
                    t.then_inc(s("logit_done"), 1)
                if c:
                    pe.wait_ge(s("rden_ready"), mc + 1)
                    broadcast(0)
                    if a:
                        pe.wait_ge(s("h1_ready"), n + 1)
                    broadcast(1)
                if b:
                    for j in range(2):
                        pe.wait_ge(s("q_exp"), 4 * mb + 3 + j)
                        k_tokens(j)
                for j in range(2, 4):
                    if c:
                        pe.wait_ge(s("qn_done"), 4 * mc + j - 1)
                        broadcast(j)
                    if b and j < NCH:
                        pe.wait_ge(s("k_exp"), NCH * mb + j - 1)
                        k_tokens(j)
                if b:
                    pe.wait_ge(s("x_ones"), mb + 1)
                    pe.wait_ge(s("k_exp"), NCH * mb + 1)
                    at_least(pe, s("m_evac"), 4 * mb)
                    if d:
                        pe.wait_ge(s("logit_read"), md + 1)
                    context_head(pb, 0)
                if a:
                    pe.wait_ge(s("ln1_x"), n + 1)
                    at_least(pe, s("x2T_copied"), n - 2)
                    transpose_tokens(lambda ch: xtok[:, pc, ch], s("xt_done"))
                front(1)
                for i in range(2):
                    if c:
                        pe.wait_ge(s("qn_done"), 4 * mc + 4)
                        for j in range(4):
                            t = pe.matmul(bank[7][:, TOK * i:TOK * i + TOK], mm[:, pc, i, j, 0:D],
                                          qf[:, pc, j, TOK * i:TOK * i + TOK], start=(j == 0), stop=(j == 3))
                        if i == 1:
                            t.then_inc(s("out_done"), 1)
                    if d and i == 1:
                        pe.wait_ge(s("before_step"), NCH * (md + 1))
                        if a:
                            pe.wait_ge(s("ln1_x"), n + 1)
                        else:
                            pe.wait_ge(s("h2_copied"), n - 2)
                        pe.matmul(ranks[:, :], ones, before[:].rearrange("p c e -> p (c e)"), start=True, stop=False)
                        pe.matmul(ranks[:, 0:NCH * E], tri, both[:].rearrange("p c e -> p (c e)"), start=False, stop=True
                                  ).then_inc(s("rank_done"), 1)
                if b:
                    if a:
                        pe.wait_ge(s("h1_ready"), n + 1)
                    pe.wait_ge(s("k_exp"), NCH * mb + NCH)
                    context_head(pb, 1)
                    context_tails(pb)
                front(2)
                if c:
                    pe.wait_ge(s("attn_added"), mc + 1)
                    if a:
                        pe.wait_ge(s("ln1_x"), n + 1)
                    if d:
                        pe.wait_ge(s("rank_read"), md + 1)
                    t = token_rows(h1T[:, (k + 2) % 4])
                    t.then_inc(s("h2t_done"), 1)
                if b:
                    pe.wait_ge(s("g_copied"), 2 * mb + 1)
                    context_out(0, 0)
                    pe.wait_ge(s("g_copied"), 2 * mb + 2)
                    context_out(0, 1)
                front(3)
                if fr and k == 1:
                    image_stats(g + 1)
                if b:
                    pe.wait_ge(s("m_evac"), 4 * mb + 1)
                    context_out(1, 0)
                    pe.wait_ge(s("m_evac"), 4 * mb + 2)
                    context_out(1, 1)

            def products(o_, left, right):
                pe.matmul(o_, left(0), right(0), start=True, stop=False)
                pe.matmul(o_, left(0), right(1), start=False, stop=False)
                return pe.matmul(o_, left(1), right(0), start=False, stop=True)

            def transpose_tokens(src, done):
                for ch in range(NCH):
                    t = pe.transpose(bank[3][:, 128 * ch:128 * ch + 128], src(ch), ident)
                t.then_inc(done, 1)

            def token_rows(columns):
                for ch, row, first, rows in PLACES:
                    if rows == HEAD:
                        pe.transpose(bank[2][:, D * ch:D * ch + D], columns[:, first:first + HEAD], ident)
                    else:
                        t = pe.matmul(bank[2][row:row + 64, D * ch:D * ch + D], columns[:, first:first + 64], ident,
                                      start=True, stop=True)
                return t

            def context_head(p, i):
                pe.matmul(bank[(6, 1)[i]][:, :], xtok[:, p, i], kf[:, i], start=True, stop=False)

            def context_tails(p):
                for i in range(2):
                    r = slice(64 * i, 64 * i + TAIL)
                    t = pe.matmul(bank[(6, 1)[i]][:, :], xtok[r, p, 2], kf[r, 2], start=False, stop=True)
                    t.then_inc(s("g_done"), 1)

            def context_out(i, jj):
                o_ = bank[(6, 1)[jj]]
                for h in range(4 * jj, 4 * jj + 4):
                    col = (h // 2 % 2) * (D + HEADS)
                    t = pe.matmul(o_[64 * (h % 2):64 * (h % 2) + 64, col:col + D + HEADS], gT[:, i, NF * h:NF * h + NF],
                                  wvo[:, h], start=True, stop=True)
                t.then_inc(s("m_done"), 1)

            steps(pe, step)

        @block.vector
        def _(ve):
            ve.memset(raw44[:], 0.0).then_inc(s("pads_zero"), 1)
            ve.memset(pjT, 0.0).then_inc(s("setup_zero"), 1)
            ve.memset(woT, 0.0).then_inc(s("setup_zero"), 1)
            ve.memset(before[:], 0.0).then_inc(s("setup_zero"), 1)
            ve.memset(h1T[:, :, PT:], 0.0)
            ve.memset(zeros, 0.0).then_inc(s("setup_zero"), 1)
            ve.wait_ge(s("small_in"), 16 * NSMALL)
            ve.wait_ge(s("setup_zero"), 4)
            ve.tensor_copy(rparts[:], zeros[0:104, 0:TOK + 1])
            for p in range(2):
                for a_ in range(2):
                    t = ve.tensor_copy(xT[:, p, a_], zeros)
            t.then_inc(s("parts_zero"), 1)
            ve.wait_ge(s("parts_zero"), 1)
            ve.tensor_copy(pick_head[:], selr[0:104].rearrange("p (i j f) -> p i j f", i=2, j=4))
            for j in range(4):
                t = ve.tensor_scalar(wv_c[:, j], qkv_raw[:, 2, j], qkv_raw[:, 2, j, D - 1:D], None, ALU.subtract)
            t.then_inc(s("wv_centred"), 1)
            ve.tensor_copy(wvo[:, :, D:], K("e127").rearrange("p (h g) -> p h g", h=HEADS)).then_inc(s("wvo_ready"), 1)
            item = [0]

            def begin():
                item[0] += 1
                ve.wait_ge(s("setup_mm"), item[0])
                return bank[(item[0] - 1) % 6]

            def end(t):
                t.then_inc(s("setup_copied"), 1)

            o_ = begin()
            end(ve.tensor_copy(wct[:, 0:4].rearrange("p g k -> p (g k)"), o_[:, :]))
            o_ = begin()
            ve.tensor_copy(wct[:, 4], o_[:, 0:128])
            for h in range(2):
                t = ve.tensor_copy(pjT[64 * h:64 * h + 64, 64 * h:64 * h + 64], o_[64 * h:64 * h + 64, 128:192])
            end(t)
            o_ = begin()
            for h in range(2):
                t = ve.tensor_copy(woT[64 * h:64 * h + 64, :, h], o_[64 * h:64 * h + 64, :].rearrange("p (j n) -> p j n", j=4))
            end(t)
            o_ = begin()
            ve.tensor_scalar(wqp[:, 0], o_[:, :], QS, None, ALU.mult).then_inc(s("high_weights"), 1)
            ve.wait_ge(s("high_weights"), 1)
            end(ve.scalar_tensor_tensor(out=wqp[:, 1], in0=o_[:, :], scalar=QS, in1=wqp[:, 0].bitcast(F32),
                                        op0=ALU.mult, op1=ALU.subtract))
            o_ = begin()
            ve.tensor_copy(wkp[:, 0], o_[:, :]).then_inc(s("high_weights"), 1)
            ve.wait_ge(s("high_weights"), 2)
            end(ve.tensor_tensor(wkp[:, 1], o_[:, :], wkp[:, 0].bitcast(F32), ALU.subtract))
            for jj in range(2):
                o_ = begin()
                end(ve.tensor_copy(wvo[:, 4 * jj:4 * jj + 4, 0:D], o_[:, :].rearrange("p (h n) -> p h n", h=4)))

            def patch_gamma(g):
                ve.tensor_copy(patched[0][g % 2].rearrange("p x (k i) -> p k x i", i=PATCH),
                               graw[:, C * g:C * g + C].rearrange("p c k (x i) -> p (c k) x i", i=PATCH)
                               ).then_inc(s("gamma_patched"), 1)

            ve.wait_ge(s("gamma_in"), 16)
            patch_gamma(0)
            patch_gamma(1)
            for g in range(5):
                o_ = begin()
                end(ve.tensor_copy(gam[:, g], o_[:, 0:TOK].rearrange("p (x y) -> p x y", x=NP1)))
                if g < 3:
                    patch_gamma(g + 2)
            ve.wait_ge(s("setup_copied"), item[0])

            def image_parts(G):
                ve.wait_ge(s("colsum_ready"), 4 * (G + 1))
                sums = colsum[:].rearrange("p (s e) -> p e s", e=2)
                ve.tensor_scalar(part[:, 2:4], sums[:, 0], K("wab")[0:R1, 0:1], None, ALU.mult).then_inc(s("part_a"), 1)
                ve.wait_ge(s("part_a"), G + 1)
                at_least(ve, s("imgstat_done"), G)
                ve.scalar_tensor_tensor(out=part[:, 0:2], in0=sums[:, 1], scalar=K("wab")[0:R1, 1:2], in1=part[:, 2:4],
                                        op0=ALU.mult, op1=ALU.add).then_inc(s("part_ready"), 1)

            def image_var(G):
                ve.wait_ge(s("imgstat_done"), G + 1)
                ve.tensor_copy(imgstat[:], image_sum[:, :].rearrange("p (l s) -> p l s", l=2)).then_inc(s("imgstat_read"), 1)
                ve.wait_ge(s("imgstat_read"), G + 1)
                ve.tensor_tensor(imgtmp[:], imgstat[:, :, 0], imgstat[:, :, 0], ALU.mult).then_inc(s("mean_squared"), 1)
                ve.wait_ge(s("mean_squared"), G + 1)
                ve.tensor_tensor(imgvar[:], imgstat[:, :, 1], imgtmp[:], ALU.subtract).then_inc(s("imgvar_ready"), 1)

            def image_norm(G, kind):
                raw, nrm, l, rows = ((raw0, nrm0, 1, R0), (raw44, nrm44, 0, R1))[kind]
                ve.wait_ge(s("imgrstd_ready"), G + 1)
                at_least(ve, s("front_t"), NPIECE * G)
                ve.tensor_scalar(nrm[:].rearrange("p x (k i) -> p k x i", i=PATCH),
                                 raw[:].rearrange("p c k (x i) -> p (c k) x i", i=PATCH), imgstat[0:rows, l, 0:1],
                                 imgrstd[0:rows, l:l + 1], ALU.subtract, ALU.mult).then_inc(s("norm_done"), 1)

            def front_piece(G, f, par, at_bank=0):
                ve.wait_ge(s("front_t"), NPIECE * G + f + 1)
                at = 0
                for kind, px0, w in PIECES[f]:
                    n_ = (NP1, NP2)[kind]
                    src = bank[at_bank][:, at:at + GI * n_ * w].rearrange("p (x b y) -> p x b y", x=w, b=GI)
                    at += GI * n_ * w
                    for q, dy, dx in ([(0, 0, 0)] if kind == 0 else [(1, 1, 0), (2, 1, 1), (3, 0, 0), (4, 0, 1)]):
                        lo, hi = max(px0 - dx, 0), min(px0 + w - dx, NP1)
                        if lo >= hi:
                            continue
                        i0 = lo + dx - px0
                        dst = patches[:, par, q].rearrange("p b (y x) -> p x b y", y=NP1)
                        t = ve.tensor_tensor(dst[:, lo:hi], src[:, i0:i0 + hi - lo, :, dy:dy + NP1],
                                             gam[:, q, lo:hi].unsqueeze(2).to_broadcast([128, hi - lo, GI, NP1]), ALU.mult)
                t.then_inc(s("front_evac"), 1)

            def norm_stats(src, which, m, stat, agg):
                for ch in range(NCH):
                    ve.bn_stats(bns[:, which, ch], src(ch)).then_inc(stat, 1)
                wait_alone(ve, setup_met, (stat, NCH * m + NCH))
                for ch in range(NCH):
                    ve.bn_aggr(mv[:, which, ch], bns[:, which, ch]).then_inc(agg, 1)

            image_parts(0)
            image_var(0)
            image_norm(0, 0)
            image_norm(0, 1)
            for f in range(NPIECE):
                front_piece(0, f, 0, f % 4)
            ve.wait_ge(s("cbeta_mm"), 1)
            ve.tensor_scalar(cbeta[:], bank[7][:, 0:TOK], convb_sb[:, 0:1], None, ALU.add).then_inc(s("cbeta_ready"), 1)
            ve.wait_ge(s("cbeta_ready"), 1)

            def step(n, k, g, par, a, b, c, d, fr):
                mb, mc, md = n - 1, n - 2, n - 3
                pb, pc, pd = (k + 1) % 2, k % 2, (k + 1) % 2
                half = lambda off: 2 * g + (k + off) // 2

                def front(i):
                    if fr and k in TURN and TURN[k][i] is not None:
                        if TURN[k][i] == 0:
                            at_least(ve, s("conv_done"), 4 * g)
                        front_piece(g + 1, TURN[k][i], 1 - par)

                def normalise(j):
                    ve.wait_ge(s("bc_done"), 4 * mc + j + 1)
                    q = qf[:, pc, j].rearrange("p (i t) -> p i t", i=2)
                    ve.tensor_tensor(q, q, bank[(7, 1)[j % 2]][:, 0:PT + 2].rearrange("p (i t) -> p i t", i=2)[:, :, 0:TOK],
                                     ALU.mult).then_inc(s("qn_done"), 1)

                if d:
                    ve.wait_ge(s("ln2_rstd"), md + 1)
                    at_least(ve, s(f"scattered{pd}"), 128 * half(-3))
                    at_least(ve, s("x2t_done"), md - 1)
                    for ch in range(NCH):
                        t = ve.tensor_scalar(xrow[:, pd, 0, ch, 0:D], h2[:, pd, ch], mv[:, 1, ch, 0:1],
                                             rstd[:, 1, ch:ch + 1], ALU.subtract, ALU.mult)
                    t.then_inc(s("ln2_x"), 1)
                if c:
                    ve.wait_ge(s("d8_done"), mc + 1)
                    ve.tensor_scalar(dsum[:], bank[7][0:40, 0:TOK], 1e-6, None, ALU.add).then_inc(s("dsum_ready"), 1)
                    ve.wait_ge(s("dsum_ready"), mc + 1)
                    ve.reciprocal(rden[:], dsum[:]).then_inc(s("rden_whole"), 1)
                    ve.wait_ge(s("rden_whole"), mc + 1)
                    for r in (0, 32):
                        t = ve.tensor_copy(rparts[r:r + HEADS, 0:TOK], rden[r:r + HEADS])
                    t.then_inc(s("rden_high"), 1)
                    ve.wait_ge(s("rden_high"), mc + 1)
                    for r in (0, 32):
                        t = ve.tensor_tensor(rparts[64 + r:64 + r + HEADS, 0:TOK], rden[r:r + HEADS],
                                             rparts[r:r + HEADS, 0:TOK].bitcast(F32), ALU.subtract)
                    t.then_inc(s("rden_ready"), 1)
                if a:
                    ve.wait_ge(s("conv_done"), n + 1)
                    at_least(ve, s("h2t_done"), n - 3)
                    ve.tensor_tensor(by_image(h1T[:, k, 0:PT]),
                                     bank[1][:, 0:PT].rearrange("p (b t) -> p b t", b=2),
                                     cbeta[:].unsqueeze(1).to_broadcast([128, 2, TOK]), ALU.add).then_inc(s("h1_ready"), 1)
                if fr and k == 2:
                    image_norm(g + 1, 0)
                if a:
                    ve.wait_ge(s("h1t_done"), n + 1)
                    norm_stats(lambda ch: bank[2][:, D * ch:D * ch + D], 0, n, s("ln1_bn"), s("ln1_mv"))
                if c:
                    normalise(0)
                    normalise(1)
                if d:
                    best(md)
                if fr and k == 2:
                    image_norm(g + 1, 1)
                front(0)
                if a:
                    ve.wait_ge(s("ln1_rstd"), n + 1)
                    at_least(ve, s("g_done"), 2 * (n - 1))
                    for ch in range(NCH):
                        t = ve.tensor_scalar(xtok[:, pc, ch], bank[2][:, D * ch:D * ch + D], mv[:, 0, ch, 0:1],
                                             rstd[:, 0, ch:ch + 1], ALU.subtract, ALU.mult)
                    t.then_inc(s("ln1_x"), 1)
                if c:
                    normalise(2)
                    normalise(3)
                if d:
                    choose(md)
                front(1)
                if fr and k == 1:
                    image_parts(g + 1)
                if a:
                    ve.wait_ge(s("xt_done"), n + 1)
                    ve.memset(xtok[:, pc, :, D - 1:D], 1.0).then_inc(s("x_ones"), 1)
                    ve.wait_ge(s("xT_high"), n + 1)
                    ve.tensor_tensor(xT[:, pc, 1], bank[3][:, 0:NCH * 128], xT[:, pc, 0].bitcast(F32), ALU.subtract
                                     ).then_inc(s("xT_low"), 1)
                if d:
                    place(md, pd, 128 * half(-3))
                if c:
                    ve.wait_ge(s("out_done"), mc + 1)
                    ve.scalar_tensor_tensor(out=h1T[:, (k + 2) % 4, 0:PT], in0=bank[7][:, 0:PT], scalar=bout_sb[:, 0:1],
                                            in1=h1T[:, (k + 2) % 4, 0:PT], op0=ALU.add, op1=ALU.add).then_inc(s("attn_added"), 1)
                front(2)
                if c:
                    ve.wait_ge(s("h2_copied"), mc + 1)
                    norm_stats(lambda ch: h2[:, pc, ch], 1, mc, s("ln2_bn"), s("ln2_mv"))
                front(3)
                if fr and k == 1:
                    image_var(g + 1)

            def best(m):
                ve.wait_ge(s("logit_done"), m + 1)
                ve.tensor_copy(logit[:], logits[:, :].rearrange("p (c e) -> p c e", c=NCH)).then_inc(s("logit_read"), 1)
                wait_alone(ve, setup_met, (s("logit_read"), m + 1))
                for ch in range(NCH):
                    ve.max(top[:, ch], logit[:, ch]).then_inc(s("top_ready"), 1)
                ve.wait_ge(s("top_ready"), NCH * m + NCH)
                ve.tensor_tensor(gap[:], top[:, :, 1], top[:, :, 0], ALU.subtract).then_inc(s("gap_ready"), 1)

            def choose(m):
                for ch in range(NCH):
                    t = ve.max_index(topi[:, ch], top[:, ch], logit[:, ch])
                t.then_inc(s("topi_ready"), 1)
                ve.wait_ge(s("topi_ready"), m + 1)
                ve.tensor_tensor(topf[:], topi[:, :, 0:2], K("dup").rearrange("p (c j) -> p c j", c=NCH), ALU.add
                                 ).then_inc(s("topf_ready"), 1)
                ve.wait_ge(s("topf_ready"), m + 1)
                for j in range(2):
                    t = ve.tensor_tensor(pick[:, j], K("iota8").unsqueeze(1).to_broadcast([128, NCH, E]),
                                         topf[:, :, j:j + 1].to_broadcast([128, NCH, E]), ALU.is_equal)
                t.then_inc(s("pick_ready"), 1)
                ve.wait_ge(s("pick_ready"), m + 1)
                ve.tensor_tensor(both[:], pick[:, 0], pick[:, 1], ALU.add).then_inc(s("both_ready"), 1)
                ve.wait_ge(s("both_ready"), m + 1)
                for ch in range(NCH):
                    ve.tensor_tensor(before[:, ch + 1], before[:, ch], both[:, ch], ALU.add).then_inc(s("before_step"), 1)
                    if ch < NCH - 1:
                        ve.wait_ge(s("before_step"), NCH * m + ch + 1)
                ve.wait_ge(s("before_step"), NCH * m + NCH)

            def place(m, p, scattered):
                ve.wait_ge(s("egap_ready"), m + 1)
                ve.tensor_scalar(esum[:], egap[:], 1.0, None, ALU.add).then_inc(s("esum_ready"), 1)
                ve.wait_ge(s("esum_ready"), m + 1)
                ve.reciprocal(xrow[:, p, 0, :, D], esum[:]).then_inc(s("w0_ready"), 1)
                ve.wait_ge(s("w0_ready"), m + 1)
                ve.tensor_tensor(xrow[:, p, 1, :, D], egap[:], xrow[:, p, 0, :, D], ALU.mult).then_inc(s("w1_ready"), 1)
                ve.wait_ge(s("rank_done"), m + 1)
                rank = ranks[:, :].rearrange("p (c e) -> p c e", c=NCH + 1)
                ve.tensor_tensor(slots[:], rank[:, 0:NCH], K("iotacap").unsqueeze(1).to_broadcast([128, NCH, E]), ALU.add
                                 ).then_inc(s("slots_ready"), 1)
                ve.tensor_copy(counts[:], rank[:, NCH]).then_inc(s("counts_ready"), 1)
                ve.tensor_copy(before[0:1, 0], rank[0:1, NCH]).then_inc(s("rank_read"), 1)
                ve.wait_ge(s("slots_ready"), m + 1)
                ve.tensor_tensor(pslot[:], slots[:].unsqueeze(1).to_broadcast([128, 2, NCH, E]), pick[:], ALU.mult).then_inc(s("pslot_ready"), 1)
                ve.wait_ge(s("pslot_ready"), m + 1)
                ve.tensor_reduce(slotf[:], pslot[:], AX_X, ALU.add).then_inc(s("slotf_ready"), 1)
                ve.wait_ge(s("slotf_ready"), m + 1)
                at_least(ve, s(f"scattered{p}"), scattered)
                ve.tensor_copy(sloti[:, p, :, 0:NCH], slotf[:])
                ve.tensor_copy(sloti[0:64, p, :, NCH], slotf[64:128, :, NCH - 1]).then_inc(s("sloti_ready"), 1)

            steps(ve, step)

            link = [0]

            def chain(q):
                link[0] += 1
                q.then_inc(s("table_step"), 1)
                ve.wait_ge(s("table_step"), link[0])

            ve.wait_ge(s("counts_ready"), NPAIR)
            chain(ve.tensor_tensor(endf[:], counts[0:1], K("iotacap")[0:1], ALU.add))
            ve.tensor_copy(ends[:], endf[:]).then_inc(s("ends_ready"), 1)
            chain(ve.tensor_tensor(has[:], counts[0:1].unsqueeze(2).to_broadcast([1, E, TILES_E]),
                                   K("steps")[0:1].unsqueeze(1).to_broadcast([1, E, TILES_E]), ALU.is_gt))
            chain(ve.tensor_reduce(tiles[:], has[:], AX_X, ALU.add))
            chain(ve.tensor_tensor(upto[:], tiles[:].unsqueeze(1).to_broadcast([1, E, E]),
                                   K("incl")[0:1].rearrange("p (a b) -> p a b", a=E), ALU.mult))
            chain(ve.tensor_reduce(cum[:], upto[:], AX_X, ALU.add))
            chain(ve.tensor_tensor(past[:], K("tile")[0:1].unsqueeze(2).to_broadcast([1, NT, E]),
                                   cum[:].unsqueeze(1).to_broadcast([1, NT, E]), ALU.is_ge))
            chain(ve.tensor_tensor(pastn[:], past[:], tiles[:].unsqueeze(1).to_broadcast([1, NT, E]), ALU.mult))
            chain(ve.tensor_reduce(owner[:], past[:], AX_X, ALU.add))
            chain(ve.tensor_reduce(first_tile[:], pastn[:], AX_X, ALU.add))
            chain(ve.tensor_tensor(inner[:], K("tile")[0:1], first_tile[:], ALU.subtract))
            chain(ve.tensor_scalar(base[:], owner[:], float(CAP), None, ALU.mult))
            chain(ve.scalar_tensor_tensor(out=row[:], in0=inner[:], scalar=float(TT), in1=base[:], op0=ALU.mult, op1=ALU.add))
            ve.tensor_scalar(table[:, :, 0], row[:], float(E * CAP), None, ALU.min).then_inc(s("table_ready"), 1)
            ve.tensor_scalar(table[:, :, 1], owner[:], float(E - 1), None, ALU.min).then_inc(s("table_ready"), 1)

        @block.scalar
        def _(ac):
            edges = sb("edges", [R1, C * PATCH, 2, HALF])
            edge_out = sb("edge_out", [R1, C * PATCH, 2, HALF])

            def image_sums(G):
                at_least(ac, s("front_t"), NPIECE * G)
                at_least(ac, s("norm_done"), 2 * G)
                at_least(ac, s("part_ready"), G)
                ac.wait_ge(s("raw_in"), 16 * NRAW * (G + 1))
                rows = raw44[:].rearrange("p c k x -> p (c k) x")
                for e_, lo in ((0, HALF), (1, S)):
                    ac.activation(edges[:, :, e_], rows[:, :, lo:lo + HALF], ACT.Copy).then_inc(s("edges_ready"), 1)
                ac.activation(nrm44[:].rearrange("p x n -> p (x n)"), raw44[:].rearrange("p c k x -> p (c k x)"), ACT.Copy,
                              accum_out=colsum[:, 0:1]).then_inc(s("colsum_ready"), 1)
                ac.wait_ge(s("edges_ready"), 2 * (G + 1))
                ac.activation(edge_out[:], edges[:], ACT.Copy, accum_out=colsum[:, 1:2]).then_inc(s("colsum_ready"), 1)

            def image_squares(G):
                ac.wait_ge(s("colsum_ready"), 4 * G + 2)
                ac.activation(nrm44[:].rearrange("p x n -> p (x n)"), raw44[:].rearrange("p c k x -> p (c k x)"), ACT.Square,
                              accum_out=colsum[:, 2:3]).then_inc(s("colsum_ready"), 1)
                ac.activation(edge_out[:], edges[:], ACT.Square, accum_out=colsum[:, 3:4]).then_inc(s("colsum_ready"), 1)

            def patch_beta(g):
                ac.copy(patched[1][g % 2].rearrange("p x (k i) -> p k x i", i=PATCH),
                        braw[:, C * g:C * g + C].rearrange("p c k (x i) -> p (c k) x i", i=PATCH)
                        ).then_inc(s("beta_patched"), 1)

            ac.wait_ge(s("beta_in"), 16)
            patch_beta(0)
            patch_beta(1)
            image_sums(0)
            image_squares(0)
            for g in range(5):
                ac.wait_ge(s("beta_mm"), g + 1)
                ac.copy(bT[:, g].rearrange("p y x -> p x y"), bank[6 + g % 2][:, 0:TOK].rearrange("p (x y) -> p x y", x=NP1)
                        ).then_inc(s("beta_copied"), 1)
                if g < 3:
                    patch_beta(g + 2)

            def step(n, k, g, par, a, b, c, d, fr):
                mb, mc, md = n - 1, n - 2, n - 3
                pb, pc, pd = (k + 1) % 2, k % 2, (k + 1) % 2

                def m_copy(f):
                    i, jj = f // 2, f % 2
                    ac.wait_ge(s("m_done"), 4 * mb + f + 1)
                    ac.copy(mm[:, pb, i, 2 * jj:2 * jj + 2],
                            bank[(6, 1)[jj]][:, 0:2 * (D + HEADS)].rearrange("p (j n) -> p j n", j=2)).then_inc(s("m_evac"), 1)

                def q_exponent(j):
                    ac.wait_ge(s("q_mm"), 4 * mb + j + 1)
                    ac.activation(by_image(qf[:, pb, j])[:, :, 0:HEAD], by_image(bank[4 + j % 2][:, 0:2 * HEAD]), ACT.Exp)
                    ac.activation(by_image(qf[:, pb, j])[:, :, HEAD:], tails(bank[4 + j % 2][:, 0:NCH * 128]),
                                  ACT.Exp).then_inc(s("q_exp"), 1)

                if b:
                    at_least(ac, s("out_done"), mb - 1)
                    q_exponent(0)
                    q_exponent(1)
                if d:
                    ac.wait_ge(s("x2t_done"), md + 1)
                    at_least(ac, s("logit_done"), md)
                    ac.copy(x2T[:], bank[3][:, 0:NCH * 128]).then_inc(s("x2T_copied"), 1)
                if b:
                    q_exponent(2)
                    q_exponent(3)
                if fr and k == 1:
                    image_sums(g + 1)
                if b:
                    at_least(ac, s("g_done"), 2 * mb)
                    for ch in range(NCH):
                        ac.wait_ge(s("k_mm"), NCH * mb + ch + 1)
                        ac.activation(kf[:, ch], bank[4 + ch % 2][:, :], ACT.Exp).then_inc(s("k_exp"), 1)
                if d:
                    ac.wait_ge(s("gap_ready"), md + 1)
                    at_least(ac, s("w1_ready"), md)
                    ac.activation(egap[:], gap[:], ACT.Exp).then_inc(s("egap_ready"), 1)
                if fr and k == 1:
                    image_squares(g + 1)
                if a:
                    ac.wait_ge(s("xt_done"), n + 1)
                    at_least(ac, s("k_mm"), NCH * (n - 1))
                    ac.copy(xT[:, pc, 0], bank[3][:, 0:NCH * 128]).then_inc(s("xT_high"), 1)
                if b:
                    at_least(ac, s("m_done"), 4 * mb)
                    ac.wait_ge(s("g_done"), 2 * mb + 1)
                    ac.copy(gT[:, 0], bank[6][:, :]).then_inc(s("g_copied"), 1)
                    ac.wait_ge(s("g_done"), 2 * mb + 2)
                    ac.copy(gT[:, 1], bank[1][:, :]).then_inc(s("g_copied"), 1)
                    at_least(ac, s("out_done"), mb - 1)
                    m_copy(0)
                if c:
                    ac.wait_ge(s("h2t_done"), mc + 1)
                    at_least(ac, s(f"h2_out{pc}"), 64 * (2 * g + (k - 2) // 2))
                    at_least(ac, s("ln2_x"), mc - 1)
                    ac.copy(h2[:, pc].rearrange("p c n -> p (c n)"), bank[2][:, 0:NCH * D]).then_inc(s("h2_copied"), 1)
                if b:
                    for f in range(1, 4):
                        m_copy(f)
            steps(ac, step)

        @block.gpsimd
        def _(po):
            def root(dst, src, tmp, eps, half, v_done, r_done, turn):
                po.tensor_scalar(tmp, src, eps, 1.0, ALU.add, ALU.mult).then_inc(v_done, 1)
                po.wait_ge(v_done, turn + 1)
                po.tensor_tensor(dst, tmp, half, ALU.pow).then_inc(r_done, 1)

            def image_root(G):
                wait_alone(po, setup_met, (s("imgvar_ready"), G + 1), (s("norm_done"), 2 * G))
                root(imgrstd[:], imgvar[:], imgeps[:], 1e-7, K("mhalf")[0:R1, 0:2], s("imgeps_ready"), s("imgrstd_ready"), G)

            imgeps = sb("imgeps", [R1, 2])
            po.wait_ge(s("small_in"), 16 * NSMALL)
            image_root(0)

            def step(n, k, g, par, a, b, c, d, fr):
                mb, mc, md = n - 1, n - 2, n - 3
                pb, pc, pd = (k + 1) % 2, k % 2, (k + 1) % 2
                if a:
                    wait_alone(po, setup_met, (s("ln1_mv"), NCH * (n + 1)), (s("ln1_x"), n))
                    root(rstd[:, 0], mv[:, 0, :, 1], vare[:, 0], 1e-5, K("mhalf")[:, 0:NCH], s("ln1_vare"), s("ln1_rstd"), n)

                def scatter(chunks):
                    for place_ in chunks:
                        ch, row, _, rows = PLACES[place_]
                        for j in range(2):
                            po.indirect_dma_start(sorted_rows, bass.IndirectOffsetOnAxis(sloti[0:rows, pd, j, place_:place_ + 1], 0),
                                                  xrow[row:row + rows, pd, j, ch], None).then_inc(s(f"scattered{pd}"), 16)

                if d:
                    wait_alone(po, setup_met, (s("ln2_x"), md + 1), (s("tok_next"), md))
                    po.tensor_copy(xrow[:, pd, 1, :, 0:D], xrow[:, pd, 0, :, 0:D]).then_inc(s("row_ready"), 1)
                    for j in range(2):
                        po.tensor_copy(xrow[:, pd, j, :, D + 1], tokid[:]).then_inc(s("row_ready"), 1)
                    wait_alone(po, setup_met, (s("row_ready"), 3 * (md + 1)))
                    po.tensor_scalar(tokid[:], tokid[:], float(PT), 1.0, ALU.add, ALU.mult).then_inc(s("tok_next"), 1)
                    wait_alone(po, setup_met, (s("sloti_ready"), md + 1), (s("w1_ready"), md + 1))
                    scatter((0, 1))
                if c:
                    wait_alone(po, setup_met, (s("ln2_mv"), NCH * (mc + 1)), (s("ln2_x"), mc))
                    root(rstd[:, 1], mv[:, 1, :, 1], vare[:, 1], 1e-5, K("mhalf")[:, 0:NCH], s("ln2_vare"), s("ln2_rstd"), mc)
                if d:
                    wait_alone(po, setup_met, (s("sloti_ready"), md + 1))
                    scatter((2, 3))
                if fr and k == 1:
                    image_root(g + 1)
            steps(po, step)
            for q in range(2):
                po.wait_ge(s(f"scattered{q}"), NPAIR // 2 * 128)



def experts(nc, ffw2, out, cst, table, wv_all, sorted_rows, bank):
    with ExitStack() as ctx:
        def sb(name, shape, dt=F32):
            return ctx.enter_context(nc.sbuf_tensor(name, shape, dt))

        def K(k):
            return cst[:, SEG[k][0]:SEG[k][1]]

        ident = K("ident")
        xr = sb("xr", [128, 2, 2, RW])
        meta_ = sb("meta_", [128, 2, 2, 2])
        dest = sb("dest", [128, 2, 2], U32)
        xT = sb("xT_e", [128, 2, 2, TT], F32R)
        wv = sb("wv", [128, 2, 2, 2, F], F32R)
        w2 = sb("w2", [128, E, 4, D])
        sil = sb("sil", [128, 2, TT])
        hid = sb("hid", [128, 2, 4, TT])
        yo = sb("yo", [128, 2, 2, D])
        S_ = {}

        def s(name):
            if name not in S_:
                S_[name] = ctx.enter_context(nc.semaphore(name))
            return S_[name]

        def steps(step):
            def run(eng):
                step(0, 0, 0, True, False)
                step(1, 0, 1, True, True)
                with eng.Fori(0, (NT - 4) // 2) as i:
                    step(2 * i + 2, i + 1, 0, True, True)
                    step(2 * i + 3, i + 1, 1, True, True)
                step(NT - 2, NT // 2 - 1, 0, True, True)
                step(NT - 1, NT // 2 - 1, 1, False, True)
            return run

        block = ctx.enter_context(nc.Block())

        @block.sync
        def _(sp):
            def rows(t, h, p):
                r = sp.value_load(table[0:1, bass.ds(t, 1), 0], min_val=0, max_val=E * CAP)
                at_least(sp, s("tok_t"), t - 1)
                at_least(sp, s("meta_done"), t - 1)
                sp.dma_start(xr[:, p], sorted_rows[bass.ds(r, TT)].rearrange("(p a) n -> p a n", a=2)
                             ).then_inc(s(f"rows_in{p}"), 16)

            rows(0, 0, 0)
            rows(1, 0, 1)
            with sp.Fori(0, (NT - 2) // 2) as i:
                rows(2 * i + 2, i + 1, 0)
                rows(2 * i + 3, i + 1, 1)

        @block.tensor
        def _(pe):
            def turn(t, h, p):
                pe.wait_ge(s(f"rows_in{p}"), 16 * (h + 1))
                at_least(pe, s("xT_low_e"), t - 1)
                for a in range(2):
                    q = pe.transpose(bank[6 + p][:, 128 * a:128 * a + 128], xr[:, p, a, 0:D], ident)
                q.then_inc(s("tok_t"), 1)

            def hidden(t, p, fc):
                if fc == 0:
                    pe.wait_ge(s("xT_low_e"), t + 1)
                    pe.wait_ge(s("w_low"), 2 * t + 2)
                at_least(pe, s("h_done"), 4 * (t - 1) + fc + 1)
                cols = slice(128 * fc, 128 * fc + 128)
                for m in range(2):
                    for w_, x_ in ((0, 0), (0, 1), (1, 0)):
                        q = pe.matmul(bank[fc][:, TT * m:TT * m + TT],
                                      wv[:, p, w_, m, cols], xT[:, p, x_],
                                      start=(w_ + x_ == 0), stop=(w_ == 1))
                q.then_inc(s("hv_done"), 1)

            def down(t, p, e):
                pe.wait_ge(s("h_done"), 4 * t + 4)
                if isinstance(t, int) and t == 0:
                    pe.wait_ge(s("w2_in"), 16 * E)
                at_least(pe, s("y_scaled"), t - 1)
                for a in range(2):
                    for fc in range(4):
                        q = pe.matmul(bank[4 + p][:, D * a:D * a + D], hid[:, p, fc, 128 * a:128 * a + 128],
                                      w2[:, bass.ds(e, 1), fc].rearrange("p e n -> p (e n)"), start=(fc == 0), stop=(fc == 3))
                q.then_inc(s("y_done"), 1)

            def expert(t):
                return pe.value_load(table[0:1, bass.ds(t, 1), 1], min_val=0, max_val=E - 1)

            def step(t, h, p, more, prev):
                hidden(t, p, 0)
                hidden(t, p, 1)
                if more:
                    turn(t + 1, h + p, 1 - p)
                if prev:
                    down(t - 1, 1 - p, expert(t - 1))
                hidden(t, p, 2)
                hidden(t, p, 3)

            turn(0, 0, 0)
            steps(step)(pe)
            down(NT - 1, 1, expert(NT - 1))

        @block.scalar
        def _(ac):
            def high_w(t, p, ms=(0, 1)):
                e = ac.value_load(table[0:1, bass.ds(t, 1), 1], min_val=0, max_val=E - 1)
                at_least(ac, s("hv_done"), 4 * (t - 1))
                for m in ms:
                    ac.copy(wv[:, p, 0, m], wv_all[:, bass.ds(e, 1), m].rearrange("p e n -> p (e n)")).then_inc(s("w_high"), 1)

            def copy_x(t, h, p):
                ac.wait_ge(s("tok_t"), t + 1)
                at_least(ac, s("hv_done"), 4 * (t - 1))
                ac.copy(xT[:, p, 0], bank[6 + p][:, 0:TT]).then_inc(s("xT_high_e"), 1)

            def step(t, h, p, more, prev):
                for fc in range(4):
                    if more and fc == 2:
                        copy_x(t + 1, h + p, 1 - p)
                        high_w(t + 1, 1 - p)
                    ac.wait_ge(s("hv_done"), 4 * t + fc + 1)
                    at_least(ac, s("h_done"), 4 * t + fc - 1)
                    ac.activation(sil[:, fc % 2], bank[fc][:, 0:TT], ACT.Silu).then_inc(s("silu_done"), 1)

            for e in range(E):
                ac.dma_start(w2[:, e], ffw2[e].rearrange("(c f) d -> f c d", c=4)).then_inc(s("w2_in"), 16)
            high_w(0, 0)
            copy_x(0, 0, 0)
            steps(step)(ac)

        @block.vector
        def _(ve):
            def low_w(t, p, ms=(0, 1)):
                e = ve.value_load(table[0:1, bass.ds(t, 1), 1], min_val=0, max_val=E - 1)
                for m in ms:
                    ve.wait_ge(s("w_high"), 2 * t + m + 1)
                    ve.tensor_tensor(wv[:, p, 1, m], wv_all[:, bass.ds(e, 1), m].rearrange("p e n -> p (e n)"),
                                     wv[:, p, 0, m].bitcast(F32), ALU.subtract).then_inc(s("w_low"), 1)

            def meta(t, h, p):
                ve.wait_ge(s(f"rows_in{p}"), 16 * (h + 1))
                at_least(ve, s("y_scaled"), t - 1)
                ve.tensor_copy(meta_[:, p], xr[:, p, :, D:]).then_inc(s("meta_done"), 1)

            def low_x(t, p):
                ve.wait_ge(s("xT_high_e"), t + 1)
                ve.tensor_tensor(xT[:, p, 1], bank[6 + p][:, 0:TT], xT[:, p, 0].bitcast(F32), ALU.subtract
                                 ).then_inc(s("xT_low_e"), 1)

            def product(t, p, fc):
                ve.wait_ge(s("silu_done"), 4 * t + fc + 1)
                if fc == 0:
                    at_least(ve, s("y_done"), t - 1)
                ve.tensor_tensor(hid[:, p, fc], sil[:, fc % 2], bank[fc][:, TT:2 * TT], ALU.mult).then_inc(s("h_done"), 1)

            def scale(t, p):
                ve.wait_ge(s("y_done"), t + 1)
                ve.wait_ge(s("meta_done"), t + 1)
                at_least(ve, s("added"), 32 * (t - 1))
                ve.tensor_copy(dest[:, p], meta_[:, p, :, 1])
                for a in range(2):
                    q = ve.tensor_scalar(yo[:, p, a], bank[4 + p][:, D * a:D * a + D], meta_[:, p, a, 0:1], None, ALU.mult)
                q.then_inc(s("y_scaled"), 1)

            def step(t, h, p, more, prev):
                product(t, p, 0)
                product(t, p, 1)
                if more:
                    low_x(t + 1, 1 - p)
                    low_w(t + 1, 1 - p)
                if prev:
                    scale(t - 1, 1 - p)
                if more:
                    meta(t + 1, h + p, 1 - p)
                product(t, p, 2)
                product(t, p, 3)

            low_w(0, 0)
            meta(0, 0, 0)
            low_x(0, 0)
            steps(step)(ve)
            scale(NT - 1, 1)

        @block.gpsimd
        def _(po):
            def add(t, p):
                wait_alone(po, (s("xT_high_e"), 1), (s("y_scaled"), t + 1), (s("added"), 32 * t))
                for a in range(2):
                    po.indirect_dma_start(out, bass.IndirectOffsetOnAxis(dest[:, p, a:a + 1], 0), yo[:, p, a], None,
                                          compute_op=ALU.add).then_inc(s("added"), 16)

            add(0, 0)
            add(1, 1)
            with po.Fori(1, NT // 2) as i:
                add(2 * i, 0)
                add(2 * i + 1, 1)
            po.wait_ge(s("added"), 32 * NT)


_INS = ["x", "L0_tok_gamma", "L0_tok_beta", "L0_tok_W", "L0_tok_b", "L0_attn_Wqkv", "L0_attn_Wout", "L0_attn_bout",
        "L0_attn_proj", "L0_ffn_Wg", "L0_ffn_W", "L0_ffn_V", "L0_ffn_W2"]


def kernel(**inputs):
    import numpy as _np
    import concourse.bacc as _bacc
    from concourse import mybir as _mybir
    from concourse.bass_utils import run_bass_kernel_spmd as _run

    nc = _bacc.Bacc("TRN2", target_bir_lowering=False, num_devices=1)
    arrays, args = {}, []
    for name in _INS:
        a = _np.ascontiguousarray(inputs[name])
        arrays[f"in_{name}"] = a
        args.append(nc.dram_tensor(f"in_{name}", a.shape, _mybir.dt.from_np(a.dtype), kind="ExternalInput").ap())
    c = constants()
    arrays["in_const"] = c
    args.append(nc.dram_tensor("in_const", c.shape, F32, kind="ExternalInput").ap())
    args.append(nc.dram_tensor("out_rows", (NTOK + TT, D), F32, kind="ExternalOutput").ap())
    build(nc, *args)
    r = _run(nc, [arrays], core_ids=[0])
    return r.results[0]["out_rows"][:NTOK].reshape(B, TOK, D)
```
